# Optimizing a Trainium2 kernel written in Bass

```python
import numpy as np
import jax
import jax.numpy as jnp

def _softmax(x, axis=-1):
    return jax.nn.softmax(x, axis=axis)

def _gelu(x):
    return jax.nn.gelu(x, approximate=True)

def _silu(x):
    return jax.nn.silu(x)

def _sigmoid(x):
    return jax.nn.sigmoid(x)

def _layernorm(x, axis=-1, eps=1e-05):
    m = jnp.mean(x, axis=axis, keepdims=True)
    v = jnp.var(x, axis=axis, keepdims=True)
    return (x - m) / jnp.sqrt(v + eps)

def _scatter_add(tgt, idx, src, axis=0):
    return tgt.at[idx].add(src)

def _segment_sum(src, seg, n):
    return jax.ops.segment_sum(src, seg, n)
kernel_name = 'mk_xattn_ffn_d2_seqx_r8_7f107a'

def setup_inputs(seed: int=0):
    np.random.seed(seed)
    _w = jnp.asarray

    def _rec_inputs():
        import jax
        import jax.numpy as jnp
        _rk = jax.random.key(seed)
        x = 0.0001212 + 1 * jax.random.normal(jax.random.fold_in(_rk, 1), (8, 128, 256), jnp.float32)
        _lenS = 128 - jax.random.randint(jax.random.fold_in(_rk, 7), (8,), 0, max(1, 128 // 4) + 1, jnp.int32)
        _lenS2 = 128 - jax.random.randint(jax.random.fold_in(_rk, 8), (8,), 0, max(1, 128 // 4) + 1, jnp.int32)
        _ctx_2048P = jax.random.normal(jax.random.fold_in(_rk, 11), (8, 16, 256), jnp.float32)
        _ctx_2048c = jax.random.dirichlet(jax.random.fold_in(_rk, 511), 0.3 * jnp.ones((16,), jnp.float32), (8, 128))
        _ctx_2048t = jnp.einsum('bsk,bkd->bsd', _ctx_2048c, _ctx_2048P)
        _ctx_2048t = _ctx_2048t * jax.lax.rsqrt(jnp.mean(jnp.square(_ctx_2048t)) + 1e-12) * 0.953939
        ctx_2048 = 0.000173663 + 1.0001 * (_ctx_2048t + 0.3 * jax.random.normal(jax.random.fold_in(_rk, 611), (8, 128, 256), jnp.float32))
        _validS = jnp.arange(128)[None, :] < _lenS[:, None]
        _validS2 = jnp.arange(128)[None, :] < _lenS2[:, None]
        _causal = jnp.tril(jnp.ones((128, 128), dtype=bool))
        mask_BxSxS2_ff0 = jnp.where(jnp.ones((8, 128, 128), dtype=bool), 0.0, -1000000000.0).astype(jnp.float32)
        return (x, ctx_2048, mask_BxSxS2_ff0)
    x, ctx_2048, mask_BxSxS2_ff0 = _rec_inputs()

    def _L0_xattn_setup():
        import jax, jax.numpy as jnp
        import numpy as np
        B_DIM, T_DIM, C_DIM = (16, 128, 256)

        def _wkv(w, u, k, v):
            Bn, Tn, Cn = k.shape
            NEG_INF = jnp.float32(-1e+38)

            def step(carry, kv_t):
                p, q, o = carry
                kt, vt = kv_t
                no = jnp.maximum(o, u + kt)
                A = jnp.exp(o - no)
                E = jnp.exp(u + kt - no)
                y = (A * p + E * vt) / (A * q + E)
                no2 = jnp.maximum(w + o, kt)
                A2 = jnp.exp(w + o - no2)
                E2 = jnp.exp(kt - no2)
                return ((A2 * p + E2 * vt, A2 * q + E2, no2), y)
            init = (jnp.zeros((Bn, Cn), k.dtype), jnp.zeros((Bn, Cn), k.dtype), jnp.full((Bn, Cn), NEG_INF, k.dtype))
            kT = jnp.moveaxis(k, 1, 0)
            vT = jnp.moveaxis(v, 1, 0)
            _, yT = jax.lax.scan(step, init, (kT, vT))
            return jnp.moveaxis(yT, 0, 1)
        key = jax.random.key(seed)
        k1, k2, k3, k4 = jax.random.split(key, 4)
        w = -jnp.exp(jax.random.normal(k1, (C_DIM,), jnp.float32))
        u = jax.random.normal(k2, (C_DIM,), jnp.float32)
        k = jax.random.normal(k3, (B_DIM, T_DIM, C_DIM), jnp.float32)
        v = jax.random.normal(k4, (B_DIM, T_DIM, C_DIM), jnp.float32)
        return {'B': B_DIM, 'T': T_DIM, 'C': C_DIM, 'w': w, 'u': u, 'k': k, 'v': v}
    _L0_xattn_all = _L0_xattn_setup()
    _L0_xattn_in = {k: v for k, v in _L0_xattn_all.items() if k in ('w', 'u')}
    del _L0_xattn_all

    def _L0_ffn_setup():
        import jax, jax.numpy as jnp
        import numpy as np
        import math
        B, S, D = (2, 128, 256)
        H, KVH, HD = (16, 4, 128)
        E, K, FF = (8, 2, 896)
        EPS = 1e-05
        ROPE_BASE = 1000000.0

        def rmsnorm(x, w, eps=EPS):
            xf = x.astype(jnp.float32)
            var = jnp.mean(xf * xf, axis=-1, keepdims=True)
            return (xf * jax.lax.rsqrt(var + eps)).astype(x.dtype) * w

        def apply_rope(x, cos, sin):
            x1 = x[..., 0::2]
            x2 = x[..., 1::2]
            r1 = x1 * cos - x2 * sin
            r2 = x1 * sin + x2 * cos
            return jnp.stack([r1, r2], axis=-1).reshape(x.shape)
        key = jax.random.key(seed)
        ks = jax.random.split(key, 12)
        sc = 0.02
        inp = {'x': jax.random.normal(ks[0], (B, S, D), jnp.float32), 'ln_w': jnp.ones((D,), jnp.float32), 'ff_ln_w': jnp.ones((D,), jnp.float32), 'wq': jax.random.normal(ks[1], (D, H * HD), jnp.float32) * sc, 'wk': jax.random.normal(ks[2], (D, KVH * HD), jnp.float32) * sc, 'wv': jax.random.normal(ks[3], (D, KVH * HD), jnp.float32) * sc, 'wo': jax.random.normal(ks[4], (H * HD, D), jnp.float32) * sc, 'gate_w': jax.random.normal(ks[5], (D, E), jnp.float32) * sc, 'w1': jax.random.normal(ks[6], (E, D, FF), jnp.float32) * sc, 'w3': jax.random.normal(ks[7], (E, D, FF), jnp.float32) * sc, 'w2': jax.random.normal(ks[8], (E, FF, D), jnp.float32) * sc}
        return inp
    _L0_ffn_all = _L0_ffn_setup()
    _L0_ffn_in = {k: v for k, v in _L0_ffn_all.items() if k in ('ln_w', 'ff_ln_w', 'wq', 'wk', 'wv', 'wo', 'gate_w', 'w1', 'w3', 'w2')}
    del _L0_ffn_all

    def _L1_xattn_setup():
        import jax, jax.numpy as jnp
        import numpy as np
        NUM_HEADS = 16
        EPS = 1e-08

        def _dyn_quant(x):
            s = jnp.maximum(jnp.max(jnp.abs(x), axis=-1, keepdims=True) / 127.0, EPS)
            q = jnp.clip(jnp.round(x / s), -127.0, 127.0)
            return (q, s)

        def _quant_weight(w):
            s = jnp.maximum(jnp.max(jnp.abs(w), axis=1, keepdims=True) / 127.0, EPS)
            q = jnp.clip(jnp.round(w / s), -127.0, 127.0)
            return (q, s)

        def _w8a8_linear(x, w, b):
            qx, sx = _dyn_quant(x)
            qw, sw = _quant_weight(w)
            y = jnp.einsum('bnc,oc->bno', qx, qw) * (sx * sw[:, 0])
            return y + b
        key = jax.random.key(seed)
        ks = jax.random.split(key, 9)
        B, N, L, C = (2, 512, 64, 256)
        sc = 0.02
        return {'x': jax.random.normal(ks[0], (B, N, C), jnp.float32), 'cond': jax.random.normal(ks[1], (B, L, C), jnp.float32), 'mask': jnp.zeros((B, N, L), jnp.float32), 'wq': jax.random.normal(ks[2], (C, C), jnp.float32) * sc, 'bq': jnp.zeros((C,), jnp.float32), 'wk': jax.random.normal(ks[3], (C, C), jnp.float32) * sc, 'bk': jnp.zeros((C,), jnp.float32), 'wv': jax.random.normal(ks[4], (C, C), jnp.float32) * sc, 'bv': jnp.zeros((C,), jnp.float32), 'wo': jax.random.normal(ks[5], (C, C), jnp.float32) * sc, 'bo': jnp.zeros((C,), jnp.float32)}
    _L1_xattn_all = _L1_xattn_setup()
    _L1_xattn_in = {k: v for k, v in _L1_xattn_all.items() if k in ('wq', 'bq', 'wk', 'bk', 'wv', 'bv', 'wo', 'bo')}
    del _L1_xattn_all

    def _L1_ffn_setup():
        import jax
        import jax.numpy as jnp
        import numpy as np
        NUM_EXPERTS = 32
        HIDDEN = 256
        INTER = 96
        TOP_K = 8
        TAU = 0.05
        BATCH, SEQ = (2, 128)
        key = jax.random.key(seed)
        k1, k2, k3, k4 = jax.random.split(key, 4)
        return {'hidden_states': jax.random.normal(k1, (BATCH, SEQ, HIDDEN), dtype=jnp.float32), 'gate_weight': jax.random.normal(k2, (NUM_EXPERTS, HIDDEN), dtype=jnp.float32) * 0.02, 'gate_up_proj': jax.random.normal(k3, (NUM_EXPERTS, 2 * INTER, HIDDEN), dtype=jnp.float32) * 0.02, 'down_proj': jax.random.normal(k4, (NUM_EXPERTS, HIDDEN, INTER), dtype=jnp.float32) * 0.02, 'layer_alpha': jnp.array(1.0, dtype=jnp.float32)}
    _L1_ffn_all = _L1_ffn_setup()
    _L1_ffn_in = {k: v for k, v in _L1_ffn_all.items() if k in ('gate_weight', 'gate_up_proj', 'down_proj', 'layer_alpha')}
    del _L1_ffn_all
    return {'x': x, 'ctx_2048': ctx_2048, 'mask_BxSxS2_ff0': mask_BxSxS2_ff0, 'L0_xattn_w': _L0_xattn_in['w'], 'L0_xattn_u': _L0_xattn_in['u'], 'L0_ffn_ln_w': _L0_ffn_in['ln_w'], 'L0_ffn_ff_ln_w': _L0_ffn_in['ff_ln_w'], 'L0_ffn_wq': _L0_ffn_in['wq'], 'L0_ffn_wk': _L0_ffn_in['wk'], 'L0_ffn_wv': _L0_ffn_in['wv'], 'L0_ffn_wo': _L0_ffn_in['wo'], 'L0_ffn_gate_w': _L0_ffn_in['gate_w'], 'L0_ffn_w1': _L0_ffn_in['w1'], 'L0_ffn_w3': _L0_ffn_in['w3'], 'L0_ffn_w2': _L0_ffn_in['w2'], 'L1_xattn_wq': _L1_xattn_in['wq'], 'L1_xattn_bq': _L1_xattn_in['bq'], 'L1_xattn_wk': _L1_xattn_in['wk'], 'L1_xattn_bk': _L1_xattn_in['bk'], 'L1_xattn_wv': _L1_xattn_in['wv'], 'L1_xattn_bv': _L1_xattn_in['bv'], 'L1_xattn_wo': _L1_xattn_in['wo'], 'L1_xattn_bo': _L1_xattn_in['bo'], 'L1_ffn_gate_weight': _L1_ffn_in['gate_weight'], 'L1_ffn_gate_up_proj': _L1_ffn_in['gate_up_proj'], 'L1_ffn_down_proj': _L1_ffn_in['down_proj'], 'L1_ffn_layer_alpha': _L1_ffn_in['layer_alpha']}

def reference(x, ctx_2048, mask_BxSxS2_ff0, L0_xattn_w, L0_xattn_u, L0_ffn_ln_w, L0_ffn_ff_ln_w, L0_ffn_wq, L0_ffn_wk, L0_ffn_wv, L0_ffn_wo, L0_ffn_gate_w, L0_ffn_w1, L0_ffn_w3, L0_ffn_w2, L1_xattn_wq, L1_xattn_bq, L1_xattn_wk, L1_xattn_bk, L1_xattn_wv, L1_xattn_bv, L1_xattn_wo, L1_xattn_bo, L1_ffn_gate_weight, L1_ffn_gate_up_proj, L1_ffn_down_proj, L1_ffn_layer_alpha):
    import jax
    import jax.numpy as jnp

    def _L0_xattn_ref(B, T, C, w, u, k, v):
        import jax, jax.numpy as jnp
        import numpy as np
        B_DIM, T_DIM, C_DIM = (16, 128, 256)

        def _wkv(w, u, k, v):
            Bn, Tn, Cn = k.shape
            NEG_INF = jnp.float32(-1e+38)

            def step(carry, kv_t):
                p, q, o = carry
                kt, vt = kv_t
                no = jnp.maximum(o, u + kt)
                A = jnp.exp(o - no)
                E = jnp.exp(u + kt - no)
                y = (A * p + E * vt) / (A * q + E)
                no2 = jnp.maximum(w + o, kt)
                A2 = jnp.exp(w + o - no2)
                E2 = jnp.exp(kt - no2)
                return ((A2 * p + E2 * vt, A2 * q + E2, no2), y)
            init = (jnp.zeros((Bn, Cn), k.dtype), jnp.zeros((Bn, Cn), k.dtype), jnp.full((Bn, Cn), NEG_INF, k.dtype))
            kT = jnp.moveaxis(k, 1, 0)
            vT = jnp.moveaxis(v, 1, 0)
            _, yT = jax.lax.scan(step, init, (kT, vT))
            return jnp.moveaxis(yT, 0, 1)
        return _wkv(w, u, k, v)

    def _L0_ffn_ref(x, ln_w, ff_ln_w, wq, wk, wv, wo, gate_w, w1, w3, w2):
        import jax, jax.numpy as jnp
        import numpy as np
        import math
        B, S, D = (2, 128, 256)
        H, KVH, HD = (16, 4, 128)
        E, K, FF = (8, 2, 896)
        EPS = 1e-05
        ROPE_BASE = 1000000.0

        def rmsnorm(x, w, eps=EPS):
            xf = x.astype(jnp.float32)
            var = jnp.mean(xf * xf, axis=-1, keepdims=True)
            return (xf * jax.lax.rsqrt(var + eps)).astype(x.dtype) * w

        def apply_rope(x, cos, sin):
            x1 = x[..., 0::2]
            x2 = x[..., 1::2]
            r1 = x1 * cos - x2 * sin
            r2 = x1 * sin + x2 * cos
            return jnp.stack([r1, r2], axis=-1).reshape(x.shape)
        Bx, Sx, Dx = x.shape
        residual = x
        h = rmsnorm(x, ln_w)
        q = (h @ wq).reshape(Bx, Sx, H, HD)
        k = (h @ wk).reshape(Bx, Sx, KVH, HD)
        v = (h @ wv).reshape(Bx, Sx, KVH, HD)
        pos = jnp.arange(Sx, dtype=jnp.float32)
        inv_freq = ROPE_BASE ** (-jnp.arange(0, HD, 2, dtype=jnp.float32) / HD)
        ang = pos[:, None] * inv_freq[None, :]
        cos = jnp.cos(ang)[None, :, None, :]
        sin = jnp.sin(ang)[None, :, None, :]
        q = apply_rope(q, cos, sin)
        k = apply_rope(k, cos, sin)
        rep = H // KVH
        k = jnp.repeat(k, rep, axis=2)
        v = jnp.repeat(v, rep, axis=2)
        scores = jnp.einsum('bqhd,bkhd->bhqk', q, k) / math.sqrt(HD)
        causal = jnp.tril(jnp.ones((Sx, Sx), dtype=bool))
        scores = jnp.where(causal[None, None], scores, jnp.finfo(scores.dtype).min)
        attn = jax.nn.softmax(scores, axis=-1)
        o = jnp.einsum('bhqk,bkhd->bqhd', attn, v).reshape(Bx, Sx, H * HD)
        x = o @ wo + residual
        residual = x
        h = rmsnorm(x, ff_ln_w)
        ht = h.reshape(-1, Dx)
        logits = ht @ gate_w
        top_vals, top_idx = jax.lax.top_k(logits, K)
        gates = jax.nn.softmax(top_vals, axis=-1)
        out = jnp.zeros_like(ht)
        for e in range(E):
            we = jnp.sum(gates * (top_idx == e), axis=-1)
            ye = jax.nn.silu(ht @ w1[e]) * (ht @ w3[e]) @ w2[e]
            out = out + we[:, None] * ye
        return out.reshape(Bx, Sx, Dx) + residual

    def _L1_xattn_ref(x, cond, mask, wq, bq, wk, bk, wv, bv, wo, bo):
        import jax, jax.numpy as jnp
        import numpy as np
        NUM_HEADS = 16
        EPS = 1e-08

        def _dyn_quant(x):
            s = jnp.maximum(jnp.max(jnp.abs(x), axis=-1, keepdims=True) / 127.0, EPS)
            q = jnp.clip(jnp.round(x / s), -127.0, 127.0)
            return (q, s)

        def _quant_weight(w):
            s = jnp.maximum(jnp.max(jnp.abs(w), axis=1, keepdims=True) / 127.0, EPS)
            q = jnp.clip(jnp.round(w / s), -127.0, 127.0)
            return (q, s)

        def _w8a8_linear(x, w, b):
            qx, sx = _dyn_quant(x)
            qw, sw = _quant_weight(w)
            y = jnp.einsum('bnc,oc->bno', qx, qw) * (sx * sw[:, 0])
            return y + b
        B, N, C = x.shape
        L = cond.shape[1]
        H = NUM_HEADS
        D = C // H
        inv_sqrt_d = np.float32(1.0 / np.sqrt(D))
        q = _w8a8_linear(x, wq, bq).reshape(B, N, H, D).transpose(0, 2, 1, 3)
        k = (cond @ wk.T + bk).reshape(B, L, H, D).transpose(0, 2, 1, 3)
        v = (cond @ wv.T + bv).reshape(B, L, H, D).transpose(0, 2, 1, 3)
        scores = jnp.einsum('bhnd,bhld->bhnl', q, k) * inv_sqrt_d + mask[:, None]
        attn = jax.nn.softmax(scores, axis=-1)
        o = jnp.einsum('bhnl,bhld->bhnd', attn, v)
        o = o.transpose(0, 2, 1, 3).reshape(B, N, C)
        return _w8a8_linear(o, wo, bo)

    def _L1_ffn_ref(hidden_states, gate_weight, gate_up_proj, down_proj, layer_alpha):
        import jax
        import jax.numpy as jnp
        import numpy as np
        NUM_EXPERTS = 32
        HIDDEN = 256
        INTER = 96
        TOP_K = 8
        TAU = 0.05
        BATCH, SEQ = (2, 128)
        B, S, H = hidden_states.shape
        x = hidden_states.reshape(-1, H)
        T = x.shape[0]
        logits = x @ gate_weight.T
        probs = jax.nn.softmax(logits.astype(jnp.float32), axis=-1).astype(logits.dtype)
        topv, topi = jax.lax.top_k(probs, TOP_K)
        topv = topv / jnp.clip(topv.sum(axis=-1, keepdims=True), 1e-12)
        scaled = topv * layer_alpha.astype(topv.dtype)
        active = scaled >= TAU
        empty = ~jnp.any(active, axis=-1)
        fallback = jnp.arange(TOP_K)[None, :] == jnp.argmax(scaled, axis=-1)[:, None]
        active = active | empty[:, None] & fallback
        routing_weights = topv * active.astype(topv.dtype)
        routing_weights = routing_weights / jnp.clip(routing_weights.sum(axis=-1, keepdims=True), 1e-12)
        combine = jnp.zeros((T, NUM_EXPERTS), dtype=x.dtype)
        combine = combine.at[jnp.arange(T)[:, None], topi].add(routing_weights)

        def expert_step(acc, xs):
            w_gu, w_d, c_e = xs
            gu = x @ w_gu.T
            g, u = jnp.split(gu, 2, axis=-1)
            h = jax.nn.silu(g) * u
            acc = acc + h @ w_d.T * c_e[:, None]
            return (acc, None)
        out, _ = jax.lax.scan(expert_step, jnp.zeros_like(x), (gate_up_proj, down_proj, combine.T))
        return out.reshape(B, S, H)
    x = x + _L0_xattn_ref(8, 128, 256, L0_xattn_w, L0_xattn_u, _layernorm(x, axis=-1), ctx_2048)
    x = x + _L0_ffn_ref(_layernorm(x, axis=-1), L0_ffn_ln_w, L0_ffn_ff_ln_w, L0_ffn_wq, L0_ffn_wk, L0_ffn_wv, L0_ffn_wo, L0_ffn_gate_w, L0_ffn_w1, L0_ffn_w3, L0_ffn_w2)
    x = x + _L1_xattn_ref(_layernorm(x, axis=-1), ctx_2048, mask_BxSxS2_ff0, L1_xattn_wq, L1_xattn_bq, L1_xattn_wk, L1_xattn_bk, L1_xattn_wv, L1_xattn_bv, L1_xattn_wo, L1_xattn_bo)
    x = x + _L1_ffn_ref(_layernorm(x, axis=-1), L1_ffn_gate_weight, L1_ffn_gate_up_proj, L1_ffn_down_proj, L1_ffn_layer_alpha)
    return x

_drawn_inputs = setup_inputs


def setup_inputs(seed=0):
    import zlib

    import numpy as np

    out = dict(_drawn_inputs(seed))
    spreads = {'L0_ffn_ln_w': (1.0, 0.6),
     'L0_ffn_ff_ln_w': (1.0, 0.6),
     'L1_xattn_bq': (0.0, 2.0),
     'L1_xattn_bk': (0.0, 2.0),
     'L1_xattn_bv': (0.0, 1.809),
     'L1_xattn_bo': (0.0, 0.519)}
    factors = {'L0_ffn_wq': 8.0,
     'L0_ffn_wk': 8.0,
     'L0_ffn_gate_w': 6.196,
     'L0_ffn_w1': 5.539,
     'L0_ffn_w3': 5.478,
     'L0_ffn_w2': 5.487,
     'L1_xattn_wq': 31.839,
     'L1_xattn_wk': 31.626,
     'L1_ffn_gate_weight': 8.0,
     'L1_ffn_gate_up_proj': 8.0,
     'L1_ffn_down_proj': 8.0,
     'L1_xattn_wv': 3.422}
    for name, (base, spread) in spreads.items():
        noise = np.random.default_rng([zlib.crc32(name.encode()), seed]).standard_normal(out[name].shape)
        drawn = base * np.exp(spread * noise) if base else spread * noise
        out[name] = jnp.asarray(drawn.astype(out[name].dtype))
    for name, factor in factors.items():
        out[name] = (out[name] * factor).astype(out[name].dtype)
    return out
```

```python
from contextlib import ExitStack

import concourse.bass as bass
from concourse import mybir
from concourse.alu_op_type import AluOpType as ALU

fp32 = mybir.dt.float32
bf16 = mybir.dt.bfloat16
u32 = mybir.dt.uint32
ACT = mybir.ActivationFunctionType
AX = mybir.AxisListType

P = 128
B = 8
C = 256
CB = C // P
T = B * P
HB = B // 2
PAD = P + 1
NEG = -1e38
LN_EPS = 1e-5


class Memory:

    def __init__(self, nc):
        self.nc, self.stack, self.sems = nc, ExitStack(), []

    def __enter__(self):
        self.stack.__enter__()
        return self

    def __exit__(self, *a):
        if a[0] is None and self.sems:
            runs = []
            for n in sorted(s.num for s in self.sems):
                if runs and runs[-1][1] == n:
                    runs[-1][1] = n + 1
                else:
                    runs.append([n, n + 1])
            with self.nc.Block() as block:

                @block.gpsimd
                def _(pool):
                    for first, end in runs:
                        pool.sem_clear(range(first, end))

        return self.stack.__exit__(*a)

    def sb(self, name, shape, dt=fp32):
        return self.stack.enter_context(self.nc.sbuf_tensor(name, shape, dt))

    def ps(self, name, shape, dt=fp32):
        return self.stack.enter_context(self.nc.psum_tensor(name, shape, dt))

    def sem(self, name):
        self.sems.append(self.stack.enter_context(self.nc.semaphore(name)))
        return self.sems[-1]


def wait_past(eng, sem, n):
    if not isinstance(n, int) or n > 0:
        eng.wait_ge(sem, n)


def wkv_stage(nc, k, io):
    with Memory(nc) as m:
        ctxT = m.sb("ctxT", [P, CB, B, P])
        xn = m.sb("xn", [P, B, C])
        stats = m.sb("ln_stats", [P, B, 6])
        mv = m.sb("ln_mean_var", [P, B, 2])
        sd = m.sb("ln_sd", [P, B])
        rstd = m.sb("ln_rstd", [P, B])
        eps = k.eps
        wk1T = m.sb("wk1T", [P, CB, C])
        wv1T = m.sb("wv1T", [P, CB, C])
        bv1 = m.sb("bv1", [P, C])
        wkv_cols = m.sb("wkv_cols", [P, 3, CB])
        pad = lambda name: [m.sb(f"{name}{c}", [P, B, PAD]) for c in range(CB)]
        flat = lambda name: [m.sb(f"{name}{c}", [P, B, P]) for c in range(CB)]
        decay, kpad, omax = pad("decay"), pad("kpad"), pad("omax")
        qsum, psum = pad("qsum"), pad("psum_")
        a2, e2, ev2 = pad("a2_"), pad("e2_"), pad("ev2_")
        d2_, d1, a1, e1, ev1 = flat("d2_"), flat("d1_"), flat("a1_"), flat("e1_"), flat("ev1_")
        kT_ps = m.ps("kT_ps", [P, CB, T])
        y_ps = m.ps("y_ps", [P, B, C])
        y_half = y_ps[:, :, :]

        x_in = [m.sem(f"x_in{h}") for h in range(2)]
        ctx_in, const_in, cols_in, w1_in = m.sem("ctx_in"), m.sem("const_in"), m.sem("cols_in"), m.sem("w1_in")
        eps_set, pads_set = m.sem("eps_set"), m.sem("pads_set")
        stats_done, var_done, sd_done, rstd_done = m.sem("stats_done"), m.sem("var_done"), m.sem("sd_done"), m.sem("rstd_done")
        xn_done, kT_done, kpad_done = m.sem("xn_done"), m.sem("kT_done"), m.sem("kpad_done")
        decay_done, omax_done, d2_done, d1_done = m.sem("decay_done"), m.sem("omax_done"), m.sem("d2_done"), m.sem("d1_done")
        relu_done, exp2_done, exp1_done = m.sem("relu_done"), m.sem("exp2_done"), m.sem("exp1_done")
        ev2_done, ev1_done, ap_done, aq_done = m.sem("ev2_done"), m.sem("ev1_done"), m.sem("ap_done"), m.sem("aq_done")
        qscan_done, pscan_done = m.sem("qscan_done"), m.sem("pscan_done")
        den_done, num_done, rden_done, yT_done = m.sem("den_done"), m.sem("num_done"), m.sem("rden_done"), m.sem("yT_done")
        y_done, x1_done = m.sem("y_done"), m.sem("x1_done")
        keys_done, keys_out, vals_done, vals_raw, vals_out = m.sem("keys_done"), m.sem("keys_out"), m.sem("vals_done"), m.sem("vals_raw"), m.sem("vals_out")

        with nc.Block() as block:

            @block.sync
            def _(sp):
                for h in range(2):
                    sp.dma_start(k.x1[:, HB * h:HB * (h + 1), :],
                                 io["x"][HB * h:HB * (h + 1)].rearrange("b s c -> s b c")).then_inc(x_in[h], 16)
                sp.dma_start(k.ident[:, :], io["ident"]).then_inc(const_in, 16)
                sp.dma_start(ctxT[:, :, :, :], io["ctxT"].rearrange("(cb p) b s -> p cb b s", p=P)).then_inc(ctx_in, 16)

            @block.scalar
            def _(act):
                act.dma_start(wkv_cols[:, :, :], io["wkv_cols"]).then_inc(cols_in, 16)
                act.dma_start(wk1T[:, :, :], io["wk1T"].rearrange("(cb p) o -> p cb o", p=P)).then_inc(w1_in, 16)
                act.dma_start(wv1T[:, :, :], io["wv1T"].rearrange("(cb p) o -> p cb o", p=P)).then_inc(w1_in, 16)
                act.dma_start(bv1[:, :], io["bv1"]).then_inc(w1_in, 16)
                act.wait_ge(eps_set, 1)
                for h in range(2):
                    act.wait_ge(var_done, HB * (h + 1))
                    act.activation(sd[:, HB * h:HB * (h + 1)], mv[:, HB * h:HB * (h + 1), 1], ACT.Sqrt,
                                   bias=eps[:, 0:1]).then_inc(sd_done, 1)
                for c in range(CB):
                    for h in range(2):
                        act.wait_ge(kT_done, 2 * c + h + 1)
                        act.activation(kpad[c][:, HB * h:HB * (h + 1), 1:PAD],
                                       kT_ps[:, c, 512 * h:512 * (h + 1)].rearrange("p (b s) -> p b s", s=P),
                                       ACT.Copy).then_inc(kpad_done, 1)
                for c in range(CB):
                    act.wait_ge(pads_set, 3 * (c + 1))
                    act.wait_ge(d2_done, c + 1)
                    d2 = d2_[c]
                    act.activation(a2[c][:, :, 1:PAD], d2[:, :, :], ACT.Relu, scale=-1.0).then_inc(relu_done, 1)
                    act.activation(e2[c][:, :, 1:PAD], d2[:, :, :], ACT.Relu).then_inc(relu_done, 1)
                    act.wait_ge(d1_done, c + 1)
                    act.activation(a1[c][:, :, :], d1[c][:, :, :], ACT.Relu, scale=-1.0).then_inc(relu_done, 1)
                    act.activation(e1[c][:, :, :], d1[c][:, :, :], ACT.Relu).then_inc(relu_done, 1)
                    act.wait_ge(relu_done, 4 * c + 4)
                    for buf, span in ((e2[c], slice(1, PAD)), (a2[c], slice(1, PAD)), ):
                        act.activation(buf[:, :, span], buf[:, :, span], ACT.Exp, scale=-1.0).then_inc(exp2_done, 1)
                    for buf in (e1[c], a1[c]):
                        act.activation(buf[:, :, :], buf[:, :, :], ACT.Exp, scale=-1.0).then_inc(exp1_done, 1)
                act.wait_ge(cols_in, 16)
                for ob in range(CB):
                    for h in range(2):
                        act.wait_ge(keys_done, 2 * ob + h + 1)
                        act.activation(k.keys1[:, ob, 512 * h:512 * (h + 1)], kT_ps[:, ob, 512 * h:512 * (h + 1)],
                                       ACT.Identity, bias=wkv_cols[:, 2, ob:ob + 1]).then_inc(keys_out, 1)
                for j in range(4):
                    act.wait_ge(vals_done, j + 1)
                    act.activation(k.vals1[:, 2 * j:2 * j + 2, :], y_ps[:, 2 * j:2 * j + 2, :], ACT.Copy).then_inc(vals_raw, 1)

            @block.tensor
            def _(pe):
                pe.wait_ge(const_in, 16)
                for c in range(CB):
                    for h in range(2):
                        for b in range(HB * h, HB * (h + 1)):
                            pe.wait_ge(xn_done, b + 1)
                            t = pe.transpose(kT_ps[:, c, P * b:P * (b + 1)], xn[:, b, P * c:P * (c + 1)], k.ident[:, :])
                        t.then_inc(kT_done, 1)
                pe.wait_ge(ctx_in, 16)
                pe.wait_ge(w1_in, 48)
                for b in range(B):
                    for c in range(CB):
                        t = pe.matmul(y_ps[:, b, :], ctxT[:, c, b, :], wv1T[:, c, :], start=(c == 0), stop=(c == CB - 1))
                    if b % 2:
                        t.then_inc(vals_done, 1)
                pe.wait_ge(kpad_done, 2 * CB)
                for ob in range(CB):
                    for h in range(2):
                        for c in range(CB):
                            t = pe.matmul(kT_ps[:, ob, 512 * h:512 * (h + 1)], wk1T[:, c, P * ob:P * (ob + 1)],
                                          ctxT[:, c, HB * h:HB * (h + 1), :], start=(c == 0), stop=(c == CB - 1))
                        t.then_inc(keys_done, 1)
                pe.wait_ge(vals_raw, 4)
                for c in range(CB):
                    pe.wait_ge(yT_done, c + 1)
                    for b in range(B):
                        t = pe.transpose(y_ps[:, b, P * c:P * (c + 1)], a1[c][:, b, :], k.ident[:, :])
                        if c == CB - 1 and b % 2:
                            t.then_inc(y_done, 1)

            @block.gpsimd
            def _(pool):
                for c in range(CB):
                    for buf in (a2[c], e2[c], ev2[c]):
                        pool.memset(buf[:, :, 0:1], 0.0).then_inc(pads_set, 1)
                for c in range(CB):
                    pool.wait_ge(exp2_done, 2 * c + 1)
                    pool.wait_ge(ctx_in, 16)
                    pool.tensor_tensor(ev2[c][:, :, 1:PAD], e2[c][:, :, 1:PAD], ctxT[:, c, :, :], ALU.mult).then_inc(ev2_done, 1)
                    pool.wait_ge(exp1_done, 2 * c + 1)
                    pool.tensor_tensor(ev1[c][:, :, :], e1[c][:, :, :], ctxT[:, c, :, :], ALU.mult).then_inc(ev1_done, 1)
                    pool.wait_ge(exp1_done, 2 * c + 2)
                    pool.wait_ge(qscan_done, c + 1)
                    pool.tensor_tensor(qsum[c][:, :, 0:P], qsum[c][:, :, 0:P], a1[c][:, :, :], ALU.mult).then_inc(aq_done, 1)
                pool.wait_ge(w1_in, 48)
                for b in range(B):
                    pool.wait_ge(vals_raw, b // 2 + 1)
                    pool.tensor_tensor(k.vals1[:, b, :], k.vals1[:, b, :], bv1[:, :], ALU.add).then_inc(vals_out, 1)

            @block.vector
            def _(dve):
                dve.memset(eps[:, :], LN_EPS).then_inc(eps_set, 1)
                for h in range(2):
                    dve.wait_ge(x_in[h], 16)
                    for b in range(HB * h, HB * (h + 1)):
                        dve.bn_stats(stats[:, b, :], k.x1[:, b, :]).then_inc(stats_done, 1)
                    for b in range(HB * h, HB * (h + 1)):
                        dve.wait_ge(stats_done, b + 1)
                        dve.bn_aggr(mv[:, b, :], stats[:, b, :]).then_inc(var_done, 1)
                    if h == 0:
                        dve.wait_ge(cols_in, 16)
                        for c in range(CB):
                            dve.memset(decay[c][:, :, 1:PAD], 0.0).then_inc(decay_done, 1)
                            dve.memset(decay[c][:, :, 0:1], NEG).then_inc(decay_done, 1)
                            dve.memset(kpad[c][:, :, 0:1], NEG).then_inc(decay_done, 1)
                            dve.wait_ge(decay_done, 4 * c + 1)
                            dve.tensor_scalar(decay[c][:, :, 1:PAD], decay[c][:, :, 1:PAD], wkv_cols[:, 0, c:c + 1], None,
                                              ALU.add).then_inc(decay_done, 1)
                for h in range(2):
                    dve.wait_ge(sd_done, h + 1)
                    dve.reciprocal(rstd[:, HB * h:HB * (h + 1)], sd[:, HB * h:HB * (h + 1)]).then_inc(rstd_done, 1)
                    dve.wait_ge(rstd_done, h + 1)
                    for b in range(HB * h, HB * (h + 1)):
                        dve.tensor_scalar(xn[:, b, :], k.x1[:, b, :], mv[:, b, 0:1], rstd[:, b:b + 1],
                                          ALU.subtract, ALU.mult).then_inc(xn_done, 1)
                for c in range(CB):
                    dve.wait_ge(kpad_done, 2 * c + 2)
                    dve.wait_ge(decay_done, 4 * c + 4)
                    dve.tensor_tensor_scan(omax[c][:, :, :].rearrange("p b s -> p (b s)"),
                                           decay[c][:, :, :].rearrange("p b s -> p (b s)"),
                                           kpad[c][:, :, :].rearrange("p b s -> p (b s)"),
                                           NEG, ALU.add, ALU.max).then_inc(omax_done, 1)
                    dve.wait_ge(omax_done, c + 1)
                    dve.scalar_tensor_tensor(d2_[c][:, :, :], omax[c][:, :, 0:P], wkv_cols[:, 0, c:c + 1],
                                             kpad[c][:, :, 1:PAD], ALU.add, ALU.subtract).then_inc(d2_done, 1)
                    dve.scalar_tensor_tensor(d1[c][:, :, :], omax[c][:, :, 0:P], wkv_cols[:, 1, c:c + 1],
                                             kpad[c][:, :, 1:PAD], ALU.subtract, ALU.subtract).then_inc(d1_done, 1)
                for c in range(CB):
                    fl = lambda t: t[c][:, :, :].rearrange("p b s -> p (b s)")
                    dve.wait_ge(exp2_done, 2 * c + 2)
                    dve.wait_ge(pads_set, 3 * CB)
                    dve.tensor_tensor_scan(fl(qsum), fl(a2), fl(e2), 0.0, ALU.mult, ALU.add).then_inc(qscan_done, 1)
                    dve.wait_ge(ev2_done, c + 1)
                    dve.tensor_tensor_scan(fl(psum), fl(a2), fl(ev2), 0.0, ALU.mult, ALU.add).then_inc(pscan_done, 1)
                    dve.wait_ge(aq_done, c + 1)
                    dve.tensor_tensor(e1[c][:, :, :], qsum[c][:, :, 0:P], e1[c][:, :, :], ALU.add).then_inc(den_done, 1)
                    dve.wait_ge(pscan_done, c + 1)
                    dve.tensor_tensor(a1[c][:, :, :], psum[c][:, :, 0:P], a1[c][:, :, :], ALU.mult).then_inc(ap_done, 1)
                    dve.wait_ge(den_done, c + 1)
                    dve.reciprocal(e1[c][:, :, :], e1[c][:, :, :]).then_inc(rden_done, 1)
                    dve.wait_ge(ap_done, c + 1)
                    dve.wait_ge(ev1_done, c + 1)
                    dve.tensor_tensor(a1[c][:, :, :], a1[c][:, :, :], ev1[c][:, :, :], ALU.add).then_inc(num_done, 1)
                    dve.wait_ge(num_done, c + 1)
                    dve.wait_ge(rden_done, c + 1)
                    dve.tensor_tensor(a1[c][:, :, :], a1[c][:, :, :], e1[c][:, :, :], ALU.mult).then_inc(yT_done, 1)
                for j in range(4):
                    dve.wait_ge(y_done, j + 1)
                    dve.tensor_tensor(k.x1[:, 2 * j:2 * j + 2, :], k.x1[:, 2 * j:2 * j + 2, :], y_ps[:, 2 * j:2 * j + 2, :],
                                      ALU.add).then_inc(x1_done, 1)
H0, KV0, HD0 = 16, 4, 128
G0 = H0 // KV0


def attention_stage(nc, k, io):
    with Memory(nc) as m:
        stats, mv = m.sb("b_stats", [P, B, 6]), m.sb("b_mean_var", [P, B, 2])
        sd, rstd = m.sb("b_sd", [P, B]), m.sb("b_rstd", [P, B])
        ssq, rms, rrms = m.sb("b_ssq", [P, B]), m.sb("b_rms", [P, B]), m.sb("b_rrms", [P, B])
        square = m.sb("b_square", [P, C])
        wq, wk = m.sb("wq0", [P, CB, H0 * HD0]), m.sb("wk0", [P, CB, KV0 * HD0])
        wv, wo = m.sb("wv0", [P, CB, KV0 * HD0]), m.sb("wo0", [P, H0, C])
        ln_w = m.sb("ln_w", [P, CB])
        rope = m.sb("rope", [P, 4, HD0])
        causal = m.sb("causal", [P, G0, P], bf16)
        identb = m.sb("identb", [P, P], bf16)
        hn = m.sb("hn", [P, C])
        hT = m.sb("hT", [P, CB, P])
        by_cos = [m.sb(f"by_cos{i}", [P, G0, HD0]) for i in range(2)]
        by_sin = [m.sb(f"by_sin{i}", [P, G0, HD0]) for i in range(2)]
        rot = [m.sb(f"rot{i}", [P, G0, HD0]) for i in range(2)]
        kT = [m.sb(f"kT{i}", [P, KV0, P]) for i in range(2)]
        qT = [m.sb(f"qT{i}", [P, H0, P]) for i in range(2)]
        v = [m.sb(f"v{i}", [P, KV0, HD0]) for i in range(2)]
        negmax, rsum, rinv = m.sb("negmax", [P, H0]), m.sb("rsum", [P, H0]), m.sb("rinv", [P, H0])
        pe_ = [m.sb(f"probs{i}", [P, G0, P]) for i in range(2)]
        pn = [m.sb(f"probs_n{i}", [P, G0, P]) for i in range(2)]
        pT = [m.sb(f"probsT{i}", [P, G0, P]) for i in range(2)]
        oT = m.sb("oT", [P, H0, P])
        qkv_ps = [m.ps(f"qkv_ps{i}", [P, G0, HD0]) for i in range(2)]
        turn_ps = m.ps("turn_ps", [P, 4, P])
        s_ps = [m.ps(f"s_ps{i}", [P, G0, P]) for i in range(2)]
        pT_ps = m.ps("pT_ps", [P, G0, P])
        o_ps = m.ps("o_ps", [P, G0, P])
        wo_ps = m.ps("wo_ps", [P, C])

        weights_in, consts_in = m.sem("weights_in"), m.sem("consts_in")
        stats_done, var_done, sd_done, rstd_done = m.sem("b_stats_done"), m.sem("b_var_done"), m.sem("b_sd_done"), m.sem("b_rstd_done")
        z_done, ssq_done, rms_done, rrms_done = m.sem("z_done"), m.sem("ssq_done"), m.sem("rms_done"), m.sem("rrms_done")
        hn_done, hT_made, hT_out = m.sem("hn_done"), m.sem("hT_made"), m.sem("hT_out")
        qkv_made, v_out = m.sem("qkv_made"), m.sem("v_out")
        rope_mul, rot_done, rT_made, rT_out = m.sem("rope_mul"), m.sem("rot_done"), m.sem("rT_made"), m.sem("rT_out")
        s_made, max_done, exp_done, rinv_done = m.sem("s_made"), m.sem("max_done"), m.sem("exp_done"), m.sem("rinv_done")
        pn_done, pT_made, pT_out = m.sem("pn_done"), m.sem("pT_made"), m.sem("pT_out")
        o_made, o_out, wo_made, xa_done = m.sem("o_made"), m.sem("o_out"), m.sem("wo_made"), m.sem("xa_done")
        NG = 1 + KV0

        def pipeline(eng, front, step):
            front(0, 0)
            step(0, 0, False)
            with eng.Fori(0, B // 2 - 1) as i:
                step(2 * i + 1, 1, False)
                step(2 * i + 2, 0, False)
            step(B - 1, 1, True)

        with nc.Block() as block:

            @block.sync
            def _(sp):
                sp.dma_start(ln_w[:, :], io["ln_w"]).then_inc(consts_in, 16)
                sp.dma_start(rope[:, :, :], io["rope"]).then_inc(consts_in, 16)
                sp.dma_start(causal[:, :, :], io["causal"]).then_inc(consts_in, 16)
                sp.dma_start(identb[:, :], io["identb"]).then_inc(consts_in, 16)
                for w, name in ((wk, "wk0"), (wq, "wq0"), (wv, "wv0")):
                    sp.dma_start(w[:, :, :], io[name].rearrange("(cb p) o -> p cb o", p=P)).then_inc(weights_in, 16)
                sp.dma_start(wo[:, :, :], io["wo0"].rearrange("(h p) o -> p h o", p=P)).then_inc(weights_in, 16)

            @block.scalar
            def _(act):
                for h in range(2):
                    act.wait_ge(var_done, HB * (h + 1))
                    act.activation(sd[:, HB * h:HB * (h + 1)], mv[:, HB * h:HB * (h + 1), 1], ACT.Sqrt,
                                   bias=k.eps[:, 0:1]).then_inc(sd_done, 1)
                for b in range(B):
                    act.wait_ge(z_done, b + 1)
                    if b:
                        act.wait_ge(ssq_done, b)
                    act.activation(square[:, :], k.z[:, b, :], ACT.Square, accum_out=ssq[:, b:b + 1]).then_inc(ssq_done, 1)
                act.wait_ge(ssq_done, B)
                act.activation(rms[:, :], ssq[:, :], ACT.Sqrt, bias=k.eps[:, 0:1], scale=1.0 / C).then_inc(rms_done, 1)

                def hT_copy(f):
                    act.wait_ge(hT_made, f + 1)
                    wait_past(act, qkv_made, 6 * f)
                    for c in range(CB):
                        act.activation(hT[:, c, :], turn_ps[:, c, :], ACT.Copy, scale=ln_w[:, c:c + 1]).then_inc(hT_out, 1)

                def rT_copy(f, par, j):
                    act.wait_ge(rT_made, NG * f + j + 1)
                    if j < 2:
                        wait_past(act, s_made, 4 * (f - 1))
                    dst = kT[par][:, :, :] if j == 0 else qT[par][:, G0 * (j - 1):G0 * j, :]
                    act.activation(dst, turn_ps[:, :, :], ACT.Copy).then_inc(rT_out, 1)

                def v_copy(f, par):
                    act.wait_ge(qkv_made, 6 * f + 6)
                    wait_past(act, o_made, 4 * (f - 1))
                    act.activation(v[par][:, :, :], qkv_ps[1][:, :, :], ACT.Copy).then_inc(v_out, 1)

                def exps(it, g):
                    act.wait_ge(max_done, 4 * it + g + 1)
                    wait_past(act, pn_done, 4 * it + max(g - 1, 0))
                    for h in range(G0):
                        act.activation(pe_[g % 2][:, h, :], s_ps[g % 2][:, h, :], ACT.Exp,
                                       bias=negmax[:, G0 * g + h:G0 * g + h + 1],
                                       accum_out=rsum[:, G0 * g + h:G0 * g + h + 1]).then_inc(exp_done, 1)

                def o_copy(it, g):
                    act.wait_ge(o_made, 4 * it + g + 1)
                    if g == 0:
                        wait_past(act, wo_made, it)
                    act.activation(oT[:, G0 * g:G0 * (g + 1), :], o_ps[:, :, :], ACT.Copy).then_inc(o_out, 1)

                def front(f, par):
                    hT_copy(f)
                    for j in range(4):
                        rT_copy(f, par, j)
                    v_copy(f, par)
                    rT_copy(f, par, 4)

                def step(it, par, last):
                    nxt = 1 - par
                    exps(it, 0)
                    if not last:
                        hT_copy(it + 1)
                    exps(it, 1)
                    o_copy(it, 0)
                    exps(it, 2)
                    if not last:
                        rT_copy(it + 1, nxt, 0)
                    o_copy(it, 1)
                    exps(it, 3)
                    if not last:
                        rT_copy(it + 1, nxt, 1)
                    o_copy(it, 2)
                    if not last:
                        rT_copy(it + 1, nxt, 2)
                    o_copy(it, 3)
                    if not last:
                        rT_copy(it + 1, nxt, 3)
                        v_copy(it + 1, nxt)
                        rT_copy(it + 1, nxt, 4)

                pipeline(act, front, step)

            @block.tensor
            def _(pe):
                def turn_h(f):
                    pe.wait_ge(hn_done, f + 1)
                    wait_past(pe, rT_out, NG * f)
                    for c in range(CB):
                        t = pe.transpose(turn_ps[:, c, :], hn[:, P * c:P * (c + 1)], k.ident[:, :])
                    t.then_inc(hT_made, 1)

                def project(f, c):
                    if c == 0:
                        pe.wait_ge(hT_out, 2 * (f + 1))
                        wait_past(pe, rope_mul, 2 * NG * f)
                    elif c == 1:
                        wait_past(pe, v_out, f)
                    else:
                        pe.wait_ge(rope_mul, 2 * (NG * f + c - 1))
                    for cb in range(CB):
                        w = wk[:, cb, :] if c == 0 else wv[:, cb, :] if c == 5 else wq[:, cb, 512 * (c - 1):512 * c]
                        t = pe.matmul(qkv_ps[c % 2][:, :, :].rearrange("p h d -> p (h d)"), hT[:, cb, :], w,
                                      start=(cb == 0), stop=(cb == CB - 1))
                    t.then_inc(qkv_made, 1)

                def turn_r(f, par, j):
                    pe.wait_ge(rot_done, NG * f + j + 1)
                    if j == 0:
                        pe.wait_ge(hT_out, 2 * (f + 1))
                    else:
                        pe.wait_ge(rT_out, NG * f + j)
                    for h in range(G0):
                        t = pe.transpose(turn_ps[:, h, :], rot[(par + j) % 2][:, h, :], k.ident[:, :])
                    t.then_inc(rT_made, 1)

                def scores(it, par, g):
                    pe.wait_ge(rT_out, NG * it + g + 2)
                    wait_past(pe, exp_done, 16 * it + 4 * max(g - 1, 0))
                    pe.matmul(s_ps[g % 2][:, :, :].rearrange("p h s -> p (h s)"), identb[:, :],
                              causal[:, :, :].rearrange("p h s -> p (h s)"), start=True, stop=False, skip_group_check=True)
                    for h in range(G0):
                        t = pe.matmul(s_ps[g % 2][:, h, :], qT[par][:, G0 * g + h, :], kT[par][:, g, :],
                                      start=False, stop=(h == G0 - 1), skip_group_check=True)
                    t.then_inc(s_made, 1)

                def turn_p(it, g):
                    pe.wait_ge(pn_done, 4 * it + g + 1)
                    wait_past(pe, pT_out, 4 * it + g)
                    for h in range(G0):
                        t = pe.transpose(pT_ps[:, h, :], pn[g % 2][:, h, :], k.ident[:, :])
                    t.then_inc(pT_made, 1)

                def mix(it, par, g):
                    pe.wait_ge(pT_out, 4 * it + g + 1)
                    wait_past(pe, o_out, 4 * it + g)
                    pe.wait_ge(v_out, it + 1)
                    pe.matmul(o_ps[:, :, :].rearrange("p h s -> p (h s)"), v[par][:, g, :],
                              pT[g % 2][:, :, :].rearrange("p h s -> p (h s)"), start=True, stop=True).then_inc(o_made, 1)

                def output(it):
                    pe.wait_ge(o_out, 4 * it + 4)
                    wait_past(pe, xa_done, it)
                    for h in range(H0):
                        t = pe.matmul(wo_ps[:, :], oT[:, h, :], wo[:, h, :], start=(h == 0), stop=(h == H0 - 1))
                    t.then_inc(wo_made, 1)

                def front(f, par):
                    turn_h(f)
                    project(f, 0)
                    project(f, 1)
                    for j in range(4):
                        turn_r(f, par, j)
                        project(f, j + 2)
                    turn_r(f, par, 4)

                def step(it, par, last):
                    nxt = 1 - par
                    scores(it, par, 0)
                    scores(it, par, 1)
                    if not last:
                        turn_h(it + 1)
                        project(it + 1, 0)
                    turn_p(it, 0)
                    if not last:
                        project(it + 1, 1)
                    mix(it, par, 0)
                    scores(it, par, 2)
                    if not last:
                        turn_r(it + 1, nxt, 0)
                    turn_p(it, 1)
                    if not last:
                        project(it + 1, 2)
                    mix(it, par, 1)
                    scores(it, par, 3)
                    if not last:
                        turn_r(it + 1, nxt, 1)
                        project(it + 1, 3)
                    turn_p(it, 2)
                    mix(it, par, 2)
                    if not last:
                        turn_r(it + 1, nxt, 2)
                        project(it + 1, 4)
                    turn_p(it, 3)
                    mix(it, par, 3)
                    if not last:
                        turn_r(it + 1, nxt, 3)
                        project(it + 1, 5)
                        turn_r(it + 1, nxt, 4)
                    output(it)

                pe.wait_ge(weights_in, 64)
                pe.wait_ge(consts_in, 64)
                pipeline(pe, front, step)

            @block.gpsimd
            def _(pool):
                def rotate(f, par, j):
                    i = (par + j) % 2
                    pool.wait_ge(rope_mul, 2 * (NG * f + j + 1))
                    wait_past(pool, rT_made, NG * f + j - 1)
                    pool.tensor_tensor(rot[i][:, :, :], by_cos[i][:, :, :], by_sin[i][:, :, :], ALU.add).then_inc(rot_done, 1)

                def normalise(it, g):
                    pool.wait_ge(rinv_done, 4 * it + g + 1)
                    wait_past(pool, pT_made, 4 * it + max(g - 1, 0))
                    pool.tensor_tensor(pn[g % 2][:, :, :], pe_[g % 2][:, :, :],
                                       rinv[:, G0 * g:G0 * (g + 1)].unsqueeze(2).to_broadcast([P, G0, P]),
                                       ALU.mult).then_inc(pn_done, 1)

                def front(f, par):
                    for j in range(NG):
                        rotate(f, par, j)

                def step(it, par, last):
                    nxt = 1 - par
                    order = ["n0", "r0", "n1", "r1", "r2", "n2", "r3", "n3", "r4"]
                    for what in order:
                        j = int(what[1])
                        if what[0] == "n":
                            normalise(it, j)
                        elif not last:
                            rotate(it + 1, nxt, j)

                pipeline(pool, front, step)

            @block.vector
            def _(dve):
                for b in range(B):
                    dve.bn_stats(stats[:, b, :], k.x1[:, b, :]).then_inc(stats_done, 1)
                for b in range(B):
                    dve.wait_ge(stats_done, b + 1)
                    dve.bn_aggr(mv[:, b, :], stats[:, b, :]).then_inc(var_done, 1)
                for h in range(2):
                    dve.wait_ge(sd_done, h + 1)
                    dve.reciprocal(rstd[:, HB * h:HB * (h + 1)], sd[:, HB * h:HB * (h + 1)]).then_inc(rstd_done, 1)
                for h in range(2):
                    dve.wait_ge(rstd_done, h + 1)
                    for b in range(HB * h, HB * (h + 1)):
                        dve.tensor_scalar(k.z[:, b, :], k.x1[:, b, :], mv[:, b, 0:1], rstd[:, b:b + 1],
                                          ALU.subtract, ALU.mult).then_inc(z_done, 1)
                dve.wait_ge(rms_done, 1)
                dve.reciprocal(rrms[:, :], rms[:, :]).then_inc(rrms_done, 1)
                dve.wait_ge(rrms_done, 1)
                dve.wait_ge(z_done, B)
                dve.wait_ge(consts_in, 64)

                def scale_h(f):
                    wait_past(dve, hT_made, f)
                    dve.tensor_scalar(hn[:, :], k.z[:, bass.ds(f, 1), :], rrms[:, bass.ds(f, 1)], None,
                                      ALU.mult).then_inc(hn_done, 1)

                def rotary(f, par, j):
                    i, tab = (par + j) % 2, 2 if j == 0 else 0
                    dve.wait_ge(qkv_made, 6 * f + j + 1)
                    wait_past(dve, rot_done, NG * f + j - 1)
                    src, half = qkv_ps[j % 2], HD0 // 2
                    dve.tensor_tensor(by_cos[i][:, :, :], src[:, :, :],
                                      rope[:, tab:tab + 1, :].to_broadcast([P, G0, HD0]), ALU.mult).then_inc(rope_mul, 1)
                    swapped = by_sin[i][:, :, :].rearrange("p h (a d) -> p h a d", a=2)
                    pairs = src[:, :, :].rearrange("p h (a d) -> p h a d", a=2)[:, :, ::-1, :]
                    dve.tensor_tensor(swapped, pairs,
                                      rope[:, tab + 1:tab + 2, :].rearrange("p o (a d) -> p o a d", a=2)
                                      .to_broadcast([P, G0, 2, half]), ALU.mult).then_inc(rope_mul, 1)

                def maxima(it, g):
                    dve.wait_ge(s_made, 4 * it + g + 1)
                    dve.tensor_reduce(negmax[:, G0 * g:G0 * (g + 1)], s_ps[g % 2][:, :, :], AX.X, ALU.max,
                                      negate=True).then_inc(max_done, 1)

                def reciprocals(it, g):
                    dve.wait_ge(exp_done, 16 * it + 4 * g + 4)
                    wait_past(dve, pn_done, 4 * it)
                    dve.reciprocal(rinv[:, G0 * g:G0 * (g + 1)], rsum[:, G0 * g:G0 * (g + 1)]).then_inc(rinv_done, 1)

                def pT_copy(it, g):
                    dve.wait_ge(pT_made, 4 * it + g + 1)
                    wait_past(dve, o_made, 4 * it + max(g - 1, 0))
                    dve.tensor_copy(pT[g % 2][:, :, :], pT_ps[:, :, :]).then_inc(pT_out, 1)

                def add_residual(it):
                    dve.wait_ge(wo_made, it + 1)
                    dve.tensor_tensor(k.xa[:, bass.ds(it, 1), :], k.z[:, bass.ds(it, 1), :], wo_ps[:, :].unsqueeze(1),
                                      ALU.add).then_inc(xa_done, 1)

                def front(f, par):
                    scale_h(f)
                    for j in range(NG):
                        rotary(f, par, j)

                def step(it, par, last):
                    nxt = 1 - par
                    if not last:
                        scale_h(it + 1)
                    maxima(it, 0)
                    maxima(it, 1)
                    reciprocals(it, 0)
                    if not last:
                        rotary(it + 1, nxt, 0)
                    pT_copy(it, 0)
                    reciprocals(it, 1)
                    maxima(it, 2)
                    if not last:
                        rotary(it + 1, nxt, 1)
                    pT_copy(it, 1)
                    maxima(it, 3)
                    if not last:
                        rotary(it + 1, nxt, 2)
                    reciprocals(it, 2)
                    pT_copy(it, 2)
                    if not last:
                        rotary(it + 1, nxt, 3)
                    reciprocals(it, 3)
                    pT_copy(it, 3)
                    if not last:
                        rotary(it + 1, nxt, 4)
                    add_residual(it)

                pipeline(dve, front, step)
def earlier(j, par):
    return (j - par) // 2 if isinstance(j, int) else (j - par) >> 1


E0, FF0 = 8, 896
FB = FF0 // P
SLOTS = 256
SG = SLOTS // P
TILES = 2 * T // SLOTS + E0 - 1


def experts0_stage(nc, k, io):
    x_slots = nc.dram_tensor("x_slots", (TILES * SLOTS, C), fp32, kind="Internal").ap()
    y_slots = nc.dram_tensor("y_slots", (TILES * SLOTS, C), fp32, kind="Internal").ap()
    with Memory(nc) as m:
        square = m.sb("c_square", [P, C])
        ssq, rms, rrms = m.sb("c_ssq", [P, B]), m.sb("c_rms", [P, B]), m.sb("c_rrms", [P, B])
        ff_w, gate_w = m.sb("ff_w", [P, C]), m.sb("gate_w", [P, CB, E0])
        iota_e, iota_t = m.sb("iota_e", [P, E0]), m.sb("iota_t", [P, TILES])
        before, ones = m.sb("before", [P, P], bf16), m.sb("ones", [P, P], bf16)
        zeros = m.sb("zeros", [P, 1920])
        h2, h2T = m.sb("h2", [P, B, C]), m.sb("h2T", [P, B, C])
        logits = m.sb("logits", [P, B, E0])
        top, top_i, top_f = m.sb("top", [P, B, 8]), m.sb("top_i", [P, B, 8], u32), m.sb("top_f", [P, B, 2])
        gap, gap_exp, gate_den = m.sb("gap", [P, B]), m.sb("gap_exp", [P, B]), m.sb("gate_den", [P, B])
        gates = m.sb("gates", [P, 2, B])
        pick = m.sb("pick", [P, 2, B, E0])
        picked = m.sb("picked", [P, B, E0], bf16)
        count, tiles_of = m.sb("count", [P, E0]), m.sb("tiles_of", [P, 4, E0])
        tile_end, first_slot = m.sb("tile_end", [P, E0]), m.sb("first_slot", [P, E0])
        place = m.sb("place", [P, B, E0])
        at = m.sb("at", [P, 2, B, E0])
        slot_f, slot = m.sb("slot_f", [P, 2 * B]), m.sb("slot", [P, 2 * B], u32)
        ended, expert_f = m.sb("ended", [P, TILES, E0]), m.sb("expert_f", [P, TILES])
        expert = m.sb("expert", [P, TILES], u32)
        w1 = [m.sb(f"w1_{i}", [P, CB, FF0]) for i in range(2)]
        w3 = [m.sb(f"w3_{i}", [P, CB, FF0]) for i in range(2)]
        w2 = [m.sb(f"w2_{i}", [P, FB, C]) for i in range(2)]
        xs = [m.sb(f"xs{i}", [P, SG, C]) for i in range(2)]
        xT = [m.sb(f"xT{i}", [P, CB, SLOTS]) for i in range(2)]
        silu = [m.sb(f"silu{i}", [P, SLOTS]) for i in range(2)]
        hid = [m.sb(f"hid{i}", [P, FB, SLOTS]) for i in range(2)]
        ys = [m.sb(f"ys{i}", [P, SG, C]) for i in range(2)]
        y_pair = m.sb("y_pair", [P, 2 * B, C])
        xT_ps = m.ps("xT_ps", [P, CB, SLOTS])
        gu_ps = [m.ps(f"gu_ps{i}", [P, 2, SLOTS]) for i in range(4)]
        y_ps = m.ps("ey_ps", [P, SG, C])
        cnt_ps = m.ps("cnt_ps", [P, 3, B, E0])

        s = lambda name: m.sem("c_" + name)
        consts_in, zeros_set, slots_clear = s("consts_in"), s("zeros_set"), s("slots_clear")
        ssq_done, rms_done, rrms_done, h2_done, h2T_made, h2T_out = s("ssq"), s("rms"), s("rrms"), s("h2"), s("h2T_made"), s("h2T_out")
        logits_made, logits_out, top_done, index_done, index_f = s("logits_made"), s("logits_out"), s("top"), s("index"), s("index_f")
        gap_done, gap_exp_done, gate_step = s("gap"), s("gap_exp"), s("gate_step")
        pick_done, picked_done, ranks_made, plan_step = s("pick"), s("picked"), s("ranks_made"), s("plan_step")
        slot_done, expert_done, sent = s("slot"), s("expert"), s("sent")
        w1_in = [s(f"w1_in{i}") for i in range(2)]
        w3_in = [s(f"w3_in{i}") for i in range(2)]
        w2_in = [s(f"w2_in{i}") for i in range(2)]
        xs_in = [s(f"xs_in{i}") for i in range(2)]
        xT_made, xT_out, gu_made, silu_done, hid_done = s("xT_made"), s("xT_out"), s("gu_made"), s("silu"), s("hid")
        y_made, y_out = s("y_made"), s("y_out")
        stored = [s(f"stored{i}") for i in range(2)]
        base_done, x2_step = s("base"), s("x2_step")
        fetched = [s(f"fetched{b}") for b in range(B)]

        def tiles(eng, step):
            step(0, 0)
            step(1, 1)
            with eng.Fori(1, TILES // 2) as i:
                step(2 * i, 0)
                step(2 * i + 1, 1)
            step(TILES - 1, 0)

        with nc.Block() as block:

            @block.sync
            def _(sp):
                sp.dma_start(ff_w[:, :], io["ff_w"]).then_inc(consts_in, 16)
                sp.dma_start(gate_w[:, :, :], io["gate_w0"].rearrange("(cb p) e -> p cb e", p=P)).then_inc(consts_in, 16)
                sp.dma_start(iota_e[:, :], io["iota"][:, 0:E0]).then_inc(consts_in, 16)
                sp.dma_start(iota_t[:, :], io["iota"][:, 0:TILES]).then_inc(consts_in, 16)
                sp.dma_start(before[:, :], io["before"]).then_inc(consts_in, 16)
                sp.dma_start(ones[:, :], io["ones"]).then_inc(consts_in, 16)
                sp.wait_ge(zeros_set, 1)
                flat = x_slots.rearrange("(p r) c -> p (r c)", p=P)
                for i in range(4):
                    sp.dma_start(flat[:, 1920 * i:1920 * (i + 1)], zeros[:, :]).then_inc(slots_clear, 16)
                sp.wait_ge(expert_done, 1)

                def load(j, par):
                    e = sp.value_load(expert[0:1, bass.ds(j, 1)], min_val=0, max_val=E0 - 1)
                    wait_past(sp, y_made, 2 * (j - 1))
                    for w, w_in, name in ((w1, w1_in, "w1"), (w3, w3_in, "w3")):
                        sp.dma_start(w[par][:, :, :], io[name][bass.ds(e, 1), :, :].rearrange("o (cb p) f -> (o p) cb f", p=P)).then_inc(w_in[par], 16)
                    sp.dma_start(w2[par][:, :, :], io["w2"][bass.ds(e, 1), :, :].rearrange("o (fb p) c -> (o p) fb c", p=P)).then_inc(w2_in[par], 16)
                    if isinstance(j, int) and j == 0:
                        sp.wait_ge(sent, 16 * 2 * B)
                    sp.dma_start(xs[par][:, :, :], x_slots[bass.ds(j * SLOTS, SLOTS), :].rearrange("(r p) c -> p r c", p=P)).then_inc(xs_in[par], 16)

                tiles(sp, load)
                for h in range(2):
                    sp.wait_ge(stored[h], 16 * ((TILES + 1 - h) // 2))

            @block.scalar
            def _(act):
                for b in range(B):
                    if b:
                        act.wait_ge(ssq_done, b)
                    act.activation(square[:, :], k.xa[:, b, :], ACT.Square, accum_out=ssq[:, b:b + 1]).then_inc(ssq_done, 1)
                act.wait_ge(ssq_done, B)
                act.activation(rms[:, :], ssq[:, :], ACT.Sqrt, bias=k.eps[:, 0:1], scale=1.0 / C).then_inc(rms_done, 1)
                for n in range(B // 2):
                    act.wait_ge(h2T_made, n + 1)
                    act.activation(h2T[:, 2 * n:2 * n + 2, :], gu_ps[n][:, :, :], ACT.Copy).then_inc(h2T_out, 1)
                act.wait_ge(logits_made, 1)
                act.activation(logits[:, :, :], cnt_ps[:, 0, :, :], ACT.Copy).then_inc(logits_out, 1)
                act.wait_ge(gap_done, 1)
                act.activation(gap_exp[:, :], gap[:, :], ACT.Exp).then_inc(gap_exp_done, 1)

                def work(j, par):
                    act.wait_ge(xT_made, j + 1)
                    wait_past(act, gu_made, FB * (j - 1))
                    act.activation(xT[par][:, :, :], xT_ps[:, :, :], ACT.Copy).then_inc(xT_out, 1)
                    for f in range(FB):
                        i = (par + f) % 2
                        act.wait_ge(gu_made, FB * j + f + 1)
                        wait_past(act, hid_done, FB * j + f - 1)
                        act.activation(silu[i][:, :], gu_ps[f % 4][:, 0, :], ACT.Silu).then_inc(silu_done, 1)
                        if f == 3 and not (isinstance(j, int) and j == 0):
                            store(j - 1, 1 - par)

                def store(j, par):
                    act.wait_ge(y_made, 2 * j + 2)
                    wait_past(act, stored[par], 16 * earlier(j, par))
                    act.activation(ys[par][:, :, :], y_ps[:, :, :], ACT.Copy).then_inc(y_out, 1)
                    act.wait_ge(y_out, j + 1)
                    act.dma_start(y_slots[bass.ds(j * SLOTS, SLOTS), :].rearrange("(r p) c -> p r c", p=P),
                                  ys[par][:, :, :]).then_inc(stored[par], 16)

                tiles(act, work)
                store(TILES - 1, 0)

            @block.tensor
            def _(pe):
                for b in range(B):
                    pe.wait_ge(h2_done, b + 1)
                    for c in range(CB):
                        t = pe.transpose(gu_ps[b // 2][:, b % 2, P * c:P * (c + 1)], h2[:, b, P * c:P * (c + 1)], k.ident[:, :])
                    if b % 2:
                        t.then_inc(h2T_made, 1)
                pe.wait_ge(consts_in, 96)
                for b in range(B):
                    pe.wait_ge(h2T_out, b // 2 + 1)
                    for c in range(CB):
                        t = pe.matmul(cnt_ps[:, 0, b, :], h2T[:, b, P * c:P * (c + 1)], gate_w[:, c, :],
                                      start=(c == 0), stop=(c == CB - 1))
                t.then_inc(logits_made, 1)
                pe.wait_ge(picked_done, 1)
                pe.wait_ge(logits_out, 1)
                flat = lambda a: a.rearrange("p b e -> p (b e)")
                pe.matmul(flat(cnt_ps[:, 2, :, :]), ones[:, :], flat(picked[:, :, :]), start=True, stop=True, skip_group_check=True)
                pe.matmul(flat(cnt_ps[:, 1, :, :]), before[:, :], flat(picked[:, :, :]), start=True, stop=False, skip_group_check=True)
                for b in range(B - 1):
                    t = pe.matmul(cnt_ps[:, 1, b + 1:B, :], ones[:, :], picked[:, b:b + 1, :].to_broadcast([P, B - 1 - b, E0]),
                                  start=False, stop=(b == B - 2), skip_group_check=True)
                t.then_inc(ranks_made, 1)

                def turn(j, par):
                    pe.wait_ge(xs_in[par], 16 * earlier(j, par) + 16)
                    wait_past(pe, xT_out, j)
                    for r in range(SG):
                        for c in range(CB):
                            t = pe.transpose(xT_ps[:, c, P * r:P * (r + 1)], xs[par][:, r, P * c:P * (c + 1)], k.ident[:, :])
                    t.then_inc(xT_made, 1)

                def up(j, par, blocks):
                    for f in blocks:
                        if f == 0:
                            pe.wait_ge(xT_out, j + 1)
                            pe.wait_ge(w1_in[par], 16 * earlier(j, par) + 16)
                            pe.wait_ge(w3_in[par], 16 * earlier(j, par) + 16)
                        wait_past(pe, hid_done, FB * j + f - 3 if f >= 4 else FB * j)
                        for n, w in enumerate((w1, w3)):
                            for c in range(CB):
                                t = pe.matmul(gu_ps[f % 4][:, n, :], w[par][:, c, P * f:P * (f + 1)], xT[par][:, c, :],
                                              start=(c == 0), stop=(c == CB - 1))
                        t.then_inc(gu_made, 1)

                def down(j, par):
                    pe.wait_ge(w2_in[par], 16 * earlier(j, par) + 16)
                    pe.wait_ge(hid_done, FB * (j + 1))
                    wait_past(pe, y_out, j)
                    for r in range(SG):
                        for f in range(FB):
                            t = pe.matmul(y_ps[:, r, :], hid[par][:, f, P * r:P * (r + 1)], w2[par][:, f, :],
                                          start=(f == 0), stop=(f == FB - 1))
                        t.then_inc(y_made, 1)

                def work(j, par):
                    turn(j, par)
                    up(j, par, range(0, 3))
                    if not (isinstance(j, int) and j == 0):
                        down(j - 1, 1 - par)
                    up(j, par, range(3, FB))

                tiles(pe, work)
                down(TILES - 1, 0)

            @block.gpsimd
            def _(pool):
                for b in range(B):
                    pool.tensor_tensor(k.x1[:, b, :], k.x1[:, b, :], k.xa[:, b, :], ALU.add).then_inc(base_done, 1)
                pool.wait_ge(slots_clear, 64)
                for n in range(2 * B):
                    pool.wait_ge(slot_done, 1)
                    pool.wait_ge(h2_done, n % B + 1)
                    pool.indirect_dma_start(x_slots, bass.IndirectOffsetOnAxis(slot[:, n:n + 1], 0), h2[:, n % B, :],
                                            None).then_inc(sent, 16)
                for h in range(2):
                    pool.wait_ge(stored[h], 16 * ((TILES + 1 - h) // 2))
                for b in range(B):
                    for i in range(2):
                        n = B * i + b
                        pool.indirect_dma_start(y_pair[:, n, :], None, y_slots, bass.IndirectOffsetOnAxis(slot[:, n:n + 1], 0)).then_inc(fetched[b], 16)

            @block.vector
            def _(dve):
                dve.memset(zeros[:, :], 0.0).then_inc(zeros_set, 1)
                dve.wait_ge(rms_done, 1)
                dve.reciprocal(rrms[:, :], rms[:, :]).then_inc(rrms_done, 1)
                dve.wait_ge(rrms_done, 1)
                dve.wait_ge(consts_in, 96)
                for b in range(B):
                    dve.scalar_tensor_tensor(h2[:, b, :], k.xa[:, b, :], rrms[:, b:b + 1], ff_w[:, :], ALU.mult, ALU.mult)\
                        .then_inc(h2_done, 1)
                dve.wait_ge(logits_out, 1)
                for b in range(B):
                    dve.max(top[:, b, :], logits[:, b, :]).then_inc(top_done, 1)
                for b in range(B):
                    dve.wait_ge(top_done, b + 1)
                    dve.max_index(top_i[:, b, :], top[:, b, :], logits[:, b, :]).then_inc(index_done, 1)
                dve.tensor_tensor(gap[:, :], top[:, :, 1], top[:, :, 0], ALU.subtract).then_inc(gap_done, 1)
                dve.wait_ge(index_done, B)
                dve.tensor_copy(top_f[:, :, :], top_i[:, :, 0:2]).then_inc(index_f, 1)
                dve.wait_ge(index_f, 1)
                for i in range(2):
                    dve.tensor_tensor(pick[:, i, :, :], iota_e[:, :].unsqueeze(1).to_broadcast([P, B, E0]),
                                      top_f[:, :, i:i + 1].to_broadcast([P, B, E0]), ALU.is_equal).then_inc(pick_done, 1)
                dve.wait_ge(pick_done, 2)
                dve.tensor_tensor(picked[:, :, :], pick[:, 0, :, :], pick[:, 1, :, :], ALU.add).then_inc(picked_done, 1)
                dve.wait_ge(gap_exp_done, 1)
                dve.tensor_scalar(gate_den[:, :], gap_exp[:, :], 1.0, None, ALU.add).then_inc(gate_step, 1)
                dve.wait_ge(gate_step, 1)
                dve.reciprocal(gates[:, 0, :], gate_den[:, :]).then_inc(gate_step, 1)
                dve.wait_ge(gate_step, 2)
                dve.tensor_tensor(gates[:, 1, :], gates[:, 0, :], gap_exp[:, :], ALU.mult).then_inc(gate_step, 1)
                dve.wait_ge(ranks_made, 1)
                dve.tensor_reduce(count[:, :], cnt_ps[:, 2, :, :].rearrange("p b e -> p e b"), AX.X, ALU.add).then_inc(plan_step, 1)
                dve.wait_ge(plan_step, 1)
                dve.tensor_scalar(tiles_of[:, 0, :], count[:, :], 0.0, None, ALU.is_gt).then_inc(plan_step, 1)
                for i in range(1, T // SLOTS):
                    dve.wait_ge(plan_step, i + 1)
                    dve.scalar_tensor_tensor(tiles_of[:, i, :], count[:, :], float(SLOTS * i), tiles_of[:, i - 1, :],
                                             ALU.is_gt, ALU.add).then_inc(plan_step, 1)
                last = T // SLOTS - 1
                dve.wait_ge(plan_step, last + 2)
                dve.tensor_tensor_scan(tile_end[:, :], tiles_of[:, last, :], tiles_of[:, last, :], 0.0, ALU.add, ALU.bypass)\
                    .then_inc(plan_step, 1)
                dve.wait_ge(plan_step, last + 3)
                dve.tensor_tensor(first_slot[:, :], tile_end[:, :], tiles_of[:, last, :], ALU.subtract).then_inc(plan_step, 1)
                dve.wait_ge(plan_step, last + 4)
                dve.scalar_tensor_tensor(place[:, :, :], first_slot[:, :].unsqueeze(1).to_broadcast([P, B, E0]), float(SLOTS),
                                         cnt_ps[:, 1, :, :], ALU.mult, ALU.add).then_inc(plan_step, 1)
                dve.wait_ge(plan_step, last + 5)
                for i in range(2):
                    dve.tensor_tensor(at[:, i, :, :], pick[:, i, :, :], place[:, :, :], ALU.mult).then_inc(plan_step, 1)
                dve.wait_ge(plan_step, last + 7)
                dve.tensor_reduce(slot_f[:, :], at[:, :, :, :].rearrange("p i b e -> p (i b) e"), AX.X, ALU.add).then_inc(plan_step, 1)
                dve.wait_ge(plan_step, last + 8)
                dve.tensor_copy(slot[:, :], slot_f[:, :]).then_inc(slot_done, 1)
                dve.tensor_tensor(ended[:, :, :], iota_t[:, :].unsqueeze(2).to_broadcast([P, TILES, E0]),
                                  tile_end[:, :].unsqueeze(1).to_broadcast([P, TILES, E0]), ALU.is_ge).then_inc(plan_step, 1)
                dve.wait_ge(plan_step, last + 9)
                dve.tensor_reduce(expert_f[:, :], ended[:, :, :], AX.X, ALU.add).then_inc(plan_step, 1)
                dve.wait_ge(plan_step, last + 10)
                dve.tensor_scalar(expert[:, :], expert_f[:, :], float(E0 - 1), None, ALU.min).then_inc(expert_done, 1)

                def work(j, par):
                    for f in range(FB):
                        i = (par + f) % 2
                        dve.wait_ge(silu_done, FB * j + f + 1)
                        if f == 0:
                            wait_past(dve, y_made, 2 * (j - 1))
                        dve.tensor_tensor(hid[par][:, f, :], gu_ps[f % 4][:, 1, :], silu[i][:, :], ALU.mult).then_inc(hid_done, 1)

                tiles(dve, work)
                dve.wait_ge(base_done, B)
                dve.wait_ge(gate_step, 3)
                for b in range(B):
                    dve.wait_ge(fetched[b], 32)
                    for i in range(2):
                        if i:
                            dve.wait_ge(x2_step, 2 * b + 1)
                        dve.scalar_tensor_tensor(k.x1[:, b, :], y_pair[:, B * i + b, :], gates[:, i, b:b + 1], k.x1[:, b, :],
                                                 ALU.mult, ALU.add).then_inc(x2_step, 1)
H1, HD1 = 16, 16
HG = 4
HPB = P // HD1
STRIDE = P + HD1
MAGIC = 1.5 * 2.0 ** 23
QMAX, QEPS = 127.0, 1e-8


def cross_stage(nc, k, io):
    with Memory(nc) as m:
        stats, mv = m.sb("d_stats", [P, B, 6]), m.sb("d_mean_var", [P, B, 2])
        sd, rstd = m.sb("d_sd", [P, B]), m.sb("d_rstd", [P, B])
        y = m.sb("d_y", [P, B, C])
        top, step_x, inv_x = m.sb("d_top", [P, 2, B]), m.sb("d_step", [P, 2, B]), m.sb("d_inv", [P, 2, B])
        yq = m.sb("d_yq", [P, B, C], bf16)
        yqT = m.sb("d_yqT", [P, CB, T], bf16)
        w = m.sb("d_w", [P, 2, CB, C])
        w_top, w_step, w_inv = m.sb("w_top", [P, 2 * CB]), m.sb("w_step", [P, 2 * CB]), m.sb("w_inv", [P, 2 * CB])
        w_q = m.sb("w_q", [P, 2, CB, C], bf16)
        w_qT = m.sb("w_qT", [P, 2, CB, C], bf16)
        w_diag = m.sb("w_diag", [P, 2 * CB, P])
        step_row = m.sb("step_row", [P, 2, C])
        bias_row = m.sb("bias_row", [P, 2, C])
        ones = m.sb("d_ones", [P, P])
        identb = m.sb("d_identb", [P, P], bf16)
        head_mask = m.sb("head_mask", [P, HPB])
        mask = m.sb("d_mask", [P, B, P])
        q1T = m.sb("q1T", [P, CB, T])
        qb = [m.sb(f"qb{i}", [P, CB, P]) for i in range(2)]
        kz = [m.sb(f"kz{i}", [P, H1, P]) for i in range(2)]
        vz = [m.sb(f"vz{i}", [P, CB, HPB * STRIDE]) for i in range(2)]
        sm = [m.sb(f"sm{i}", [P, HG, P]) for i in range(2)]
        probs = [m.sb(f"d_probs{i}", [P, HG, P]) for i in range(2)]
        pT = [m.sb(f"d_pT{i}", [P, HG, P]) for i in range(2)]
        negmax, rsum, rinv = m.sb("d_negmax", [P, H1]), m.sb("d_rsum", [P, H1]), m.sb("d_rinv", [P, H1])
        banks = [m.ps(f"d_bank{i}", [P, 512]) for i in range(8)]
        half = lambda i: banks[i][:, :].bitcast(bf16)

        s = lambda name: m.sem("d_" + name)
        consts_in, w_in, mask_in = s("consts_in"), s("w_in"), s("mask_in")
        ones_set, vz_set = s("ones_set"), s("vz_set")
        w_step_done, w_q_done, w_diag_done, w_turned, w_copied, row_made, row_out = (
            s("w_step"), s("w_q"), s("w_diag"), s("w_turned"), s("w_copied"), s("row_made"), s("row_out"))
        stats_done, var_done, sd_done, rstd_done, y_done = s("stats"), s("var"), s("sd"), s("rstd"), s("y")
        step_done, quant_done, yq_done = s("step"), s("quant"), s("yq")
        turned, yqT_out, q_made, q_scaled, q_done, qT_made, qT_out = (
            s("turned"), s("yqT_out"), s("q_made"), s("q_scaled"), s("q"), s("qT_made"), s("qT_out"))
        qb_done, kz_done, vz_done = s("qb"), s("kz"), s("vz")
        s_made, sm_done, max_done, exp_done, rinv_done = s("s_made"), s("sm"), s("max"), s("exp"), s("rinv")
        pT_made, pT_out, o_made, o_out = s("pT_made"), s("pT_out"), s("o_made"), s("o_out")
        r_made, r_step, x3_done = s("r_made"), s("r_step"), s("x3")

        def quantise(eng, src, out, which):
            for b in range(B):
                eng.tensor_scalar(src[:, b, :], src[:, b, :], inv_x[:, which, b:b + 1], QMAX, ALU.mult, ALU.min).then_inc(quant_done, 1)
            eng.wait_ge(quant_done, (B + 1) * which + B)
            eng.tensor_scalar(src[:, :, :], src[:, :, :], -QMAX, MAGIC, ALU.max, ALU.add).then_inc(quant_done, 1)
            eng.wait_ge(quant_done, (B + 1) * (which + 1))
            eng.tensor_scalar(out[:, :, :], src[:, :, :], MAGIC, None, ALU.subtract).then_inc(yq_done, 1)

        def row_steps(eng, src, which):
            eng.tensor_reduce(top[:, which, :], src[:, :, :], AX.X, ALU.max, apply_absolute_value=True).then_inc(step_done, 1)
            eng.wait_ge(step_done, 3 * which + 1)
            eng.tensor_scalar(step_x[:, which, :], top[:, which, :], 1.0 / QMAX, QEPS, ALU.mult, ALU.max).then_inc(step_done, 1)
            eng.wait_ge(step_done, 3 * which + 2)
            eng.reciprocal(inv_x[:, which, :], step_x[:, which, :]).then_inc(step_done, 1)
            eng.wait_ge(step_done, 3 * which + 3)

        def sequences(eng, step):
            step(0, 0, False)
            with eng.Fori(0, B // 2 - 1) as i:
                step(2 * i + 1, 1, False)
                step(2 * i + 2, 0, False)
            step(B - 1, 1, True)

        with nc.Block() as block:

            @block.sync
            def _(sp):
                sp.dma_start(w[:, 0, :, :], io["wq1"].rearrange("(ob p) c -> p ob c", p=P)).then_inc(w_in, 16)
                sp.dma_start(w[:, 1, :, :], io["wo1"].rearrange("(ob p) c -> p ob c", p=P)).then_inc(w_in, 16)
                sp.dma_start(bias_row[:, :, :], io["bias_row"]).then_inc(consts_in, 16)
                sp.dma_start(identb[:, :], io["identb"]).then_inc(consts_in, 16)
                sp.dma_start(head_mask[:, :], io["head_mask"]).then_inc(consts_in, 16)
                sp.dma_start(mask[:, :, :], io["mask"].rearrange("b q s -> q b s")).then_inc(mask_in, 16)

            @block.scalar
            def _(act):
                for h in range(2):
                    act.wait_ge(var_done, HB * (h + 1))
                    act.activation(sd[:, HB * h:HB * (h + 1)], mv[:, HB * h:HB * (h + 1), 1], ACT.Sqrt,
                                   bias=k.eps[:, 0:1]).then_inc(sd_done, 1)
                act.wait_ge(w_turned, 2)
                act.activation(w_qT[:, :, :, :].rearrange("p i c o -> p (i c o)"), half(0), ACT.Copy).then_inc(w_copied, 1)
                act.wait_ge(row_made, 1)
                act.activation(step_row[:, :, :].rearrange("p i c -> p (i c)"), banks[1][:, :], ACT.Copy).then_inc(row_out, 1)
                for c in range(CB):
                    act.wait_ge(turned, c + 1)
                    act.activation(yqT[:, c, :], half(2 + c), ACT.Copy).then_inc(yqT_out, 1)
                for c in range(CB):
                    for h in range(2):
                        n = 2 * c + h
                        act.wait_ge(qT_made, n + 1)
                        act.activation(q1T[:, c, 512 * h:512 * (h + 1)], banks[n][:, :], ACT.Copy).then_inc(qT_out, 1)

                def slots(f, par):
                    wait_past(act, s_made, 4 * (f - 1))
                    wait_past(act, o_made, 4 * (f - 1))
                    act.activation(qb[par][:, :, :], q1T[:, :, bass.ds(f * P, P)], ACT.Copy).then_inc(qb_done, 1)
                    act.activation(vz[par][:, :, :].rearrange("p c (j x) -> p c j x", x=STRIDE)[:, :, :, 0:HD1],
                                   k.vals1[:, bass.ds(f, 1), :].rearrange("p o (c j d) -> p (o c) j d", c=CB, d=HD1),
                                   ACT.Copy).then_inc(vz_done, 1)

                def exps(it, g):
                    act.wait_ge(max_done, 4 * it + g + 1)
                    wait_past(act, pT_made, 4 * it + g - 1)
                    if g == 0:
                        wait_past(act, rinv_done, it)
                    for h in range(HG):
                        n = HG * g + h
                        act.activation(probs[g % 2][:, h, :], sm[g % 2][:, h, :], ACT.Exp, bias=negmax[:, n:n + 1],
                                       accum_out=rsum[:, n:n + 1]).then_inc(exp_done, 1)

                act.wait_ge(qT_out, 4)
                act.wait_ge(vz_set, 2)
                slots(0, 0)
                exps(0, 0)
                exps(0, 1)

                def step(it, par, last):
                    if not last:
                        slots(it + 1, 1 - par)
                    exps(it, 2)
                    exps(it, 3)
                    if not last:
                        exps(it + 1, 0)
                        exps(it + 1, 1)

                sequences(act, step)
                for c in range(CB):
                    act.wait_ge(turned, CB + c + 1)
                    act.activation(yqT[:, c, :], half(2 + c), ACT.Copy).then_inc(yqT_out, 1)

            @block.tensor
            def _(pe):
                pe.wait_ge(consts_in, 48)
                pe.wait_ge(w_q_done, 1)
                for i in range(2):
                    for c in range(CB):
                        for ob in range(CB):
                            t = pe.transpose(half(0)[:, (i * CB + c) * C + P * ob:(i * CB + c) * C + P * (ob + 1)],
                                             w_q[:, i, ob, P * c:P * (c + 1)], identb[:, :])
                    t.then_inc(w_turned, 1)
                pe.wait_ge(w_diag_done, 2 * CB)
                pe.wait_ge(ones_set, 1)
                for n in range(2 * CB):
                    t = pe.matmul(banks[1][:, P * n:P * (n + 1)], ones[:, :], w_diag[:, n, :], start=True, stop=True)
                t.then_inc(row_made, 1)
                pe.wait_ge(yq_done, 1)
                for c in range(CB):
                    for b in range(B):
                        t = pe.transpose(half(2 + c)[:, P * b:P * (b + 1)], yq[:, b, P * c:P * (c + 1)], identb[:, :])
                    t.then_inc(turned, 1)
                pe.wait_ge(w_copied, 1)
                pe.wait_ge(yqT_out, CB)
                for b in range(B):
                    for c in range(CB):
                        t = pe.matmul(banks[4 + b // 2][:, C * (b % 2):C * (b % 2 + 1)], yqT[:, c, P * b:P * (b + 1)],
                                      w_qT[:, 0, c, :], start=(c == 0), stop=(c == CB - 1))
                    t.then_inc(q_made, 1)
                pe.wait_ge(row_out, 1)
                for c in range(CB):
                    for h in range(2):
                        pe.wait_ge(q_done, HB * (h + 1))
                        for b in range(HB * h, HB * (h + 1)):
                            t = pe.transpose(banks[2 * c + h][:, P * (b % HB):P * (b % HB + 1)], y[:, b, P * c:P * (c + 1)], k.ident[:, :])
                        t.then_inc(qT_made, 1)

                def scores(it, par, g):
                    if g == 0:
                        pe.wait_ge(qb_done, it + 1)
                        pe.wait_ge(kz_done, 2 * (it + 1))
                    wait_past(pe, sm_done, 4 * it + g - 1)
                    pe.matmul(banks[g % 2][:, :], qb[par][:, g // 2, :],
                              kz[par][:, HG * g:HG * (g + 1), :].rearrange("p h s -> p (h s)"), start=True, stop=True).then_inc(s_made, 1)

                def turn_p(it, g):
                    pe.wait_ge(exp_done, 16 * it + 4 * (g + 1))
                    wait_past(pe, pT_out, 4 * it + max(g - 1, 0))
                    for h in range(HG):
                        t = pe.transpose(banks[2 + g % 2][:, P * h:P * (h + 1)], probs[g % 2][:, h, :], k.ident[:, :])
                    t.then_inc(pT_made, 1)

                def mix(it, par, g):
                    if g == 0:
                        pe.wait_ge(vz_done, it + 1)
                        wait_past(pe, o_out, it)
                    pe.wait_ge(pT_out, 4 * it + g + 1)
                    c = g // 2
                    for h in range(HG):
                        j = HG * (g % 2) + h
                        t = pe.matmul(banks[4][:, P * c:P * (c + 1)], pT[g % 2][:, h, :], vz[par][:, c, P * j:P * (j + 1)],
                                      start=(j == 0), stop=(j == HPB - 1))
                    t.then_inc(o_made, 1)

                pe.wait_ge(qT_out, 4)
                scores(0, 0, 0)
                pe.wait_ge(qT_out, 4)
                scores(0, 0, 1)

                def step(it, par, last):
                    for g in range(4):
                        if g >= 2 and not last:
                            scores(it + 1, 1 - par, g - 2)
                        turn_p(it, g)
                        mix(it, par, g)
                        if g < 2:
                            scores(it, par, g + 2)

                sequences(pe, step)
                pe.wait_ge(yq_done, 2)
                for c in range(CB):
                    for b in range(B):
                        t = pe.transpose(half(2 + c)[:, P * b:P * (b + 1)], yq[:, b, P * c:P * (c + 1)], identb[:, :])
                    t.then_inc(turned, 1)
                pe.wait_ge(yqT_out, 2 * CB)
                for b in range(B):
                    for c in range(CB):
                        t = pe.matmul(banks[4 + b // 2][:, C * (b % 2):C * (b % 2 + 1)], yqT[:, c, P * b:P * (b + 1)],
                                      w_qT[:, 1, c, :], start=(c == 0), stop=(c == CB - 1))
                    t.then_inc(r_made, 1)

            @block.gpsimd
            def _(pool):
                pool.memset(ones[:, :], 1.0).then_inc(ones_set, 1)
                for i in range(2):
                    pool.memset(vz[i][:, :, :], 0.0).then_inc(vz_set, 1)
                pool.wait_ge(consts_in, 48)

                def heads(f, par):
                    wait_past(pool, s_made, 4 * (f - 1))
                    for c in range(CB):
                        pool.tensor_tensor(kz[par][:, HPB * c:HPB * (c + 1), :],
                                           k.keys1[:, c:c + 1, bass.ds(f * P, P)].to_broadcast([P, HPB, P]),
                                           head_mask[:, :].unsqueeze(2).to_broadcast([P, HPB, P]), ALU.mult).then_inc(kz_done, 1)

                heads(0, 0)

                def step(it, par, last):
                    if not last:
                        heads(it + 1, 1 - par)

                sequences(pool, step)

            @block.vector
            def _(dve):
                for b in range(B):
                    dve.bn_stats(stats[:, b, :], k.x1[:, b, :]).then_inc(stats_done, 1)
                for b in range(B):
                    dve.wait_ge(stats_done, b + 1)
                    dve.bn_aggr(mv[:, b, :], stats[:, b, :]).then_inc(var_done, 1)
                dve.wait_ge(w_in, 32)
                flat_w = w[:, :, :, :].rearrange("p i o c -> p (i o) c")
                dve.tensor_reduce(w_top[:, :], flat_w, AX.X, ALU.max, apply_absolute_value=True).then_inc(w_step_done, 1)
                dve.wait_ge(w_step_done, 1)
                dve.tensor_scalar(w_step[:, :], w_top[:, :], 1.0 / QMAX, QEPS, ALU.mult, ALU.max).then_inc(w_step_done, 1)
                dve.wait_ge(w_step_done, 2)
                dve.reciprocal(w_inv[:, :], w_step[:, :]).then_inc(w_step_done, 1)
                dve.wait_ge(w_step_done, 3)
                for n in range(2 * CB):
                    dve.tensor_scalar(flat_w[:, n, :], flat_w[:, n, :], w_inv[:, n:n + 1], QMAX, ALU.mult, ALU.min).then_inc(w_step_done, 1)
                dve.wait_ge(w_step_done, 3 + 2 * CB)
                dve.tensor_scalar(flat_w, flat_w, -QMAX, MAGIC, ALU.max, ALU.add).then_inc(w_step_done, 1)
                dve.wait_ge(w_step_done, 4 + 2 * CB)
                dve.tensor_scalar(w_q[:, :, :, :].rearrange("p i o c -> p (i o) c"), flat_w, MAGIC, None, ALU.subtract).then_inc(w_q_done, 1)
                for n in range(2 * CB):
                    dve.tensor_scalar(w_diag[:, n, :], k.ident[:, :], w_step[:, n:n + 1], None, ALU.mult).then_inc(w_diag_done, 1)
                for h in range(2):
                    dve.wait_ge(sd_done, h + 1)
                    dve.reciprocal(rstd[:, HB * h:HB * (h + 1)], sd[:, HB * h:HB * (h + 1)]).then_inc(rstd_done, 1)
                for h in range(2):
                    dve.wait_ge(rstd_done, h + 1)
                    for b in range(HB * h, HB * (h + 1)):
                        dve.tensor_scalar(y[:, b, :], k.x1[:, b, :], mv[:, b, 0:1], rstd[:, b:b + 1],
                                          ALU.subtract, ALU.mult).then_inc(y_done, 1)
                dve.wait_ge(y_done, B)
                row_steps(dve, y, 0)
                quantise(dve, y, yq, 0)
                dve.wait_ge(row_out, 1)
                dve.wait_ge(consts_in, 48)
                dve.wait_ge(yq_done, 1)
                for b in range(B):
                    dve.wait_ge(q_made, b - b % 2 + 2)
                    acc = banks[4 + b // 2][:, C * (b % 2):C * (b % 2 + 1)]
                    dve.scalar_tensor_tensor(y[:, b, :], acc, step_x[:, 0, b:b + 1], step_row[:, 0, :], ALU.mult, ALU.mult).then_inc(q_scaled, 1)
                    dve.wait_ge(q_scaled, b + 1)
                    dve.tensor_tensor(y[:, b, :], y[:, b, :], bias_row[:, 0, :], ALU.add).then_inc(q_done, 1)
                dve.wait_ge(mask_in, 16)

                def add_mask(it, g):
                    dve.wait_ge(s_made, 4 * it + g + 1)
                    wait_past(dve, exp_done, 16 * it + 4 * (g - 1))
                    dve.scalar_tensor_tensor(sm[g % 2][:, :, :], banks[g % 2][:, :].rearrange("p (h s) -> p h s", h=HG), HD1 ** -0.5,
                                             mask[:, bass.ds(it, 1), :].to_broadcast([P, HG, P]), ALU.mult, ALU.add).then_inc(sm_done, 1)
                    dve.wait_ge(sm_done, 4 * it + g + 1)
                    dve.tensor_reduce(negmax[:, HG * g:HG * (g + 1)], sm[g % 2][:, :, :], AX.X, ALU.max, negate=True).then_inc(max_done, 1)

                def pT_copy(it, g):
                    dve.wait_ge(pT_made, 4 * it + g + 1)
                    wait_past(dve, o_made, 4 * it + max(g - 1, 0))
                    dve.tensor_copy(pT[g % 2][:, :, :], banks[2 + g % 2][:, :].rearrange("p (h s) -> p h s", h=HG)).then_inc(pT_out, 1)

                def row_sums(it):
                    dve.wait_ge(exp_done, 16 * (it + 1))
                    dve.reciprocal(rinv[:, :], rsum[:, :]).then_inc(rinv_done, 1)

                def normalise(it):
                    dve.wait_ge(rinv_done, it + 1)
                    dve.wait_ge(o_made, 4 * (it + 1))
                    dve.tensor_tensor(y[:, bass.ds(it, 1), :].rearrange("p o (h d) -> p (o h) d", d=HD1),
                                      banks[4][:, 0:C].rearrange("p (h d) -> p h d", d=HD1),
                                      rinv[:, :].unsqueeze(2).to_broadcast([P, H1, HD1]), ALU.mult).then_inc(o_out, 1)

                dve.wait_ge(qT_made, 4)
                add_mask(0, 0)
                add_mask(0, 1)

                def step(it, par, last):
                    pT_copy(it, 0)
                    add_mask(it, 2)
                    pT_copy(it, 1)
                    add_mask(it, 3)
                    row_sums(it)
                    if not last:
                        add_mask(it + 1, 0)
                    pT_copy(it, 2)
                    if not last:
                        add_mask(it + 1, 1)
                    pT_copy(it, 3)
                    normalise(it)

                sequences(dve, step)
                dve.wait_ge(o_out, B)
                row_steps(dve, y, 1)
                quantise(dve, y, yq, 1)
                for b in range(B):
                    dve.wait_ge(r_made, b - b % 2 + 2)
                    acc = banks[4 + b // 2][:, C * (b % 2):C * (b % 2 + 1)]
                    dve.scalar_tensor_tensor(y[:, b, :], acc, step_x[:, 1, b:b + 1], step_row[:, 1, :], ALU.mult, ALU.mult).then_inc(r_step, 1)
                    dve.tensor_tensor(k.x1[:, b, :], k.x1[:, b, :], bias_row[:, 1, :], ALU.add).then_inc(r_step, 1)
                    dve.wait_ge(r_step, 2 * (b + 1))
                    dve.tensor_tensor(k.x1[:, b, :], k.x1[:, b, :], y[:, b, :], ALU.add).then_inc(x3_done, 1)
E1, I1, K1 = 32, 96, 8
TAU = 0.05
FEW = 1e-12


def experts1_stage(nc, k, io):
    with Memory(nc) as m:
        stats, mv = m.sb("e_stats", [P, B, 6]), m.sb("e_mean_var", [P, B, 2])
        sd, rstd = m.sb("e_sd", [P, B]), m.sb("e_rstd", [P, B])
        y, yT = m.sb("e_y", [P, B, C]), m.sb("e_yT", [P, CB, T])
        gate_w = m.sb("e_gate_w", [P, CB, E1])
        iota = m.sb("e_iota", [P, E1])
        alpha = m.sb("alpha", [P, 1])
        probs = m.sb("e_probs", [P, B, E1])
        row = {n: m.sb("e_row_" + n, [P, B]) for n in ("max", "sum", "inv", "topsum", "topinv", "best", "idle", "first", "wsum", "winv")}
        top, top_i, top_f = m.sb("e_top", [P, B, K1]), m.sb("e_top_i", [P, B, K1], u32), m.sb("e_top_f", [P, B, K1])
        scaled, active, is_best = m.sb("scaled", [P, B, K1]), m.sb("active", [P, B, K1]), m.sb("is_best", [P, B, K1])
        where, fallback = m.sb("where", [P, B, K1]), m.sb("fallback", [P, B, K1])
        weight = m.sb("weight", [P, B, K1])
        spread = m.sb("spread", [P, B, E1, K1])
        combine = m.sb("combine", [P, B, E1])
        wgu = [m.sb(f"wgu{i}", [P, CB, 2 * I1]) for i in range(2)]
        wd = [m.sb(f"wd{i}", [I1, C]) for i in range(2)]
        silu = [m.sb(f"e_silu{i}", [I1, 512]) for i in range(2)]
        hid = [m.sb(f"e_hid{i}", [I1, T]) for i in range(2)]
        gu_ps = [m.ps(f"e_gu{i}", [P, 512]) for i in range(4)]
        y_ps = [m.ps(f"e_y{i}", [P, 2, C]) for i in range(4)]

        s = lambda name: m.sem("e_" + name)
        consts_in, gate_in = s("consts_in"), s("gate_in")
        stats_done, var_done, sd_done, rstd_done, y_done = s("stats"), s("var"), s("sd"), s("rstd"), s("y")
        turned, yT_out, logits_made, route, exp_done = s("turned"), s("yT_out"), s("logits"), s("route"), s("exp")
        wgu_in, wd_in = [s(f"wgu_in{i}") for i in range(2)], [s(f"wd_in{i}") for i in range(2)]
        gu_made, silu_done, hid_done, y_made, added = s("gu_made"), s("silu"), s("hid"), s("y_made"), s("added")
        out_done = s("out_done")

        def experts(eng, step):
            step(0, 0)
            step(1, 1)
            with eng.Fori(1, E1 // 2) as i:
                step(2 * i, 0)
                step(2 * i + 1, 1)

        with nc.Block() as block:

            @block.sync
            def _(sp):
                sp.dma_start(gate_w[:, :, :], io["gate_w1"].rearrange("(cb p) e -> p cb e", p=P)).then_inc(gate_in, 16)
                sp.dma_start(iota[:, :], io["iota"]).then_inc(consts_in, 16)
                sp.dma_start(alpha[:, :], io["alpha"]).then_inc(consts_in, 16)

                def load(e, par):
                    wait_past(sp, gu_made, 4 * (e - 1))
                    sp.dma_start(wgu[par][:, :, :], io["wgu"][bass.ds(e, 1), :, :].rearrange("o (cb p) i -> (o p) cb i", p=P)).then_inc(wgu_in[par], 16)
                    wait_past(sp, y_made, 4 * (e - 1))
                    sp.dma_start(wd[par][:, :], io["wd"][bass.ds(e, 1), :, :].rearrange("o i c -> (o i) c")).then_inc(wd_in[par], 16)

                experts(sp, load)
                sp.wait_ge(added, B * E1)
                sp.dma_start(io["out"].rearrange("b s c -> s b c"), k.x1[:, :, :]).then_inc(out_done, 16)
                sp.wait_ge(out_done, 16)

            @block.scalar
            def _(act):
                for h in range(2):
                    act.wait_ge(var_done, HB * (h + 1))
                    act.activation(sd[:, HB * h:HB * (h + 1)], mv[:, HB * h:HB * (h + 1), 1], ACT.Sqrt,
                                   bias=k.eps[:, 0:1]).then_inc(sd_done, 1)
                for h in range(2):
                    for c in range(CB):
                        n = CB * h + c
                        act.wait_ge(turned, n + 1)
                        act.activation(yT[:, c, 512 * h:512 * (h + 1)], gu_ps[n][:, :], ACT.Copy).then_inc(yT_out, 1)
                act.wait_ge(route, 2)
                act.activation(probs[:, :, :], probs[:, :, :], ACT.Exp).then_inc(exp_done, 1)

                def work(e, par):
                    for h in range(2):
                        act.wait_ge(gu_made, 4 * e + 2 * h + 1)
                        wait_past(act, hid_done, 2 * e + h - 1)
                        act.activation(silu[h][:, :], gu_ps[2 * h][0:I1, :], ACT.Silu).then_inc(silu_done, 1)

                experts(act, work)

            @block.tensor
            def _(pe):
                for h in range(2):
                    pe.wait_ge(y_done, HB * (h + 1))
                    for c in range(CB):
                        for b in range(HB):
                            t = pe.transpose(gu_ps[CB * h + c][:, P * b:P * (b + 1)], y[:, HB * h + b, P * c:P * (c + 1)], k.ident[:, :])
                        t.then_inc(turned, 1)
                pe.wait_ge(gate_in, 16)
                pe.wait_ge(yT_out, 2 * CB)
                for b in range(B):
                    for c in range(CB):
                        t = pe.matmul(y_ps[3][:, 0, E1 * b:E1 * (b + 1)], yT[:, c, P * b:P * (b + 1)], gate_w[:, c, :],
                                      start=(c == 0), stop=(c == CB - 1))
                t.then_inc(logits_made, 1)

                def up(e, par):
                    pe.wait_ge(wgu_in[par], 16 * earlier(e, par) + 16)
                    for h in range(2):
                        for n in range(2):
                            wait_past(pe, hid_done if n else silu_done, 2 * e + h - 1)
                            for c in range(CB):
                                t = pe.matmul(gu_ps[2 * h + n][0:I1, :], wgu[par][:, c, I1 * n:I1 * (n + 1)],
                                              yT[:, c, 512 * h:512 * (h + 1)], start=(c == 0), stop=(c == CB - 1))
                            t.then_inc(gu_made, 1)

                def down(e, par):
                    pe.wait_ge(wd_in[par], 16 * earlier(e, par) + 16)
                    for j in range(4):
                        pe.wait_ge(hid_done, 2 * e + j // 2 + 1)
                        if not (isinstance(e, int) and e == 0):
                            pe.wait_ge(added, B * (e - 1) + 2 * (j + 1))
                        elif j == 3:
                            pe.wait_ge(route, 1)
                        for r in range(2):
                            t = pe.matmul(y_ps[j][:, r, :], hid[par][:, P * (2 * j + r):P * (2 * j + r + 1)], wd[par][:, :],
                                          start=True, stop=True)
                        t.then_inc(y_made, 1)

                up(0, 0)
                up(1, 1)
                down(0, 0)
                with pe.Fori(1, E1 // 2) as i:
                    up(2 * i, 0)
                    down(2 * i - 1, 1)
                    up(2 * i + 1, 1)
                    down(2 * i, 0)
                down(E1 - 1, 1)

            @block.vector
            def _(dve):
                for b in range(B):
                    dve.bn_stats(stats[:, b, :], k.x1[:, b, :]).then_inc(stats_done, 1)
                for b in range(B):
                    dve.wait_ge(stats_done, b + 1)
                    dve.bn_aggr(mv[:, b, :], stats[:, b, :]).then_inc(var_done, 1)
                for h in range(2):
                    dve.wait_ge(sd_done, h + 1)
                    dve.reciprocal(rstd[:, HB * h:HB * (h + 1)], sd[:, HB * h:HB * (h + 1)]).then_inc(rstd_done, 1)
                    dve.wait_ge(rstd_done, h + 1)
                    for b in range(HB * h, HB * (h + 1)):
                        dve.tensor_scalar(y[:, b, :], k.x1[:, b, :], mv[:, b, 0:1], rstd[:, b:b + 1],
                                          ALU.subtract, ALU.mult).then_inc(y_done, 1)

                count = [0]

                def then(t):
                    t.then_inc(route, 1)
                    count[0] += 1
                    dve.wait_ge(route, count[0])

                wide = lambda a, n: a[:, :].unsqueeze(2).to_broadcast([P, B, n])
                dve.wait_ge(logits_made, 1)
                logits = y_ps[3][:, 0, :].rearrange("p (b e) -> p b e", b=B)
                dve.tensor_reduce(row["max"][:, :], logits, AX.X, ALU.max).then_inc(y_done, 1)
                dve.wait_ge(y_done, B + 1)
                then(dve.tensor_tensor(probs[:, :, :], logits, wide(row["max"], E1), ALU.subtract))
                dve.wait_ge(consts_in, 32)
                then(dve.tensor_copy(row["first"][:, :], row["max"][:, :]))
                dve.wait_ge(exp_done, 1)
                then(dve.tensor_reduce(row["sum"][:, :], probs[:, :, :], AX.X, ALU.add))
                then(dve.reciprocal(row["inv"][:, :], row["sum"][:, :]))
                then(dve.tensor_tensor(probs[:, :, :], probs[:, :, :], wide(row["inv"], E1), ALU.mult))
                for b in range(B):
                    t = dve.max(top[:, b, :], probs[:, b, :])
                then(t)
                for b in range(B):
                    t = dve.max_index(top_i[:, b, :], top[:, b, :], probs[:, b, :])
                then(t)
                then(dve.tensor_copy(top_f[:, :, :], top_i[:, :, :]))
                then(dve.tensor_reduce(row["topsum"][:, :], top[:, :, :], AX.X, ALU.add))
                then(dve.tensor_scalar(row["topsum"][:, :], row["topsum"][:, :], FEW, None, ALU.max))
                then(dve.reciprocal(row["topinv"][:, :], row["topsum"][:, :]))
                then(dve.tensor_tensor(top[:, :, :], top[:, :, :], wide(row["topinv"], K1), ALU.mult))
                then(dve.tensor_scalar(scaled[:, :, :], top[:, :, :], alpha[:, 0:1], None, ALU.mult))
                then(dve.tensor_scalar(active[:, :, :], scaled[:, :, :], TAU, None, ALU.is_ge))
                then(dve.tensor_reduce(row["best"][:, :], scaled[:, :, :], AX.X, ALU.max))
                then(dve.tensor_tensor(is_best[:, :, :], scaled[:, :, :], wide(row["best"], K1), ALU.is_equal))
                then(dve.scalar_tensor_tensor(where[:, :, :], is_best[:, :, :], -100.0,
                                              iota[:, 0:K1].unsqueeze(1).to_broadcast([P, B, K1]), ALU.mult, ALU.add))
                then(dve.tensor_reduce(row["first"][:, :], where[:, :, :], AX.X, ALU.min))
                then(dve.tensor_tensor(fallback[:, :, :], where[:, :, :], wide(row["first"], K1), ALU.is_equal))
                then(dve.tensor_reduce(row["idle"][:, :], active[:, :, :], AX.X, ALU.max))
                then(dve.tensor_scalar(row["idle"][:, :], row["idle"][:, :], -1.0, 1.0, ALU.mult, ALU.add))
                then(dve.tensor_tensor(fallback[:, :, :], fallback[:, :, :], wide(row["idle"], K1), ALU.mult))
                then(dve.tensor_tensor(active[:, :, :], active[:, :, :], fallback[:, :, :], ALU.max))
                then(dve.tensor_tensor(weight[:, :, :], top[:, :, :], active[:, :, :], ALU.mult))
                then(dve.tensor_reduce(row["wsum"][:, :], weight[:, :, :], AX.X, ALU.add))
                then(dve.tensor_scalar(row["wsum"][:, :], row["wsum"][:, :], FEW, None, ALU.max))
                then(dve.reciprocal(row["winv"][:, :], row["wsum"][:, :]))
                then(dve.tensor_tensor(weight[:, :, :], weight[:, :, :], wide(row["winv"], K1), ALU.mult))
                for b in range(B):
                    t = dve.tensor_tensor(spread[:, b, :, :], iota[:, :].unsqueeze(2).to_broadcast([P, E1, K1]),
                                          top_f[:, b:b + 1, :].to_broadcast([P, E1, K1]), ALU.is_equal)
                then(t)
                for b in range(B):
                    t = dve.tensor_tensor(spread[:, b, :, :], spread[:, b, :, :], weight[:, b:b + 1, :].to_broadcast([P, E1, K1]), ALU.mult)
                then(t)
                then(dve.tensor_reduce(combine[:, :, :].rearrange("p b e -> p (b e)"),
                                       spread[:, :, :, :].rearrange("p b e k -> p (b e) k"), AX.X, ALU.add))

                def gate(e, par):
                    for h in range(2):
                        dve.wait_ge(silu_done, 2 * e + h + 1)
                        dve.wait_ge(gu_made, 4 * e + 2 * h + 2)
                        wait_past(dve, y_made, 4 * (e - 1))
                        dve.tensor_tensor(hid[par][:, 512 * h:512 * (h + 1)], gu_ps[2 * h + 1][0:I1, :], silu[h][:, :], ALU.mult)\
                            .then_inc(hid_done, 1)

                def add(e, par):
                    for b in range(B):
                        dve.wait_ge(y_made, 4 * e + b // 2 + 1)
                        if not (isinstance(e, int) and e == 0):
                            dve.wait_ge(added, B * (e - 1) + b + 1)
                        dve.scalar_tensor_tensor(k.x1[:, b, :], y_ps[b // 2][:, b % 2, :], combine[:, b, bass.ds(e, 1)], k.x1[:, b, :],
                                                 ALU.mult, ALU.add).then_inc(added, 1)

                gate(0, 0)
                gate(1, 1)
                add(0, 0)
                with dve.Fori(1, E1 // 2) as i:
                    gate(2 * i, 0)
                    add(2 * i - 1, 1)
                    gate(2 * i + 1, 1)
                    add(2 * i, 0)
                add(E1 - 1, 1)
class Kept:

    def __init__(self, m):
        self.x1 = m.sb("x1", [P, B, C])
        self.z = m.sb("z", [P, B, C])
        self.xa = m.sb("xa", [P, B, C])
        self.keys1 = m.sb("keys1", [P, CB, T])
        self.vals1 = m.sb("vals1", [P, B, C])
        self.ident = m.sb("ident", [P, P])
        self.eps = m.sb("eps", [P, 1])


def build_program(nc, io):
    with Memory(nc) as m:
        kept = Kept(m)
        wkv_stage(nc, kept, io)
        attention_stage(nc, kept, io)
        experts0_stage(nc, kept, io)
        cross_stage(nc, kept, io)
        experts1_stage(nc, kept, io)


def rope_tables(np):
    f = np.float32
    freq = (f(1e6) ** (-np.arange(0, HD0, 2, dtype=f) / f(HD0))).astype(f)
    angle = np.arange(P, dtype=f)[:, None] * freq[None]
    cos, sin = np.cos(angle), np.sin(angle)
    cos, sin = np.concatenate([cos, cos], 1), np.concatenate([-sin, sin], 1)
    scale = f(HD0 ** -0.5)
    return np.stack([cos * scale, sin * scale, cos, sin], 1).astype(f)


def kernel(**inputs):
    import ml_dtypes
    import numpy as np
    import concourse.bacc as bacc
    from concourse.bass_utils import run_bass_kernel_spmd

    a = {n: np.asarray(v) for n, v in inputs.items()}
    half = ml_dtypes.bfloat16
    column = lambda v: v.reshape(CB, P).T
    rows = lambda v: np.broadcast_to(v, (P,) + v.shape)
    pairs_apart = lambda w, h: w.reshape(C, h, HD0 // 2, 2).transpose(0, 1, 3, 2).reshape(C, h * HD0)
    visible = np.tril(np.ones((P, P), bool))
    arrays = dict(
        x=a["x"], ctxT=a["ctx_2048"].transpose(2, 0, 1),
        wkv_cols=np.stack([column(a[n]) for n in ("L0_xattn_w", "L0_xattn_u", "L1_xattn_bk")], 1),
        wk1T=a["L1_xattn_wk"].T, wv1T=a["L1_xattn_wv"].T, bv1=rows(a["L1_xattn_bv"]),
        ln_w=column(a["L0_ffn_ln_w"]),
        wq0=pairs_apart(a["L0_ffn_wq"], H0), wk0=pairs_apart(a["L0_ffn_wk"], KV0), wv0=a["L0_ffn_wv"], wo0=a["L0_ffn_wo"],
        ff_w=rows(a["L0_ffn_ff_ln_w"]), gate_w0=a["L0_ffn_gate_w"], w1=a["L0_ffn_w1"], w3=a["L0_ffn_w3"], w2=a["L0_ffn_w2"],
        wq1=a["L1_xattn_wq"], wo1=a["L1_xattn_wo"], bias_row=rows(np.stack([a["L1_xattn_bq"], a["L1_xattn_bo"]])),
        mask=a["mask_BxSxS2_ff0"],
        gate_w1=a["L1_ffn_gate_weight"].T, alpha=rows(a["L1_ffn_layer_alpha"].reshape(1)),
        wgu=a["L1_ffn_gate_up_proj"].transpose(0, 2, 1), wd=a["L1_ffn_down_proj"].transpose(0, 2, 1),
        ident=np.eye(P, dtype=np.float32), identb=np.eye(P).astype(half), rope=rope_tables(np),
        causal=np.broadcast_to(np.where(visible, 0, -1e30).astype(half)[:, None], (P, G0, P)),
        iota=rows(np.arange(E1, dtype=np.float32)), before=(~visible).astype(half), ones=np.ones((P, P), half),
        head_mask=(np.arange(P)[:, None] // HD1 == np.arange(HPB)[None]).astype(np.float32),
    )
    nc = bacc.Bacc("TRN2", target_bir_lowering=False, num_devices=1)
    feed, io = {}, {}
    for name, value in arrays.items():
        value = np.ascontiguousarray(value)
        feed[f"in_{name}"] = value
        io[name] = nc.dram_tensor(f"in_{name}", value.shape, mybir.dt.from_np(value.dtype), kind="ExternalInput").ap()
    io["out"] = nc.dram_tensor("out_x", (B, P, C), fp32, kind="ExternalOutput").ap()
    build_program(nc, io)
    result = run_bass_kernel_spmd(nc, [feed], core_ids=[0])
    return result.results[0]["out_x"]
```

```python
from contextlib import ExitStack

import concourse.bass as bass
from concourse import mybir
from concourse.alu_op_type import AluOpType as ALU

fp32 = mybir.dt.float32
bf16 = mybir.dt.bfloat16
u32 = mybir.dt.uint32
ACT = mybir.ActivationFunctionType
AX = mybir.AxisListType

P = 128
B = 8
C = 256
CB = C // P
T = B * P
HB = B // 2
PAD = P + 1
NEG = -1e38
LN_EPS = 1e-5


class Memory:

    def __init__(self, nc):
        self.nc, self.stack, self.sems = nc, ExitStack(), []

    def __enter__(self):
        self.stack.__enter__()
        return self

    def __exit__(self, *a):
        if a[0] is None and self.sems:
            runs = []
            for n in sorted(s.num for s in self.sems):
                if runs and runs[-1][1] == n:
                    runs[-1][1] = n + 1
                else:
                    runs.append([n, n + 1])
            with self.nc.Block() as block:

                @block.gpsimd
                def _(pool):
                    for first, end in runs:
                        pool.sem_clear(range(first, end))

        return self.stack.__exit__(*a)

    def sb(self, name, shape, dt=fp32):
        return self.stack.enter_context(self.nc.sbuf_tensor(name, shape, dt))

    def ps(self, name, shape, dt=fp32):
        return self.stack.enter_context(self.nc.psum_tensor(name, shape, dt))

    def sem(self, name):
        self.sems.append(self.stack.enter_context(self.nc.semaphore(name)))
        return self.sems[-1]


def wait_past(eng, sem, n):
    if not isinstance(n, int) or n > 0:
        eng.wait_ge(sem, n)


def wkv_stage(nc, k, io):
    with Memory(nc) as m:
        ctxT = m.sb("ctxT", [P, CB, B, P])
        xn = m.sb("xn", [P, B, C])
        stats = m.sb("ln_stats", [P, B, 6])
        mv = m.sb("ln_mean_var", [P, B, 2])
        sd = m.sb("ln_sd", [P, B])
        rstd = m.sb("ln_rstd", [P, B])
        eps = k.eps
        wk1T = m.sb("wk1T", [P, CB, C])
        wv1T = m.sb("wv1T", [P, CB, C])
        bv1 = m.sb("bv1", [P, C])
        wkv_cols = m.sb("wkv_cols", [P, 3, CB])
        pad = lambda name: [m.sb(f"{name}{c}", [P, B, PAD]) for c in range(CB)]
        flat = lambda name: [m.sb(f"{name}{c}", [P, B, P]) for c in range(CB)]
        decay, kpad, omax = pad("decay"), pad("kpad"), pad("omax")
        qsum, psum = pad("qsum"), pad("psum_")
        a2, e2, ev2 = pad("a2_"), pad("e2_"), pad("ev2_")
        d2_, d1, a1, e1, ev1 = flat("d2_"), flat("d1_"), flat("a1_"), flat("e1_"), flat("ev1_")
        kT_ps = m.ps("kT_ps", [P, CB, T])
        y_ps = m.ps("y_ps", [P, B, C])
        y_half = y_ps[:, :, :]

        x_in = [m.sem(f"x_in{h}") for h in range(2)]
        ctx_in, const_in, cols_in, w1_in = m.sem("ctx_in"), m.sem("const_in"), m.sem("cols_in"), m.sem("w1_in")
        eps_set, pads_set = m.sem("eps_set"), m.sem("pads_set")
        stats_done, var_done, sd_done, rstd_done = m.sem("stats_done"), m.sem("var_done"), m.sem("sd_done"), m.sem("rstd_done")
        xn_done, kT_done, kpad_done = m.sem("xn_done"), m.sem("kT_done"), m.sem("kpad_done")
        decay_done, omax_done, d2_done, d1_done = m.sem("decay_done"), m.sem("omax_done"), m.sem("d2_done"), m.sem("d1_done")
        relu_done, exp2_done, exp1_done = m.sem("relu_done"), m.sem("exp2_done"), m.sem("exp1_done")
        ev2_done, ev1_done, ap_done, aq_done = m.sem("ev2_done"), m.sem("ev1_done"), m.sem("ap_done"), m.sem("aq_done")
        qscan_done, pscan_done = m.sem("qscan_done"), m.sem("pscan_done")
        den_done, num_done, rden_done, yT_done = m.sem("den_done"), m.sem("num_done"), m.sem("rden_done"), m.sem("yT_done")
        y_done, x1_done = m.sem("y_done"), m.sem("x1_done")
        keys_done, keys_out, vals_done, vals_raw, vals_out = m.sem("keys_done"), m.sem("keys_out"), m.sem("vals_done"), m.sem("vals_raw"), m.sem("vals_out")

        with nc.Block() as block:

            @block.sync
            def _(sp):
                for h in range(2):
                    sp.dma_start(k.x1[:, HB * h:HB * (h + 1), :],
                                 io["x"][HB * h:HB * (h + 1)].rearrange("b s c -> s b c")).then_inc(x_in[h], 16)
                sp.dma_start(k.ident[:, :], io["ident"]).then_inc(const_in, 16)
                sp.dma_start(ctxT[:, :, :, :], io["ctxT"].rearrange("(cb p) b s -> p cb b s", p=P)).then_inc(ctx_in, 16)

            @block.scalar
            def _(act):
                act.dma_start(wkv_cols[:, :, :], io["wkv_cols"]).then_inc(cols_in, 16)
                act.dma_start(wk1T[:, :, :], io["wk1T"].rearrange("(cb p) o -> p cb o", p=P)).then_inc(w1_in, 16)
                act.dma_start(wv1T[:, :, :], io["wv1T"].rearrange("(cb p) o -> p cb o", p=P)).then_inc(w1_in, 16)
                act.dma_start(bv1[:, :], io["bv1"]).then_inc(w1_in, 16)
                act.wait_ge(eps_set, 1)
                for h in range(2):
                    act.wait_ge(var_done, HB * (h + 1))
                    act.activation(sd[:, HB * h:HB * (h + 1)], mv[:, HB * h:HB * (h + 1), 1], ACT.Sqrt,
                                   bias=eps[:, 0:1]).then_inc(sd_done, 1)
                for c in range(CB):
                    for h in range(2):
                        act.wait_ge(kT_done, 2 * c + h + 1)
                        act.activation(kpad[c][:, HB * h:HB * (h + 1), 1:PAD],
                                       kT_ps[:, c, 512 * h:512 * (h + 1)].rearrange("p (b s) -> p b s", s=P),
                                       ACT.Copy).then_inc(kpad_done, 1)
                for c in range(CB):
                    act.wait_ge(pads_set, 3 * (c + 1))
                    act.wait_ge(d2_done, c + 1)
                    d2 = d2_[c]
                    act.activation(a2[c][:, :, 1:PAD], d2[:, :, :], ACT.Relu, scale=-1.0).then_inc(relu_done, 1)
                    act.activation(e2[c][:, :, 1:PAD], d2[:, :, :], ACT.Relu).then_inc(relu_done, 1)
                    act.wait_ge(d1_done, c + 1)
                    act.activation(a1[c][:, :, :], d1[c][:, :, :], ACT.Relu, scale=-1.0).then_inc(relu_done, 1)
                    act.activation(e1[c][:, :, :], d1[c][:, :, :], ACT.Relu).then_inc(relu_done, 1)
                    act.wait_ge(relu_done, 4 * c + 4)
                    for buf, span in ((e2[c], slice(1, PAD)), (a2[c], slice(1, PAD)), ):
                        act.activation(buf[:, :, span], buf[:, :, span], ACT.Exp, scale=-1.0).then_inc(exp2_done, 1)
                    for buf in (e1[c], a1[c]):
                        act.activation(buf[:, :, :], buf[:, :, :], ACT.Exp, scale=-1.0).then_inc(exp1_done, 1)
                act.wait_ge(cols_in, 16)
                for ob in range(CB):
                    for h in range(2):
                        act.wait_ge(keys_done, 2 * ob + h + 1)
                        act.activation(k.keys1[:, ob, 512 * h:512 * (h + 1)], kT_ps[:, ob, 512 * h:512 * (h + 1)],
                                       ACT.Identity, bias=wkv_cols[:, 2, ob:ob + 1]).then_inc(keys_out, 1)
                for j in range(4):
                    act.wait_ge(vals_done, j + 1)
                    act.activation(k.vals1[:, 2 * j:2 * j + 2, :], y_ps[:, 2 * j:2 * j + 2, :], ACT.Copy).then_inc(vals_raw, 1)

            @block.tensor
            def _(pe):
                pe.wait_ge(const_in, 16)
                for c in range(CB):
                    for h in range(2):
                        for b in range(HB * h, HB * (h + 1)):
                            pe.wait_ge(xn_done, b + 1)
                            t = pe.transpose(kT_ps[:, c, P * b:P * (b + 1)], xn[:, b, P * c:P * (c + 1)], k.ident[:, :])
                        t.then_inc(kT_done, 1)
                pe.wait_ge(ctx_in, 16)
                pe.wait_ge(w1_in, 48)
                for b in range(B):
                    for c in range(CB):
                        t = pe.matmul(y_ps[:, b, :], ctxT[:, c, b, :], wv1T[:, c, :], start=(c == 0), stop=(c == CB - 1))
                    if b % 2:
                        t.then_inc(vals_done, 1)
                pe.wait_ge(kpad_done, 2 * CB)
                for ob in range(CB):
                    for h in range(2):
                        for c in range(CB):
                            t = pe.matmul(kT_ps[:, ob, 512 * h:512 * (h + 1)], wk1T[:, c, P * ob:P * (ob + 1)],
                                          ctxT[:, c, HB * h:HB * (h + 1), :], start=(c == 0), stop=(c == CB - 1))
                        t.then_inc(keys_done, 1)
                pe.wait_ge(vals_raw, 4)
                for c in range(CB):
                    pe.wait_ge(yT_done, c + 1)
                    for b in range(B):
                        t = pe.transpose(y_ps[:, b, P * c:P * (c + 1)], a1[c][:, b, :], k.ident[:, :])
                        if c == CB - 1 and b % 2:
                            t.then_inc(y_done, 1)

            @block.gpsimd
            def _(pool):
                for c in range(CB):
                    for buf in (a2[c], e2[c], ev2[c]):
                        pool.memset(buf[:, :, 0:1], 0.0).then_inc(pads_set, 1)
                for c in range(CB):
                    pool.wait_ge(exp2_done, 2 * c + 1)
                    pool.wait_ge(ctx_in, 16)
                    pool.tensor_tensor(ev2[c][:, :, 1:PAD], e2[c][:, :, 1:PAD], ctxT[:, c, :, :], ALU.mult).then_inc(ev2_done, 1)
                    pool.wait_ge(exp1_done, 2 * c + 1)
                    pool.tensor_tensor(ev1[c][:, :, :], e1[c][:, :, :], ctxT[:, c, :, :], ALU.mult).then_inc(ev1_done, 1)
                    pool.wait_ge(exp1_done, 2 * c + 2)
                    pool.wait_ge(qscan_done, c + 1)
                    pool.tensor_tensor(qsum[c][:, :, 0:P], qsum[c][:, :, 0:P], a1[c][:, :, :], ALU.mult).then_inc(aq_done, 1)
                pool.wait_ge(w1_in, 48)
                for b in range(B):
                    pool.wait_ge(vals_raw, b // 2 + 1)
                    pool.tensor_tensor(k.vals1[:, b, :], k.vals1[:, b, :], bv1[:, :], ALU.add).then_inc(vals_out, 1)

            @block.vector
            def _(dve):
                dve.memset(eps[:, :], LN_EPS).then_inc(eps_set, 1)
                for h in range(2):
                    dve.wait_ge(x_in[h], 16)
                    for b in range(HB * h, HB * (h + 1)):
                        dve.bn_stats(stats[:, b, :], k.x1[:, b, :]).then_inc(stats_done, 1)
                    for b in range(HB * h, HB * (h + 1)):
                        dve.wait_ge(stats_done, b + 1)
                        dve.bn_aggr(mv[:, b, :], stats[:, b, :]).then_inc(var_done, 1)
                    if h == 0:
                        dve.wait_ge(cols_in, 16)
                        for c in range(CB):
                            dve.memset(decay[c][:, :, 1:PAD], 0.0).then_inc(decay_done, 1)
                            dve.memset(decay[c][:, :, 0:1], NEG).then_inc(decay_done, 1)
                            dve.memset(kpad[c][:, :, 0:1], NEG).then_inc(decay_done, 1)
                            dve.wait_ge(decay_done, 4 * c + 1)
                            dve.tensor_scalar(decay[c][:, :, 1:PAD], decay[c][:, :, 1:PAD], wkv_cols[:, 0, c:c + 1], None,
                                              ALU.add).then_inc(decay_done, 1)
                for h in range(2):
                    dve.wait_ge(sd_done, h + 1)
                    dve.reciprocal(rstd[:, HB * h:HB * (h + 1)], sd[:, HB * h:HB * (h + 1)]).then_inc(rstd_done, 1)
                    dve.wait_ge(rstd_done, h + 1)
                    for b in range(HB * h, HB * (h + 1)):
                        dve.tensor_scalar(xn[:, b, :], k.x1[:, b, :], mv[:, b, 0:1], rstd[:, b:b + 1],
                                          ALU.subtract, ALU.mult).then_inc(xn_done, 1)
                for c in range(CB):
                    dve.wait_ge(kpad_done, 2 * c + 2)
                    dve.wait_ge(decay_done, 4 * c + 4)
                    dve.tensor_tensor_scan(omax[c][:, :, :].rearrange("p b s -> p (b s)"),
                                           decay[c][:, :, :].rearrange("p b s -> p (b s)"),
                                           kpad[c][:, :, :].rearrange("p b s -> p (b s)"),
                                           NEG, ALU.add, ALU.max).then_inc(omax_done, 1)
                    dve.wait_ge(omax_done, c + 1)
                    dve.scalar_tensor_tensor(d2_[c][:, :, :], omax[c][:, :, 0:P], wkv_cols[:, 0, c:c + 1],
                                             kpad[c][:, :, 1:PAD], ALU.add, ALU.subtract).then_inc(d2_done, 1)
                    dve.scalar_tensor_tensor(d1[c][:, :, :], omax[c][:, :, 0:P], wkv_cols[:, 1, c:c + 1],
                                             kpad[c][:, :, 1:PAD], ALU.subtract, ALU.subtract).then_inc(d1_done, 1)
                for c in range(CB):
                    fl = lambda t: t[c][:, :, :].rearrange("p b s -> p (b s)")
                    dve.wait_ge(exp2_done, 2 * c + 2)
                    dve.wait_ge(pads_set, 3 * CB)
                    dve.tensor_tensor_scan(fl(qsum), fl(a2), fl(e2), 0.0, ALU.mult, ALU.add).then_inc(qscan_done, 1)
                    dve.wait_ge(ev2_done, c + 1)
                    dve.tensor_tensor_scan(fl(psum), fl(a2), fl(ev2), 0.0, ALU.mult, ALU.add).then_inc(pscan_done, 1)
                    dve.wait_ge(aq_done, c + 1)
                    dve.tensor_tensor(e1[c][:, :, :], qsum[c][:, :, 0:P], e1[c][:, :, :], ALU.add).then_inc(den_done, 1)
                    dve.wait_ge(pscan_done, c + 1)
                    dve.tensor_tensor(a1[c][:, :, :], psum[c][:, :, 0:P], a1[c][:, :, :], ALU.mult).then_inc(ap_done, 1)
                    dve.wait_ge(den_done, c + 1)
                    dve.reciprocal(e1[c][:, :, :], e1[c][:, :, :]).then_inc(rden_done, 1)
                    dve.wait_ge(ap_done, c + 1)
                    dve.wait_ge(ev1_done, c + 1)
                    dve.tensor_tensor(a1[c][:, :, :], a1[c][:, :, :], ev1[c][:, :, :], ALU.add).then_inc(num_done, 1)
                    dve.wait_ge(num_done, c + 1)
                    dve.wait_ge(rden_done, c + 1)
                    dve.tensor_tensor(a1[c][:, :, :], a1[c][:, :, :], e1[c][:, :, :], ALU.mult).then_inc(yT_done, 1)
                for j in range(4):
                    dve.wait_ge(y_done, j + 1)
                    dve.tensor_tensor(k.x1[:, 2 * j:2 * j + 2, :], k.x1[:, 2 * j:2 * j + 2, :], y_ps[:, 2 * j:2 * j + 2, :],
                                      ALU.add).then_inc(x1_done, 1)
H0, KV0, HD0 = 16, 4, 128
G0 = H0 // KV0


def attention_stage(nc, k, io):
    with Memory(nc) as m:
        stats, mv = m.sb("b_stats", [P, B, 6]), m.sb("b_mean_var", [P, B, 2])
        sd, rstd = m.sb("b_sd", [P, B]), m.sb("b_rstd", [P, B])
        ssq, rms, rrms = m.sb("b_ssq", [P, B]), m.sb("b_rms", [P, B]), m.sb("b_rrms", [P, B])
        square = m.sb("b_square", [P, C])
        wq, wk = m.sb("wq0", [P, CB, H0 * HD0]), m.sb("wk0", [P, CB, KV0 * HD0])
        wv, wo = m.sb("wv0", [P, CB, KV0 * HD0]), m.sb("wo0", [P, H0, C])
        ln_w = m.sb("ln_w", [P, CB])
        rope = m.sb("rope", [P, 4, HD0])
        causal = m.sb("causal", [P, G0, P], bf16)
        identb = m.sb("identb", [P, P], bf16)
        hn = m.sb("hn", [P, C])
        hT = m.sb("hT", [P, CB, P])
        by_cos = [m.sb(f"by_cos{i}", [P, G0, HD0]) for i in range(2)]
        by_sin = [m.sb(f"by_sin{i}", [P, G0, HD0]) for i in range(2)]
        rot = [m.sb(f"rot{i}", [P, G0, HD0]) for i in range(2)]
        kT = [m.sb(f"kT{i}", [P, KV0, P]) for i in range(2)]
        qT = [m.sb(f"qT{i}", [P, H0, P]) for i in range(2)]
        v = [m.sb(f"v{i}", [P, KV0, HD0]) for i in range(2)]
        negmax, rsum, rinv = m.sb("negmax", [P, H0]), m.sb("rsum", [P, H0]), m.sb("rinv", [P, H0])
        pe_ = [m.sb(f"probs{i}", [P, G0, P]) for i in range(2)]
        pn = [m.sb(f"probs_n{i}", [P, G0, P]) for i in range(2)]
        pT = [m.sb(f"probsT{i}", [P, G0, P]) for i in range(2)]
        oT = m.sb("oT", [P, H0, P])
        qkv_ps = [m.ps(f"qkv_ps{i}", [P, G0, HD0]) for i in range(2)]
        turn_ps = m.ps("turn_ps", [P, 4, P])
        s_ps = [m.ps(f"s_ps{i}", [P, G0, P]) for i in range(2)]
        pT_ps = m.ps("pT_ps", [P, G0, P])
        o_ps = m.ps("o_ps", [P, G0, P])
        wo_ps = m.ps("wo_ps", [P, C])

        weights_in, consts_in = m.sem("weights_in"), m.sem("consts_in")
        stats_done, var_done, sd_done, rstd_done = m.sem("b_stats_done"), m.sem("b_var_done"), m.sem("b_sd_done"), m.sem("b_rstd_done")
        z_done, ssq_done, rms_done, rrms_done = m.sem("z_done"), m.sem("ssq_done"), m.sem("rms_done"), m.sem("rrms_done")
        hn_done, hT_made, hT_out = m.sem("hn_done"), m.sem("hT_made"), m.sem("hT_out")
        qkv_made, v_out = m.sem("qkv_made"), m.sem("v_out")
        rope_mul, rot_done, rT_made, rT_out = m.sem("rope_mul"), m.sem("rot_done"), m.sem("rT_made"), m.sem("rT_out")
        s_made, max_done, exp_done, rinv_done = m.sem("s_made"), m.sem("max_done"), m.sem("exp_done"), m.sem("rinv_done")
        pn_done, pT_made, pT_out = m.sem("pn_done"), m.sem("pT_made"), m.sem("pT_out")
        o_made, o_out, wo_made, xa_done = m.sem("o_made"), m.sem("o_out"), m.sem("wo_made"), m.sem("xa_done")
        NG = 1 + KV0

        def pipeline(eng, front, step):
            front(0, 0)
            step(0, 0, False)
            with eng.Fori(0, B // 2 - 1) as i:
                step(2 * i + 1, 1, False)
                step(2 * i + 2, 0, False)
            step(B - 1, 1, True)

        with nc.Block() as block:

            @block.sync
            def _(sp):
                sp.dma_start(ln_w[:, :], io["ln_w"]).then_inc(consts_in, 16)
                sp.dma_start(rope[:, :, :], io["rope"]).then_inc(consts_in, 16)
                sp.dma_start(causal[:, :, :], io["causal"]).then_inc(consts_in, 16)
                sp.dma_start(identb[:, :], io["identb"]).then_inc(consts_in, 16)
                for w, name in ((wk, "wk0"), (wq, "wq0"), (wv, "wv0")):
                    sp.dma_start(w[:, :, :], io[name].rearrange("(cb p) o -> p cb o", p=P)).then_inc(weights_in, 16)
                sp.dma_start(wo[:, :, :], io["wo0"].rearrange("(h p) o -> p h o", p=P)).then_inc(weights_in, 16)

            @block.scalar
            def _(act):
                for h in range(2):
                    act.wait_ge(var_done, HB * (h + 1))
                    act.activation(sd[:, HB * h:HB * (h + 1)], mv[:, HB * h:HB * (h + 1), 1], ACT.Sqrt,
                                   bias=k.eps[:, 0:1]).then_inc(sd_done, 1)
                for b in range(B):
                    act.wait_ge(z_done, b + 1)
                    if b:
                        act.wait_ge(ssq_done, b)
                    act.activation(square[:, :], k.z[:, b, :], ACT.Square, accum_out=ssq[:, b:b + 1]).then_inc(ssq_done, 1)
                act.wait_ge(ssq_done, B)
                act.activation(rms[:, :], ssq[:, :], ACT.Sqrt, bias=k.eps[:, 0:1], scale=1.0 / C).then_inc(rms_done, 1)

                def hT_copy(f):
                    act.wait_ge(hT_made, f + 1)
                    wait_past(act, qkv_made, 6 * f)
                    for c in range(CB):
                        act.activation(hT[:, c, :], turn_ps[:, c, :], ACT.Copy, scale=ln_w[:, c:c + 1]).then_inc(hT_out, 1)

                def rT_copy(f, par, j):
                    act.wait_ge(rT_made, NG * f + j + 1)
                    if j < 2:
                        wait_past(act, s_made, 4 * (f - 1))
                    dst = kT[par][:, :, :] if j == 0 else qT[par][:, G0 * (j - 1):G0 * j, :]
                    act.activation(dst, turn_ps[:, :, :], ACT.Copy).then_inc(rT_out, 1)

                def v_copy(f, par):
                    act.wait_ge(qkv_made, 6 * f + 6)
                    wait_past(act, o_made, 4 * (f - 1))
                    act.activation(v[par][:, :, :], qkv_ps[1][:, :, :], ACT.Copy).then_inc(v_out, 1)

                def exps(it, g):
                    act.wait_ge(max_done, 4 * it + g + 1)
                    wait_past(act, pn_done, 4 * it + max(g - 1, 0))
                    for h in range(G0):
                        act.activation(pe_[g % 2][:, h, :], s_ps[g % 2][:, h, :], ACT.Exp,
                                       bias=negmax[:, G0 * g + h:G0 * g + h + 1],
                                       accum_out=rsum[:, G0 * g + h:G0 * g + h + 1]).then_inc(exp_done, 1)

                def o_copy(it, g):
                    act.wait_ge(o_made, 4 * it + g + 1)
                    if g == 0:
                        wait_past(act, wo_made, it)
                    act.activation(oT[:, G0 * g:G0 * (g + 1), :], o_ps[:, :, :], ACT.Copy).then_inc(o_out, 1)

                def front(f, par):
                    hT_copy(f)
                    for j in range(4):
                        rT_copy(f, par, j)
                    v_copy(f, par)
                    rT_copy(f, par, 4)

                def step(it, par, last):
                    nxt = 1 - par
                    exps(it, 0)
                    if not last:
                        hT_copy(it + 1)
                    exps(it, 1)
                    o_copy(it, 0)
                    exps(it, 2)
                    if not last:
                        rT_copy(it + 1, nxt, 0)
                    o_copy(it, 1)
                    exps(it, 3)
                    if not last:
                        rT_copy(it + 1, nxt, 1)
                    o_copy(it, 2)
                    if not last:
                        rT_copy(it + 1, nxt, 2)
                    o_copy(it, 3)
                    if not last:
                        rT_copy(it + 1, nxt, 3)
                        v_copy(it + 1, nxt)
                        rT_copy(it + 1, nxt, 4)

                pipeline(act, front, step)

            @block.tensor
            def _(pe):
                def turn_h(f):
                    pe.wait_ge(hn_done, f + 1)
                    wait_past(pe, rT_out, NG * f)
                    for c in range(CB):
                        t = pe.transpose(turn_ps[:, c, :], hn[:, P * c:P * (c + 1)], k.ident[:, :])
                    t.then_inc(hT_made, 1)

                def project(f, c):
                    if c == 0:
                        pe.wait_ge(hT_out, 2 * (f + 1))
                        wait_past(pe, rope_mul, 2 * NG * f)
                    elif c == 1:
                        wait_past(pe, v_out, f)
                    else:
                        pe.wait_ge(rope_mul, 2 * (NG * f + c - 1))
                    for cb in range(CB):
                        w = wk[:, cb, :] if c == 0 else wv[:, cb, :] if c == 5 else wq[:, cb, 512 * (c - 1):512 * c]
                        t = pe.matmul(qkv_ps[c % 2][:, :, :].rearrange("p h d -> p (h d)"), hT[:, cb, :], w,
                                      start=(cb == 0), stop=(cb == CB - 1))
                    t.then_inc(qkv_made, 1)

                def turn_r(f, par, j):
                    pe.wait_ge(rot_done, NG * f + j + 1)
                    if j == 0:
                        pe.wait_ge(hT_out, 2 * (f + 1))
                    else:
                        pe.wait_ge(rT_out, NG * f + j)
                    for h in range(G0):
                        t = pe.transpose(turn_ps[:, h, :], rot[(par + j) % 2][:, h, :], k.ident[:, :])
                    t.then_inc(rT_made, 1)

                def scores(it, par, g):
                    pe.wait_ge(rT_out, NG * it + g + 2)
                    wait_past(pe, exp_done, 16 * it + 4 * max(g - 1, 0))
                    pe.matmul(s_ps[g % 2][:, :, :].rearrange("p h s -> p (h s)"), identb[:, :],
                              causal[:, :, :].rearrange("p h s -> p (h s)"), start=True, stop=False, skip_group_check=True)
                    for h in range(G0):
                        t = pe.matmul(s_ps[g % 2][:, h, :], qT[par][:, G0 * g + h, :], kT[par][:, g, :],
                                      start=False, stop=(h == G0 - 1), skip_group_check=True)
                    t.then_inc(s_made, 1)

                def turn_p(it, g):
                    pe.wait_ge(pn_done, 4 * it + g + 1)
                    wait_past(pe, pT_out, 4 * it + g)
                    for h in range(G0):
                        t = pe.transpose(pT_ps[:, h, :], pn[g % 2][:, h, :], k.ident[:, :])
                    t.then_inc(pT_made, 1)

                def mix(it, par, g):
                    pe.wait_ge(pT_out, 4 * it + g + 1)
                    wait_past(pe, o_out, 4 * it + g)
                    pe.wait_ge(v_out, it + 1)
                    pe.matmul(o_ps[:, :, :].rearrange("p h s -> p (h s)"), v[par][:, g, :],
                              pT[g % 2][:, :, :].rearrange("p h s -> p (h s)"), start=True, stop=True).then_inc(o_made, 1)

                def output(it):
                    pe.wait_ge(o_out, 4 * it + 4)
                    wait_past(pe, xa_done, it)
                    for h in range(H0):
                        t = pe.matmul(wo_ps[:, :], oT[:, h, :], wo[:, h, :], start=(h == 0), stop=(h == H0 - 1))
                    t.then_inc(wo_made, 1)

                def front(f, par):
                    turn_h(f)
                    project(f, 0)
                    project(f, 1)
                    for j in range(4):
                        turn_r(f, par, j)
                        project(f, j + 2)
                    turn_r(f, par, 4)

                def step(it, par, last):
                    nxt = 1 - par
                    scores(it, par, 0)
                    scores(it, par, 1)
                    if not last:
                        turn_h(it + 1)
                        project(it + 1, 0)
                    turn_p(it, 0)
                    if not last:
                        project(it + 1, 1)
                    mix(it, par, 0)
                    scores(it, par, 2)
                    if not last:
                        turn_r(it + 1, nxt, 0)
                    turn_p(it, 1)
                    if not last:
                        project(it + 1, 2)
                    mix(it, par, 1)
                    scores(it, par, 3)
                    if not last:
                        turn_r(it + 1, nxt, 1)
                        project(it + 1, 3)
                    turn_p(it, 2)
                    mix(it, par, 2)
                    if not last:
                        turn_r(it + 1, nxt, 2)
                        project(it + 1, 4)
                    turn_p(it, 3)
                    mix(it, par, 3)
                    if not last:
                        turn_r(it + 1, nxt, 3)
                        project(it + 1, 5)
                        turn_r(it + 1, nxt, 4)
                    output(it)

                pe.wait_ge(weights_in, 64)
                pe.wait_ge(consts_in, 64)
                pipeline(pe, front, step)

            @block.gpsimd
            def _(pool):
                def rotate(f, par, j):
                    i = (par + j) % 2
                    pool.wait_ge(rope_mul, 2 * (NG * f + j + 1))
                    wait_past(pool, rT_made, NG * f + j - 1)
                    pool.tensor_tensor(rot[i][:, :, :], by_cos[i][:, :, :], by_sin[i][:, :, :], ALU.add).then_inc(rot_done, 1)

                def normalise(it, g):
                    pool.wait_ge(rinv_done, 4 * it + g + 1)
                    wait_past(pool, pT_made, 4 * it + max(g - 1, 0))
                    pool.tensor_tensor(pn[g % 2][:, :, :], pe_[g % 2][:, :, :],
                                       rinv[:, G0 * g:G0 * (g + 1)].unsqueeze(2).to_broadcast([P, G0, P]),
                                       ALU.mult).then_inc(pn_done, 1)

                def front(f, par):
                    for j in range(NG):
                        rotate(f, par, j)

                def step(it, par, last):
                    nxt = 1 - par
                    order = ["n0", "r0", "n1", "r1", "r2", "n2", "r3", "n3", "r4"]
                    for what in order:
                        j = int(what[1])
                        if what[0] == "n":
                            normalise(it, j)
                        elif not last:
                            rotate(it + 1, nxt, j)

                pipeline(pool, front, step)

            @block.vector
            def _(dve):
                for b in range(B):
                    dve.bn_stats(stats[:, b, :], k.x1[:, b, :]).then_inc(stats_done, 1)
                for b in range(B):
                    dve.wait_ge(stats_done, b + 1)
                    dve.bn_aggr(mv[:, b, :], stats[:, b, :]).then_inc(var_done, 1)
                for h in range(2):
                    dve.wait_ge(sd_done, h + 1)
                    dve.reciprocal(rstd[:, HB * h:HB * (h + 1)], sd[:, HB * h:HB * (h + 1)]).then_inc(rstd_done, 1)
                for h in range(2):
                    dve.wait_ge(rstd_done, h + 1)
                    for b in range(HB * h, HB * (h + 1)):
                        dve.tensor_scalar(k.z[:, b, :], k.x1[:, b, :], mv[:, b, 0:1], rstd[:, b:b + 1],
                                          ALU.subtract, ALU.mult).then_inc(z_done, 1)
                dve.wait_ge(rms_done, 1)
                dve.reciprocal(rrms[:, :], rms[:, :]).then_inc(rrms_done, 1)
                dve.wait_ge(rrms_done, 1)
                dve.wait_ge(z_done, B)
                dve.wait_ge(consts_in, 64)

                def scale_h(f):
                    wait_past(dve, hT_made, f)
                    dve.tensor_scalar(hn[:, :], k.z[:, bass.ds(f, 1), :], rrms[:, bass.ds(f, 1)], None,
                                      ALU.mult).then_inc(hn_done, 1)

                def rotary(f, par, j):
                    i, tab = (par + j) % 2, 2 if j == 0 else 0
                    dve.wait_ge(qkv_made, 6 * f + j + 1)
                    wait_past(dve, rot_done, NG * f + j - 1)
                    src, half = qkv_ps[j % 2], HD0 // 2
                    dve.tensor_tensor(by_cos[i][:, :, :], src[:, :, :],
                                      rope[:, tab:tab + 1, :].to_broadcast([P, G0, HD0]), ALU.mult).then_inc(rope_mul, 1)
                    swapped = by_sin[i][:, :, :].rearrange("p h (a d) -> p h a d", a=2)
                    pairs = src[:, :, :].rearrange("p h (a d) -> p h a d", a=2)[:, :, ::-1, :]
                    dve.tensor_tensor(swapped, pairs,
                                      rope[:, tab + 1:tab + 2, :].rearrange("p o (a d) -> p o a d", a=2)
                                      .to_broadcast([P, G0, 2, half]), ALU.mult).then_inc(rope_mul, 1)

                def maxima(it, g):
                    dve.wait_ge(s_made, 4 * it + g + 1)
                    dve.tensor_reduce(negmax[:, G0 * g:G0 * (g + 1)], s_ps[g % 2][:, :, :], AX.X, ALU.max,
                                      negate=True).then_inc(max_done, 1)

                def reciprocals(it, g):
                    dve.wait_ge(exp_done, 16 * it + 4 * g + 4)
                    wait_past(dve, pn_done, 4 * it)
                    dve.reciprocal(rinv[:, G0 * g:G0 * (g + 1)], rsum[:, G0 * g:G0 * (g + 1)]).then_inc(rinv_done, 1)

                def pT_copy(it, g):
                    dve.wait_ge(pT_made, 4 * it + g + 1)
                    wait_past(dve, o_made, 4 * it + max(g - 1, 0))
                    dve.tensor_copy(pT[g % 2][:, :, :], pT_ps[:, :, :]).then_inc(pT_out, 1)

                def add_residual(it):
                    dve.wait_ge(wo_made, it + 1)
                    dve.tensor_tensor(k.xa[:, bass.ds(it, 1), :], k.z[:, bass.ds(it, 1), :], wo_ps[:, :].unsqueeze(1),
                                      ALU.add).then_inc(xa_done, 1)

                def front(f, par):
                    scale_h(f)
                    for j in range(NG):
                        rotary(f, par, j)

                def step(it, par, last):
                    nxt = 1 - par
                    if not last:
                        scale_h(it + 1)
                    maxima(it, 0)
                    maxima(it, 1)
                    reciprocals(it, 0)
                    if not last:
                        rotary(it + 1, nxt, 0)
                    pT_copy(it, 0)
                    reciprocals(it, 1)
                    maxima(it, 2)
                    if not last:
                        rotary(it + 1, nxt, 1)
                    pT_copy(it, 1)
                    maxima(it, 3)
                    if not last:
                        rotary(it + 1, nxt, 2)
                    reciprocals(it, 2)
                    pT_copy(it, 2)
                    if not last:
                        rotary(it + 1, nxt, 3)
                    reciprocals(it, 3)
                    pT_copy(it, 3)
                    if not last:
                        rotary(it + 1, nxt, 4)
                    add_residual(it)

                pipeline(dve, front, step)
def earlier(j, par):
    return (j - par) // 2 if isinstance(j, int) else (j - par) >> 1


f32r = mybir.dt.float32r


def low(eng, out, x, high):
    return eng.tensor_tensor(out, x, high.bitcast(fp32), ALU.subtract)


def products(pe, out, stationary, moving, first, last):
    (sh, sl), (mh, ml) = stationary, moving
    pe.matmul(out, sh, mh, start=first, stop=False, skip_group_check=True)
    pe.matmul(out, sh, ml, start=False, stop=False, skip_group_check=True)
    return pe.matmul(out, sl, mh, start=False, stop=last, skip_group_check=True)


E0, FF0 = 8, 896
FB = FF0 // P
PACK = 4 * P + C
RING = 4
SLOTS = 256
SG = SLOTS // P
TILES = 2 * T // SLOTS + E0 - 1


def experts0_stage(nc, k, io):
    x_slots = nc.dram_tensor("x_slots", (TILES * SLOTS, C), fp32, kind="Internal").ap()
    y_slots = nc.dram_tensor("y_slots", (TILES * SLOTS, C), fp32, kind="Internal").ap()
    with Memory(nc) as m:
        square = m.sb("c_square", [P, C])
        ssq, rms, rrms = m.sb("c_ssq", [P, B]), m.sb("c_rms", [P, B]), m.sb("c_rrms", [P, B])
        ff_w, gate_w = m.sb("ff_w", [P, C]), m.sb("gate_w", [P, CB, E0])
        iota_e, iota_t = m.sb("iota_e", [P, E0]), m.sb("iota_t", [P, TILES])
        before, ones = m.sb("before", [P, P], bf16), m.sb("ones", [P, P], bf16)
        zeros = m.sb("zeros", [P, 1920])
        h2, h2T = m.sb("h2", [P, B, C]), m.sb("h2T", [P, B, C])
        logits = m.sb("logits", [P, B, E0])
        top, top_i, top_f = m.sb("top", [P, B, 8]), m.sb("top_i", [P, B, 8], u32), m.sb("top_f", [P, B, 2])
        gap, gap_exp, gate_den = m.sb("gap", [P, B]), m.sb("gap_exp", [P, B]), m.sb("gate_den", [P, B])
        gates = m.sb("gates", [P, 2, B])
        pick = m.sb("pick", [P, 2, B, E0])
        picked = m.sb("picked", [P, B, E0], bf16)
        count, tiles_of = m.sb("count", [P, E0]), m.sb("tiles_of", [P, 4, E0])
        tile_end, first_slot = m.sb("tile_end", [P, E0]), m.sb("first_slot", [P, E0])
        place = m.sb("place", [P, B, E0])
        at = m.sb("at", [P, 2, B, E0])
        slot_f, slot = m.sb("slot_f", [P, 2 * B]), m.sb("slot", [P, 2 * B], u32)
        ended, expert_f = m.sb("ended", [P, TILES, E0]), m.sb("expert_f", [P, TILES])
        expert = m.sb("expert", [P, TILES], u32)
        w = [m.sb(f"c_w{f}", [P, PACK]) for f in range(FB)]
        w_hi = [m.sb(f"c_w_hi{f}", [P, PACK], f32r) for f in range(FB)]
        w_lo = [m.sb(f"c_w_lo{f}", [P, PACK], f32r) for f in range(FB)]
        xs = [m.sb(f"xs{i}", [P, SG, C]) for i in range(2)]
        xT_hi = [m.sb(f"xT_hi{i}", [P, CB, SLOTS], f32r) for i in range(2)]
        xT_lo = [m.sb(f"xT_lo{i}", [P, CB, SLOTS], f32r) for i in range(2)]
        silu = [m.sb(f"silu{i}", [P, SLOTS]) for i in range(2)]
        hid = [m.sb(f"hid{i}", [P, SLOTS]) for i in range(2)]
        h_hi = [m.sb(f"c_h_hi{i}", [P, SLOTS], f32r) for i in range(RING)]
        h_lo = [m.sb(f"c_h_lo{i}", [P, SLOTS], f32r) for i in range(RING)]
        ys = [m.sb(f"ys{i}", [P, SG, C]) for i in range(2)]
        y_pair = m.sb("y_pair", [P, 2 * B, C])
        xT_ps = m.ps("xT_ps", [P, CB, SLOTS])
        gu_ps = [m.ps(f"gu_ps{i}", [P, 2, SLOTS]) for i in range(RING)]
        y_ps = [m.ps(f"ey_ps{i}", [P, SG, C]) for i in range(2)]
        cnt_ps = m.ps("cnt_ps", [P, 3, B, E0])

        s = lambda name: m.sem("c_" + name)
        consts_in, zeros_set, slots_clear = s("consts_in"), s("zeros_set"), s("slots_clear")
        ssq_done, rms_done, rrms_done, h2_done, h2T_made, h2T_out = s("ssq"), s("rms"), s("rrms"), s("h2"), s("h2T_made"), s("h2T_out")
        logits_made, logits_out, top_done, index_done, index_f = s("logits_made"), s("logits_out"), s("top"), s("index"), s("index_f")
        gap_done, gap_exp_done, gate_step = s("gap"), s("gap_exp"), s("gate_step")
        pick_done, picked_done, ranks_made, plan_step = s("pick"), s("picked"), s("ranks_made"), s("plan_step")
        slot_done, expert_done, sent = s("slot"), s("expert"), s("sent")
        w_in = [s(f"w_in{f}") for f in range(FB)]
        w_hi_done, w13_lo_done, w2_lo_done = s("w_hi"), s("w13_lo"), s("w2_lo")
        xs_in = [s(f"xs_in{i}") for i in range(2)]
        xT_made, xT_hi_done, xT_lo_done = s("xT_made"), s("xT_hi"), s("xT_lo")
        gu_made, silu_done, hid_done, h_hi_done, h_lo_done = s("gu_made"), s("silu"), s("hid"), s("h_hi"), s("h_lo")
        added, y_out = s("added"), s("y_out")
        stored = [s(f"stored{i}") for i in range(2)]
        base_done, x2_step = s("base"), s("x2_step")
        fetched = [s(f"fetched{b}") for b in range(B)]

        def tiles(eng, step):
            step(0, 0)
            step(1, 1)
            with eng.Fori(1, TILES // 2) as i:
                step(2 * i, 0)
                step(2 * i + 1, 1)
            step(TILES - 1, 0)

        def ring_free(eng, sem, j, f):
            n = FB * j + f
            wait_past(eng, sem, n + 1 - (RING if f >= RING else FB if f == RING - 1 else FB - RING))

        def ahead(j, f, by):
            return (j, f + by) if f + by < FB else (j + 1, f + by - FB)

        def is_last(j):
            return isinstance(j, int) and j == TILES - 1

        with nc.Block() as block:

            @block.sync
            def _(sp):
                sp.dma_start(ff_w[:, :], io["ff_w"]).then_inc(consts_in, 16)
                sp.dma_start(gate_w[:, :, :], io["gate_w0"].rearrange("(cb p) e -> p cb e", p=P)).then_inc(consts_in, 16)
                sp.dma_start(iota_e[:, :], io["iota"][:, 0:E0]).then_inc(consts_in, 16)
                sp.dma_start(iota_t[:, :], io["iota"][:, 0:TILES]).then_inc(consts_in, 16)
                sp.dma_start(before[:, :], io["before"]).then_inc(consts_in, 16)
                sp.dma_start(ones[:, :], io["ones"]).then_inc(consts_in, 16)
                sp.wait_ge(zeros_set, 1)
                flat = x_slots.rearrange("(p r) c -> p (r c)", p=P)
                for i in range(4):
                    sp.dma_start(flat[:, 1920 * i:1920 * (i + 1)], zeros[:, :]).then_inc(slots_clear, 16)
                sp.wait_ge(expert_done, 1)

                def load(j, par):
                    e = sp.value_load(expert[0:1, bass.ds(j, 1)], min_val=0, max_val=E0 - 1)
                    first = isinstance(j, int) and j == 0
                    if not first:
                        load_x(j, par)
                    for f in range(FB):
                        for split in (w_hi_done, w13_lo_done, w2_lo_done):
                            wait_past(sp, split, FB * (j - 1) + f + 1)
                        sp.dma_start(w[f][:, :], io["pack0"][bass.ds(e, 1), :, PACK * f:PACK * (f + 1)].rearrange("o p n -> (o p) n"))\
                            .then_inc(w_in[f], 16)
                    if first:
                        sp.wait_ge(sent, 16 * 2 * B)
                        load_x(j, par)

                def load_x(j, par):
                    wait_past(sp, xT_made, j - 1)
                    sp.dma_start(xs[par][:, :, :], x_slots[bass.ds(j * SLOTS, SLOTS), :].rearrange("(r p) c -> p r c", p=P)).then_inc(xs_in[par], 16)

                tiles(sp, load)
                for h in range(2):
                    sp.wait_ge(stored[h], 16 * ((TILES + 1 - h) // 2))

            @block.scalar
            def _(act):
                for b in range(B):
                    if b:
                        act.wait_ge(ssq_done, b)
                    act.activation(square[:, :], k.xa[:, b, :], ACT.Square, accum_out=ssq[:, b:b + 1]).then_inc(ssq_done, 1)
                act.wait_ge(ssq_done, B)
                act.activation(rms[:, :], ssq[:, :], ACT.Sqrt, bias=k.eps[:, 0:1], scale=1.0 / C).then_inc(rms_done, 1)
                for n in range(B // 2):
                    act.wait_ge(h2T_made, n + 1)
                    act.activation(h2T[:, 2 * n:2 * n + 2, :], gu_ps[n][:, :, :], ACT.Copy).then_inc(h2T_out, 1)
                act.wait_ge(logits_made, 1)
                act.activation(logits[:, :, :], cnt_ps[:, 0, :, :], ACT.Copy).then_inc(logits_out, 1)
                act.wait_ge(gap_done, 1)
                act.activation(gap_exp[:, :], gap[:, :], ACT.Exp).then_inc(gap_exp_done, 1)

                def round_w(j, f):
                    act.wait_ge(w_in[f], 16 * j + 16)
                    wait_past(act, added, FB * (j - 1) + f + 1)
                    act.activation(w_hi[f][:, :], w[f][:, :], ACT.Copy).then_inc(w_hi_done, 1)

                def round_x(j, par):
                    act.wait_ge(xT_made, j + 1)
                    act.activation(xT_hi[par][:, :, :], xT_ps[:, :, :], ACT.Copy).then_inc(xT_hi_done, 1)

                def store(j, par):
                    act.wait_ge(added, FB * (j + 1))
                    wait_past(act, stored[par], 16 * earlier(j, par))
                    act.activation(ys[par][:, :, :], y_ps[par][:, :, :], ACT.Copy).then_inc(y_out, 1)
                    act.wait_ge(y_out, j + 1)
                    act.dma_start(y_slots[bass.ds(j * SLOTS, SLOTS), :].rearrange("(r p) c -> p r c", p=P),
                                  ys[par][:, :, :]).then_inc(stored[par], 16)

                def work(j, par):
                    for f in range(FB):
                        i = (par + f) % 2
                        n = FB * j + f
                        act.wait_ge(gu_made, n + 1)
                        wait_past(act, hid_done, n - 1)
                        act.activation(silu[i][:, :], gu_ps[f % RING][:, 0, :], ACT.Silu).then_inc(silu_done, 1)
                        if f == 3 and not (isinstance(j, int) and j == 0):
                            store(j - 1, 1 - par)
                        if f == 4 and not is_last(j):
                            round_x(j + 1, 1 - par)
                        if f + 3 < FB or not is_last(j):
                            round_w(*ahead(j, f, 3))

                for f in range(3):
                    round_w(0, f)
                round_x(0, 0)
                tiles(act, work)
                store(TILES - 1, 0)

            @block.tensor
            def _(pe):
                for b in range(B):
                    pe.wait_ge(h2_done, b + 1)
                    for c in range(CB):
                        t = pe.transpose(gu_ps[b // 2][:, b % 2, P * c:P * (c + 1)], h2[:, b, P * c:P * (c + 1)], k.ident[:, :])
                    if b % 2:
                        t.then_inc(h2T_made, 1)
                pe.wait_ge(consts_in, 96)
                for b in range(B):
                    pe.wait_ge(h2T_out, b // 2 + 1)
                    for c in range(CB):
                        t = pe.matmul(cnt_ps[:, 0, b, :], h2T[:, b, P * c:P * (c + 1)], gate_w[:, c, :],
                                      start=(c == 0), stop=(c == CB - 1))
                t.then_inc(logits_made, 1)
                pe.wait_ge(picked_done, 1)
                pe.wait_ge(logits_out, 1)
                flat = lambda a: a.rearrange("p b e -> p (b e)")
                pe.matmul(flat(cnt_ps[:, 2, :, :]), ones[:, :], flat(picked[:, :, :]), start=True, stop=True, skip_group_check=True)
                pe.matmul(flat(cnt_ps[:, 1, :, :]), before[:, :], flat(picked[:, :, :]), start=True, stop=False, skip_group_check=True)
                for b in range(B - 1):
                    t = pe.matmul(cnt_ps[:, 1, b + 1:B, :], ones[:, :], picked[:, b:b + 1, :].to_broadcast([P, B - 1 - b, E0]),
                                  start=False, stop=(b == B - 2), skip_group_check=True)
                t.then_inc(ranks_made, 1)

                def turn(j, par):
                    pe.wait_ge(xs_in[par], 16 * earlier(j, par) + 16)
                    wait_past(pe, xT_lo_done, j)
                    for r in range(SG):
                        for c in range(CB):
                            t = pe.transpose(xT_ps[:, c, P * r:P * (r + 1)], xs[par][:, r, P * c:P * (c + 1)], k.ident[:, :])
                    t.then_inc(xT_made, 1)

                def up(j, par, f):
                    if f == 0:
                        pe.wait_ge(xT_lo_done, j + 1)
                    pe.wait_ge(w13_lo_done, FB * j + f + 1)
                    ring_free(pe, hid_done, j, f)
                    for what in range(2):
                        for c in range(CB):
                            cols = slice(P * (2 * what + c), P * (2 * what + c + 1))
                            t = products(pe, gu_ps[f % RING][:, what, :], (w_hi[f][:, cols], w_lo[f][:, cols]),
                                         (xT_hi[par][:, c, :], xT_lo[par][:, c, :]), c == 0, c == CB - 1)
                    t.then_inc(gu_made, 1)

                def down(j, par, f):
                    n = FB * j + f
                    pe.wait_ge(h_lo_done, n + 1)
                    pe.wait_ge(w2_lo_done, n + 1)
                    if f == 0:
                        wait_past(pe, y_out, j - 1)
                    for r in range(SG):
                        rows = slice(P * r, P * (r + 1))
                        t = products(pe, y_ps[par][:, r, :], (h_hi[f % RING][:, rows], h_lo[f % RING][:, rows]),
                                     (w_hi[f][:, 4 * P:PACK], w_lo[f][:, 4 * P:PACK]), f == 0 and r == 0, f == FB - 1 and r == SG - 1)
                    t.then_inc(added, 1)

                def work(j, par):
                    for f in range(FB):
                        if f == 3 and not is_last(j):
                            turn(j + 1, 1 - par)
                        up(j, par, f)
                        if f >= 2:
                            down(j, par, f - 2)
                        elif not (isinstance(j, int) and j == 0):
                            down(j - 1, 1 - par, FB + f - 2)

                turn(0, 0)
                tiles(pe, work)
                down(TILES - 1, 0, FB - 2)
                down(TILES - 1, 0, FB - 1)

            @block.gpsimd
            def _(pool):
                for b in range(B):
                    pool.tensor_tensor(k.x1[:, b, :], k.x1[:, b, :], k.xa[:, b, :], ALU.add).then_inc(base_done, 1)
                pool.wait_ge(slots_clear, 64)
                for n in range(2 * B):
                    pool.wait_ge(slot_done, 1)
                    pool.wait_ge(h2_done, n % B + 1)
                    pool.indirect_dma_start(x_slots, bass.IndirectOffsetOnAxis(slot[:, n:n + 1], 0), h2[:, n % B, :],
                                            None).then_inc(sent, 16)
                def split_w(j, par):
                    for f in range(FB):
                        pool.wait_ge(w_hi_done, FB * j + f + 1)
                        low(pool, w_lo[f][:, 0:4 * P], w[f][:, 0:4 * P], w_hi[f][:, 0:4 * P]).then_inc(w13_lo_done, 1)

                tiles(pool, split_w)
                for h in range(2):
                    pool.wait_ge(stored[h], 16 * ((TILES + 1 - h) // 2))
                for b in range(B):
                    for i in range(2):
                        n = B * i + b
                        pool.indirect_dma_start(y_pair[:, n, :], None, y_slots, bass.IndirectOffsetOnAxis(slot[:, n:n + 1], 0)).then_inc(fetched[b], 16)

            @block.vector
            def _(dve):
                dve.memset(zeros[:, :], 0.0).then_inc(zeros_set, 1)
                dve.wait_ge(rms_done, 1)
                dve.reciprocal(rrms[:, :], rms[:, :]).then_inc(rrms_done, 1)
                dve.wait_ge(rrms_done, 1)
                dve.wait_ge(consts_in, 96)
                for b in range(B):
                    dve.scalar_tensor_tensor(h2[:, b, :], k.xa[:, b, :], rrms[:, b:b + 1], ff_w[:, :], ALU.mult, ALU.mult)\
                        .then_inc(h2_done, 1)
                dve.wait_ge(logits_out, 1)
                for b in range(B):
                    dve.max(top[:, b, :], logits[:, b, :]).then_inc(top_done, 1)
                for b in range(B):
                    dve.wait_ge(top_done, b + 1)
                    dve.max_index(top_i[:, b, :], top[:, b, :], logits[:, b, :]).then_inc(index_done, 1)
                dve.tensor_tensor(gap[:, :], top[:, :, 1], top[:, :, 0], ALU.subtract).then_inc(gap_done, 1)
                dve.wait_ge(index_done, B)
                dve.tensor_copy(top_f[:, :, :], top_i[:, :, 0:2]).then_inc(index_f, 1)
                dve.wait_ge(index_f, 1)
                for i in range(2):
                    dve.tensor_tensor(pick[:, i, :, :], iota_e[:, :].unsqueeze(1).to_broadcast([P, B, E0]),
                                      top_f[:, :, i:i + 1].to_broadcast([P, B, E0]), ALU.is_equal).then_inc(pick_done, 1)
                dve.wait_ge(pick_done, 2)
                dve.tensor_tensor(picked[:, :, :], pick[:, 0, :, :], pick[:, 1, :, :], ALU.add).then_inc(picked_done, 1)
                dve.wait_ge(gap_exp_done, 1)
                dve.tensor_scalar(gate_den[:, :], gap_exp[:, :], 1.0, None, ALU.add).then_inc(gate_step, 1)
                dve.wait_ge(gate_step, 1)
                dve.reciprocal(gates[:, 0, :], gate_den[:, :]).then_inc(gate_step, 1)
                dve.wait_ge(gate_step, 2)
                dve.tensor_tensor(gates[:, 1, :], gates[:, 0, :], gap_exp[:, :], ALU.mult).then_inc(gate_step, 1)
                dve.wait_ge(ranks_made, 1)
                dve.tensor_reduce(count[:, :], cnt_ps[:, 2, :, :].rearrange("p b e -> p e b"), AX.X, ALU.add).then_inc(plan_step, 1)
                dve.wait_ge(plan_step, 1)
                dve.tensor_scalar(tiles_of[:, 0, :], count[:, :], 0.0, None, ALU.is_gt).then_inc(plan_step, 1)
                for i in range(1, T // SLOTS):
                    dve.wait_ge(plan_step, i + 1)
                    dve.scalar_tensor_tensor(tiles_of[:, i, :], count[:, :], float(SLOTS * i), tiles_of[:, i - 1, :],
                                             ALU.is_gt, ALU.add).then_inc(plan_step, 1)
                last = T // SLOTS - 1
                dve.wait_ge(plan_step, last + 2)
                dve.tensor_tensor_scan(tile_end[:, :], tiles_of[:, last, :], tiles_of[:, last, :], 0.0, ALU.add, ALU.bypass)\
                    .then_inc(plan_step, 1)
                dve.wait_ge(plan_step, last + 3)
                dve.tensor_tensor(first_slot[:, :], tile_end[:, :], tiles_of[:, last, :], ALU.subtract).then_inc(plan_step, 1)
                dve.wait_ge(plan_step, last + 4)
                dve.scalar_tensor_tensor(place[:, :, :], first_slot[:, :].unsqueeze(1).to_broadcast([P, B, E0]), float(SLOTS),
                                         cnt_ps[:, 1, :, :], ALU.mult, ALU.add).then_inc(plan_step, 1)
                dve.wait_ge(plan_step, last + 5)
                for i in range(2):
                    dve.tensor_tensor(at[:, i, :, :], pick[:, i, :, :], place[:, :, :], ALU.mult).then_inc(plan_step, 1)
                dve.wait_ge(plan_step, last + 7)
                dve.tensor_reduce(slot_f[:, :], at[:, :, :, :].rearrange("p i b e -> p (i b) e"), AX.X, ALU.add).then_inc(plan_step, 1)
                dve.wait_ge(plan_step, last + 8)
                dve.tensor_copy(slot[:, :], slot_f[:, :]).then_inc(slot_done, 1)
                dve.tensor_tensor(ended[:, :, :], iota_t[:, :].unsqueeze(2).to_broadcast([P, TILES, E0]),
                                  tile_end[:, :].unsqueeze(1).to_broadcast([P, TILES, E0]), ALU.is_ge).then_inc(plan_step, 1)
                dve.wait_ge(plan_step, last + 9)
                dve.tensor_reduce(expert_f[:, :], ended[:, :, :], AX.X, ALU.add).then_inc(plan_step, 1)
                dve.wait_ge(plan_step, last + 10)
                dve.tensor_scalar(expert[:, :], expert_f[:, :], float(E0 - 1), None, ALU.min).then_inc(expert_done, 1)

                def split_w2(j, f):
                    dve.wait_ge(w_hi_done, FB * j + f + 1)
                    low(dve, w_lo[f][:, 4 * P:PACK], w[f][:, 4 * P:PACK], w_hi[f][:, 4 * P:PACK]).then_inc(w2_lo_done, 1)

                def split_x(j, par):
                    dve.wait_ge(xT_hi_done, j + 1)
                    low(dve, xT_lo[par][:, :, :], xT_ps[:, :, :], xT_hi[par][:, :, :]).then_inc(xT_lo_done, 1)

                def work(j, par):
                    for f in range(FB):
                        i = (par + f) % 2
                        n = FB * j + f
                        dve.wait_ge(silu_done, n + 1)
                        dve.tensor_tensor(hid[i][:, :], gu_ps[f % RING][:, 1, :], silu[i][:, :], ALU.mult).then_inc(hid_done, 1)
                        if f + 2 < FB or not is_last(j):
                            split_w2(*ahead(j, f, 2))
                        dve.wait_ge(hid_done, n + 1)
                        ring_free(dve, added, j, f)
                        dve.tensor_copy(h_hi[f % RING][:, :], hid[i][:, :]).then_inc(h_hi_done, 1)
                        dve.wait_ge(h_hi_done, n + 1)
                        low(dve, h_lo[f % RING][:, :], hid[i][:, :], h_hi[f % RING][:, :]).then_inc(h_lo_done, 1)
                        if f == 4 and not is_last(j):
                            split_x(j + 1, 1 - par)

                for f in range(2):
                    split_w2(0, f)
                split_x(0, 0)
                tiles(dve, work)
                dve.wait_ge(base_done, B)
                dve.wait_ge(gate_step, 3)
                for b in range(B):
                    dve.wait_ge(fetched[b], 32)
                    for i in range(2):
                        if i:
                            dve.wait_ge(x2_step, 2 * b + 1)
                        dve.scalar_tensor_tensor(k.x1[:, b, :], y_pair[:, B * i + b, :], gates[:, i, b:b + 1], k.x1[:, b, :],
                                                 ALU.mult, ALU.add).then_inc(x2_step, 1)
H1, HD1 = 16, 16
HG = 4
GROUPS = H1 // HG
HPB = P // HD1
STRIDE = P + HD1
MAGIC = 1.5 * 2.0 ** 23
QMAX, QEPS = 127.0, 1e-8


def cross_stage(nc, k, io):
    with Memory(nc) as m:
        stats, mv = m.sb("d_stats", [P, B, 6]), m.sb("d_mean_var", [P, B, 2])
        sd, rstd = m.sb("d_sd", [P, B]), m.sb("d_rstd", [P, B])
        y = m.sb("d_y", [P, B, C])
        top, step_x, inv_x = m.sb("d_top", [P, 2, B]), m.sb("d_step", [P, 2, B]), m.sb("d_inv", [P, 2, B])
        yq = m.sb("d_yq", [P, B, C], bf16)
        yqT = m.sb("d_yqT", [P, CB, T], bf16)
        w = m.sb("d_w", [P, 2, CB, C])
        w_top, w_step, w_inv = m.sb("w_top", [P, 2 * CB]), m.sb("w_step", [P, 2 * CB]), m.sb("w_inv", [P, 2 * CB])
        w_q = m.sb("w_q", [P, 2, CB, C], bf16)
        w_qT = m.sb("w_qT", [P, 2, CB, C], bf16)
        w_diag = m.sb("w_diag", [P, 2 * CB, P])
        step_row = m.sb("step_row", [P, 2, C])
        bias_row = m.sb("bias_row", [P, 2, C])
        ones = m.sb("d_ones", [P, P])
        identb = m.sb("d_identb", [P, P], bf16)
        head_mask = m.sb("head_mask", [P, HPB])
        mask = m.sb("d_mask", [P, B, P])
        q1T = m.sb("q1T", [P, CB, T])
        qb = [m.sb(f"qb{i}", [P, CB, P]) for i in range(2)]
        kz = [m.sb(f"kz{i}", [P, H1, P]) for i in range(2)]
        vz = [m.sb(f"vz{i}", [P, CB, HPB * STRIDE]) for i in range(2)]
        sm = [m.sb(f"sm{g}", [P, HG, P]) for g in range(GROUPS)]
        probs = [m.sb(f"d_probs{g}", [P, HG, P]) for g in range(GROUPS)]
        pT = [m.sb(f"d_pT{g}", [P, HG, P]) for g in range(GROUPS)]
        negmax, rsum, rinv = (m.sb(n, [P, 2, H1]) for n in ("d_negmax", "d_rsum", "d_rinv"))
        banks = [m.ps(f"d_bank{i}", [P, 512]) for i in range(8)]
        half = lambda i: banks[i][:, :].bitcast(bf16)

        s = lambda name: m.sem("d_" + name)
        consts_in, w_in, mask_in = s("consts_in"), s("w_in"), s("mask_in")
        ones_set, vz_set = s("ones_set"), s("vz_set")
        w_step_done, w_q_done, w_diag_done, w_turned, w_copied, row_made, row_out = (
            s("w_step"), s("w_q"), s("w_diag"), s("w_turned"), s("w_copied"), s("row_made"), s("row_out"))
        stats_done, var_done, sd_done, rstd_done, y_done = s("stats"), s("var"), s("sd"), s("rstd"), s("y")
        step_done, quant_done, yq_done = s("step"), s("quant"), s("yq")
        turned, yqT_out, q_made, q_scaled, q_done, qT_made, qT_out = (
            s("turned"), s("yqT_out"), s("q_made"), s("q_scaled"), s("q"), s("qT_made"), s("qT_out"))
        qb_done, kz_done, vz_done = s("qb"), s("kz"), s("vz")
        s_made, sm_done, max_done, exp_done, rinv_done = s("s_made"), s("sm"), s("max"), s("exp"), s("rinv")
        pT_made, pT_out, o_made, o_out = s("pT_made"), s("pT_out"), s("o_made"), s("o_out")
        r_made, r_step, x3_done = s("r_made"), s("r_step"), s("x3")

        def quantise(eng, src, out, which):
            for b in range(B):
                eng.tensor_scalar(src[:, b, :], src[:, b, :], inv_x[:, which, b:b + 1], QMAX, ALU.mult, ALU.min).then_inc(quant_done, 1)
            eng.wait_ge(quant_done, (B + 1) * which + B)
            eng.tensor_scalar(src[:, :, :], src[:, :, :], -QMAX, MAGIC, ALU.max, ALU.add).then_inc(quant_done, 1)
            eng.wait_ge(quant_done, (B + 1) * (which + 1))
            eng.tensor_scalar(out[:, :, :], src[:, :, :], MAGIC, None, ALU.subtract).then_inc(yq_done, 1)

        def row_steps(eng, src, which):
            eng.tensor_reduce(top[:, which, :], src[:, :, :], AX.X, ALU.max, apply_absolute_value=True).then_inc(step_done, 1)
            eng.wait_ge(step_done, 3 * which + 1)
            eng.tensor_scalar(step_x[:, which, :], top[:, which, :], 1.0 / QMAX, QEPS, ALU.mult, ALU.max).then_inc(step_done, 1)
            eng.wait_ge(step_done, 3 * which + 2)
            eng.reciprocal(inv_x[:, which, :], step_x[:, which, :]).then_inc(step_done, 1)
            eng.wait_ge(step_done, 3 * which + 3)

        def sequences(eng, step):
            step(0, 0, False)
            with eng.Fori(0, B // 2 - 1) as i:
                step(2 * i + 1, 1, False)
                step(2 * i + 2, 0, False)
            step(B - 1, 1, True)

        with nc.Block() as block:

            @block.sync
            def _(sp):
                sp.dma_start(w[:, 0, :, :], io["wq1"].rearrange("(ob p) c -> p ob c", p=P)).then_inc(w_in, 16)
                sp.dma_start(w[:, 1, :, :], io["wo1"].rearrange("(ob p) c -> p ob c", p=P)).then_inc(w_in, 16)
                sp.dma_start(bias_row[:, :, :], io["bias_row"]).then_inc(consts_in, 16)
                sp.dma_start(identb[:, :], io["identb"]).then_inc(consts_in, 16)
                sp.dma_start(head_mask[:, :], io["head_mask"]).then_inc(consts_in, 16)
                sp.dma_start(mask[:, :, :], io["mask"].rearrange("b q s -> q b s")).then_inc(mask_in, 16)

            @block.scalar
            def _(act):
                for h in range(2):
                    act.wait_ge(var_done, HB * (h + 1))
                    act.activation(sd[:, HB * h:HB * (h + 1)], mv[:, HB * h:HB * (h + 1), 1], ACT.Sqrt,
                                   bias=k.eps[:, 0:1]).then_inc(sd_done, 1)
                act.wait_ge(w_turned, 2)
                act.activation(w_qT[:, :, :, :].rearrange("p i c o -> p (i c o)"), half(0), ACT.Copy).then_inc(w_copied, 1)
                act.wait_ge(row_made, 1)
                act.activation(step_row[:, :, :].rearrange("p i c -> p (i c)"), banks[1][:, :], ACT.Copy).then_inc(row_out, 1)
                for c in range(CB):
                    act.wait_ge(turned, c + 1)
                    act.activation(yqT[:, c, :], half(2 + c), ACT.Copy).then_inc(yqT_out, 1)
                for c in range(CB):
                    for h in range(2):
                        n = 2 * c + h
                        act.wait_ge(qT_made, n + 1)
                        act.activation(q1T[:, c, 512 * h:512 * (h + 1)], banks[n][:, :], ACT.Copy).then_inc(qT_out, 1)

                def exps(it, par, g):
                    act.wait_ge(max_done, GROUPS * it + g + 1)
                    wait_past(act, pT_made, GROUPS * (it - 1) + g + 1)
                    if g == 0:
                        wait_past(act, rinv_done, it - 1)
                    for h in range(HG):
                        n = HG * g + h
                        t = act.activation(probs[g][:, h, :], sm[g][:, h, :], ACT.Exp, bias=negmax[:, par, n:n + 1],
                                           accum_out=rsum[:, par, n:n + 1])
                        t.then_inc(exp_done, 1)

                def step(it, par, last):
                    for g in range(GROUPS):
                        exps(it, par, g)

                sequences(act, step)
                for c in range(CB):
                    act.wait_ge(turned, CB + c + 1)
                    act.activation(yqT[:, c, :], half(2 + c), ACT.Copy).then_inc(yqT_out, 1)

            @block.tensor
            def _(pe):
                pe.wait_ge(consts_in, 48)
                pe.wait_ge(w_q_done, 1)
                for i in range(2):
                    for c in range(CB):
                        for ob in range(CB):
                            t = pe.transpose(half(0)[:, (i * CB + c) * C + P * ob:(i * CB + c) * C + P * (ob + 1)],
                                             w_q[:, i, ob, P * c:P * (c + 1)], identb[:, :])
                    t.then_inc(w_turned, 1)
                pe.wait_ge(w_diag_done, 2 * CB)
                pe.wait_ge(ones_set, 1)
                for n in range(2 * CB):
                    t = pe.matmul(banks[1][:, P * n:P * (n + 1)], ones[:, :], w_diag[:, n, :], start=True, stop=True)
                t.then_inc(row_made, 1)
                pe.wait_ge(yq_done, 1)
                for c in range(CB):
                    for b in range(B):
                        t = pe.transpose(half(2 + c)[:, P * b:P * (b + 1)], yq[:, b, P * c:P * (c + 1)], identb[:, :])
                    t.then_inc(turned, 1)
                pe.wait_ge(w_copied, 1)
                pe.wait_ge(yqT_out, CB)
                for b in range(B):
                    for c in range(CB):
                        t = pe.matmul(banks[4 + b // 2][:, C * (b % 2):C * (b % 2 + 1)], yqT[:, c, P * b:P * (b + 1)],
                                      w_qT[:, 0, c, :], start=(c == 0), stop=(c == CB - 1))
                    t.then_inc(q_made, 1)
                pe.wait_ge(row_out, 1)
                for c in range(CB):
                    for h in range(2):
                        pe.wait_ge(q_done, HB * (h + 1))
                        for b in range(HB * h, HB * (h + 1)):
                            t = pe.transpose(banks[2 * c + h][:, P * (b % HB):P * (b % HB + 1)], y[:, b, P * c:P * (c + 1)], k.ident[:, :])
                        t.then_inc(qT_made, 1)

                def scores(it, par, g):
                    if g == 0:
                        pe.wait_ge(qb_done, it + 1)
                        pe.wait_ge(kz_done, 2 * (it + 1))
                    wait_past(pe, sm_done, GROUPS * it + g - 1)
                    pe.matmul(banks[g % 2][:, :], qb[par][:, g // 2, :],
                              kz[par][:, HG * g:HG * (g + 1), :].rearrange("p h s -> p (h s)"), start=True, stop=True).then_inc(s_made, 1)

                def turn_p(it, g):
                    pe.wait_ge(exp_done, H1 * it + HG * (g + 1))
                    wait_past(pe, pT_out, GROUPS * it + g - 1)
                    for h in range(HG):
                        t = pe.transpose(banks[2 + g % 2][:, P * h:P * (h + 1)], probs[g][:, h, :], k.ident[:, :])
                    t.then_inc(pT_made, 1)

                def mix(it, par, g):
                    if g == 0:
                        pe.wait_ge(vz_done, it + 1)
                        wait_past(pe, o_out, it - 1)
                    pe.wait_ge(pT_out, GROUPS * it + g + 1)
                    c = g // 2
                    for h in range(HG):
                        j = HG * (g % 2) + h
                        t = pe.matmul(banks[4 + par][:, P * c:P * (c + 1)], pT[g][:, h, :], vz[par][:, c, P * j:P * (j + 1)],
                                      start=(j == 0), stop=(j == HPB - 1))
                    t.then_inc(o_made, 1)

                scores(0, 0, 0)
                scores(0, 0, 1)

                def step(it, par, last):
                    for g in range(GROUPS):
                        if g < GROUPS - 2:
                            scores(it, par, g + 2)
                        elif not last:
                            scores(it + 1, 1 - par, g + 2 - GROUPS)
                        turn_p(it, g)
                        if g:
                            mix(it, par, g - 1)
                        elif not (isinstance(it, int) and it == 0):
                            mix(it - 1, 1 - par, GROUPS - 1)

                sequences(pe, step)
                mix(B - 1, 1, GROUPS - 1)
                pe.wait_ge(yq_done, 2)
                for c in range(CB):
                    for b in range(B):
                        t = pe.transpose(half(2 + c)[:, P * b:P * (b + 1)], yq[:, b, P * c:P * (c + 1)], identb[:, :])
                    t.then_inc(turned, 1)
                pe.wait_ge(yqT_out, 2 * CB)
                for b in range(B):
                    for c in range(CB):
                        t = pe.matmul(banks[4 + b // 2][:, C * (b % 2):C * (b % 2 + 1)], yqT[:, c, P * b:P * (b + 1)],
                                      w_qT[:, 1, c, :], start=(c == 0), stop=(c == CB - 1))
                    t.then_inc(r_made, 1)

            @block.gpsimd
            def _(pool):
                pool.memset(ones[:, :], 1.0).then_inc(ones_set, 1)
                for i in range(2):
                    pool.memset(vz[i][:, :, :], 0.0).then_inc(vz_set, 1)
                pool.wait_ge(consts_in, 48)

                def heads(f, par):
                    wait_past(pool, s_made, 4 * (f - 1))
                    for c in range(CB):
                        pool.tensor_tensor(kz[par][:, HPB * c:HPB * (c + 1), :],
                                           k.keys1[:, c:c + 1, bass.ds(f * P, P)].to_broadcast([P, HPB, P]),
                                           head_mask[:, :].unsqueeze(2).to_broadcast([P, HPB, P]), ALU.mult).then_inc(kz_done, 1)

                def slots(f, par):
                    wait_past(pool, s_made, GROUPS * (f - 1))
                    pool.tensor_copy(qb[par][:, :, :], q1T[:, :, bass.ds(f * P, P)]).then_inc(qb_done, 1)
                    wait_past(pool, o_made, GROUPS * (f - 1))
                    pool.tensor_copy(vz[par][:, :, :].rearrange("p c (j x) -> p c j x", x=STRIDE)[:, :, :, 0:HD1],
                                     k.vals1[:, bass.ds(f, 1), :].rearrange("p o (c j d) -> p (o c) j d", c=CB, d=HD1)).then_inc(vz_done, 1)

                heads(0, 0)
                pool.wait_ge(vz_set, 2)
                pool.wait_ge(qT_out, 4)
                slots(0, 0)

                def step(it, par, last):
                    if not last:
                        heads(it + 1, 1 - par)
                        slots(it + 1, 1 - par)

                sequences(pool, step)

            @block.vector
            def _(dve):
                for b in range(B):
                    dve.bn_stats(stats[:, b, :], k.x1[:, b, :]).then_inc(stats_done, 1)
                for b in range(B):
                    dve.wait_ge(stats_done, b + 1)
                    dve.bn_aggr(mv[:, b, :], stats[:, b, :]).then_inc(var_done, 1)
                dve.wait_ge(w_in, 32)
                flat_w = w[:, :, :, :].rearrange("p i o c -> p (i o) c")
                dve.tensor_reduce(w_top[:, :], flat_w, AX.X, ALU.max, apply_absolute_value=True).then_inc(w_step_done, 1)
                dve.wait_ge(w_step_done, 1)
                dve.tensor_scalar(w_step[:, :], w_top[:, :], 1.0 / QMAX, QEPS, ALU.mult, ALU.max).then_inc(w_step_done, 1)
                dve.wait_ge(w_step_done, 2)
                dve.reciprocal(w_inv[:, :], w_step[:, :]).then_inc(w_step_done, 1)
                dve.wait_ge(w_step_done, 3)
                for n in range(2 * CB):
                    dve.tensor_scalar(flat_w[:, n, :], flat_w[:, n, :], w_inv[:, n:n + 1], QMAX, ALU.mult, ALU.min).then_inc(w_step_done, 1)
                dve.wait_ge(w_step_done, 3 + 2 * CB)
                dve.tensor_scalar(flat_w, flat_w, -QMAX, MAGIC, ALU.max, ALU.add).then_inc(w_step_done, 1)
                dve.wait_ge(w_step_done, 4 + 2 * CB)
                dve.tensor_scalar(w_q[:, :, :, :].rearrange("p i o c -> p (i o) c"), flat_w, MAGIC, None, ALU.subtract).then_inc(w_q_done, 1)
                for n in range(2 * CB):
                    dve.tensor_scalar(w_diag[:, n, :], k.ident[:, :], w_step[:, n:n + 1], None, ALU.mult).then_inc(w_diag_done, 1)
                for h in range(2):
                    dve.wait_ge(sd_done, h + 1)
                    dve.reciprocal(rstd[:, HB * h:HB * (h + 1)], sd[:, HB * h:HB * (h + 1)]).then_inc(rstd_done, 1)
                for h in range(2):
                    dve.wait_ge(rstd_done, h + 1)
                    for b in range(HB * h, HB * (h + 1)):
                        dve.tensor_scalar(y[:, b, :], k.x1[:, b, :], mv[:, b, 0:1], rstd[:, b:b + 1],
                                          ALU.subtract, ALU.mult).then_inc(y_done, 1)
                dve.wait_ge(y_done, B)
                row_steps(dve, y, 0)
                quantise(dve, y, yq, 0)
                dve.wait_ge(row_out, 1)
                dve.wait_ge(consts_in, 48)
                dve.wait_ge(yq_done, 1)
                for b in range(B):
                    dve.wait_ge(q_made, b - b % 2 + 2)
                    acc = banks[4 + b // 2][:, C * (b % 2):C * (b % 2 + 1)]
                    dve.scalar_tensor_tensor(y[:, b, :], acc, step_x[:, 0, b:b + 1], step_row[:, 0, :], ALU.mult, ALU.mult).then_inc(q_scaled, 1)
                    dve.wait_ge(q_scaled, b + 1)
                    dve.tensor_tensor(y[:, b, :], y[:, b, :], bias_row[:, 0, :], ALU.add).then_inc(q_done, 1)
                dve.wait_ge(mask_in, 16)

                def add_mask(it, par, g):
                    dve.wait_ge(s_made, GROUPS * it + g + 1)
                    wait_past(dve, exp_done, H1 * (it - 1) + HG * (g + 1))
                    dve.scalar_tensor_tensor(sm[g][:, :, :], banks[g % 2][:, :].rearrange("p (h s) -> p h s", h=HG), HD1 ** -0.5,
                                             mask[:, bass.ds(it, 1), :].to_broadcast([P, HG, P]), ALU.mult, ALU.add).then_inc(sm_done, 1)
                    dve.wait_ge(sm_done, GROUPS * it + g + 1)
                    dve.tensor_reduce(negmax[:, par, HG * g:HG * (g + 1)], sm[g][:, :, :], AX.X, ALU.max, negate=True).then_inc(max_done, 1)

                def pT_copy(it, g):
                    dve.wait_ge(pT_made, GROUPS * it + g + 1)
                    wait_past(dve, o_made, GROUPS * (it - 1) + g + 1)
                    dve.tensor_copy(pT[g][:, :, :], banks[2 + g % 2][:, :].rearrange("p (h s) -> p h s", h=HG)).then_inc(pT_out, 1)

                def row_sums(it, par):
                    dve.wait_ge(exp_done, H1 * (it + 1))
                    dve.reciprocal(rinv[:, par, :], rsum[:, par, :]).then_inc(rinv_done, 1)

                def normalise(it, par):
                    dve.wait_ge(rinv_done, it + 1)
                    dve.wait_ge(o_made, GROUPS * (it + 1))
                    dve.tensor_tensor(y[:, bass.ds(it, 1), :].rearrange("p o (h d) -> p (o h) d", d=HD1),
                                      banks[4 + par][:, 0:C].rearrange("p (h d) -> p h d", d=HD1),
                                      rinv[:, par, :].unsqueeze(2).to_broadcast([P, H1, HD1]), ALU.mult).then_inc(o_out, 1)

                dve.wait_ge(qT_made, 4)
                add_mask(0, 0, 0)
                add_mask(0, 0, 1)

                def step(it, par, last):
                    for g in range(GROUPS):
                        if g < GROUPS - 2:
                            add_mask(it, par, g + 2)
                        elif not last:
                            add_mask(it + 1, 1 - par, g + 2 - GROUPS)
                        if g == 1 and not (isinstance(it, int) and it == 0):
                            normalise(it - 1, 1 - par)
                        pT_copy(it, g)
                    row_sums(it, par)

                sequences(dve, step)
                normalise(B - 1, 1)
                dve.wait_ge(o_out, B)
                row_steps(dve, y, 1)
                quantise(dve, y, yq, 1)
                for b in range(B):
                    dve.wait_ge(r_made, b - b % 2 + 2)
                    acc = banks[4 + b // 2][:, C * (b % 2):C * (b % 2 + 1)]
                    dve.scalar_tensor_tensor(y[:, b, :], acc, step_x[:, 1, b:b + 1], step_row[:, 1, :], ALU.mult, ALU.mult).then_inc(r_step, 1)
                    dve.tensor_tensor(k.x1[:, b, :], k.x1[:, b, :], bias_row[:, 1, :], ALU.add).then_inc(r_step, 1)
                    dve.wait_ge(r_step, 2 * (b + 1))
                    dve.tensor_tensor(k.x1[:, b, :], k.x1[:, b, :], y[:, b, :], ALU.add).then_inc(x3_done, 1)
E1, I1, K1 = 32, 96, 8
TAU = 0.05
FEW = 1e-12
BLOCKS = E1 * I1 // P


def experts1_stage(nc, k, io):
    with Memory(nc) as m:
        stats, mv = m.sb("e_stats", [P, B, 6]), m.sb("e_mean_var", [P, B, 2])
        sd, rstd = m.sb("e_sd", [P, B]), m.sb("e_rstd", [P, B])
        y, yT = m.sb("e_y", [P, B, C]), m.sb("e_yT", [P, CB, T])
        gate_w = m.sb("e_gate_w", [P, CB, E1])
        iota = m.sb("e_iota", [P, E1])
        alpha = m.sb("alpha", [P, 1])
        probs = m.sb("e_probs", [P, B, E1])
        row = {n: m.sb("e_row_" + n, [P, B]) for n in ("max", "sum", "inv", "topsum", "topinv", "best", "idle", "first", "wsum", "winv")}
        top, top_i, top_f = m.sb("e_top", [P, B, K1]), m.sb("e_top_i", [P, B, K1], u32), m.sb("e_top_f", [P, B, K1])
        scaled, active, is_best = m.sb("scaled", [P, B, K1]), m.sb("active", [P, B, K1]), m.sb("is_best", [P, B, K1])
        where, fallback = m.sb("where", [P, B, K1]), m.sb("fallback", [P, B, K1])
        weight = m.sb("weight", [P, B, K1])
        spread = m.sb("spread", [P, B, E1, K1])
        combine = m.sb("combine", [P, B, E1])
        combine2 = m.sb("combine2", [P, B, 2, E1], f32r)
        cT = m.sb("cT", [2 * E1, T], f32r)
        yT_hi, yT_lo = m.sb("e_yT_hi", [P, CB, T], f32r), m.sb("e_yT_lo", [P, CB, T], f32r)
        pack = [m.sb(f"pack{i}", [P, PACK + P]) for i in range(2)]
        w_hi = [m.sb(f"e_w_hi{i}", [P, PACK + P], f32r) for i in range(2)]
        w_lo = [m.sb(f"e_w_lo{i}", [P, PACK], f32r) for i in range(2)]
        silu = [m.sb(f"e_silu{i}", [P, 512]) for i in range(2)]
        gated = [m.sb(f"e_gated{i}", [P, 512]) for i in range(2)]
        hid = [m.sb(f"e_hid{i}", [P, 512]) for i in range(2)]
        h_hi = [m.sb(f"e_h_hi{i}", [P, 512], f32r) for i in range(2)]
        h_lo = [m.sb(f"e_h_lo{i}", [P, 512], f32r) for i in range(2)]
        ring = [m.ps(f"e_ring{i}", [P, 512]) for i in range(4)]
        acc = [m.ps(f"e_acc{i}", [P, 2, C]) for i in range(4)]

        s = lambda name: m.sem("e_" + name)
        consts_in, gate_in = s("consts_in"), s("gate_in")
        stats_done, var_done, sd_done, rstd_done, y_done = s("stats"), s("var"), s("sd"), s("rstd"), s("y")
        turned, yT_out, logits_made, route, exp_done = s("turned"), s("yT_out"), s("logits"), s("route"), s("exp")
        yT_split, c_split, c_turned, cT_out = s("yT_split"), s("c_split"), s("c_turned"), s("cT_out")
        w_in = [s(f"w_in{i}") for i in range(2)]
        w_hi_done, w_lo_done = s("w_hi"), s("w_lo")
        made, silu_done, gated_done, hid_done, hi_done, lo_done = s("made"), s("silu"), s("gated"), s("hid"), s("h_hi"), s("h_lo")
        added, x_done, out_done = s("added"), s("x_out"), s("out_done")

        def blocks(eng, step):
            step(0, 0)
            step(1, 1)
            with eng.Fori(1, BLOCKS // 2) as i:
                step(2 * i, 0)
                step(2 * i + 1, 1)

        def blocks_but_last(eng, step):
            step(0, 0)
            step(1, 1)
            with eng.Fori(1, BLOCKS // 2 - 1) as i:
                step(2 * i, 0)
                step(2 * i + 1, 1)
            step(BLOCKS - 2, 0)
            step(BLOCKS - 1, 1)

        def bank(par, h, what):
            return ring[(3 * (2 * par + h) + what) % 4]

        with nc.Block() as block:

            @block.sync
            def _(sp):
                sp.dma_start(gate_w[:, :, :], io["gate_w1"].rearrange("(cb p) e -> p cb e", p=P)).then_inc(gate_in, 16)
                sp.dma_start(iota[:, :], io["iota"]).then_inc(consts_in, 16)
                sp.dma_start(alpha[:, :], io["alpha"]).then_inc(consts_in, 16)

                def load(blk, par):
                    wait_past(sp, w_lo_done, blk - 1)
                    sp.dma_start(pack[par][:, :], io["pack"][bass.ds(blk, 1), :, :].rearrange("o p n -> (o p) n")).then_inc(w_in[par], 16)

                blocks(sp, load)
                for j in range(4):
                    sp.wait_ge(x_done, j + 1)
                    sp.dma_start(io["out"][2 * j:2 * j + 2].rearrange("b s c -> s b c"), k.x1[:, 2 * j:2 * j + 2, :]).then_inc(out_done, 16)
                sp.wait_ge(out_done, 64)

            @block.scalar
            def _(act):
                for h in range(2):
                    act.wait_ge(var_done, HB * (h + 1))
                    act.activation(sd[:, HB * h:HB * (h + 1)], mv[:, HB * h:HB * (h + 1), 1], ACT.Sqrt,
                                   bias=k.eps[:, 0:1]).then_inc(sd_done, 1)
                for h in range(2):
                    for c in range(CB):
                        n = CB * h + c
                        act.wait_ge(turned, n + 1)
                        act.activation(yT[:, c, 512 * h:512 * (h + 1)], ring[n][:, :], ACT.Copy).then_inc(yT_out, 1)
                act.wait_ge(route, 2)
                act.activation(probs[:, :, :], probs[:, :, :], ACT.Exp).then_inc(exp_done, 1)

                act.wait_ge(c_turned, 2)
                for h in range(2):
                    act.activation(cT[:, 512 * h:512 * (h + 1)], acc[h][0:2 * E1, :, :].rearrange("p r c -> p (r c)"), ACT.Copy)\
                        .then_inc(cT_out, 1)

                def work(blk, par):
                    for h in range(2):
                        n = 2 * blk + h
                        act.wait_ge(made, 3 * n + 1)
                        wait_past(act, gated_done, n - 1)
                        act.activation(silu[h][:, :], bank(par, h, 0)[:, :], ACT.Silu).then_inc(silu_done, 1)

                blocks(act, work)

            @block.tensor
            def _(pe):
                for h in range(2):
                    pe.wait_ge(y_done, HB * (h + 1))
                    for c in range(CB):
                        for b in range(HB):
                            t = pe.transpose(ring[CB * h + c][:, P * b:P * (b + 1)], y[:, HB * h + b, P * c:P * (c + 1)], k.ident[:, :])
                        t.then_inc(turned, 1)
                pe.wait_ge(gate_in, 16)
                pe.wait_ge(yT_out, 2 * CB)
                for b in range(B):
                    for c in range(CB):
                        t = pe.matmul(acc[3][:, 0, E1 * b:E1 * (b + 1)], yT[:, c, P * b:P * (b + 1)], gate_w[:, c, :],
                                      start=(c == 0), stop=(c == CB - 1))
                t.then_inc(logits_made, 1)

                pe.wait_ge(c_split, 2)
                for h in range(2):
                    for b in range(HB):
                        t = pe.transpose(acc[h][0:2 * E1, :, :].rearrange("p r c -> p (r c)")[:, P * b:P * (b + 1)],
                                         combine2[:, HB * h + b, :, :].rearrange("p i e -> p (i e)").bitcast(fp32), k.ident[:, :])
                    t.then_inc(c_turned, 1)

                def up(blk, par, h):
                    n = 2 * blk + h
                    if isinstance(blk, int) and n == 0:
                        pe.wait_ge(yT_split, 4)
                    if h == 0:
                        pe.wait_ge(w_lo_done, blk + 1)
                    for what in range(2):
                        wait_past(pe, silu_done if what else hid_done, n if what else n - 1)
                        for c in range(CB):
                            cols, tokens = slice(P * (2 * what + c), P * (2 * what + c + 1)), slice(512 * h, 512 * (h + 1))
                            t = products(pe, bank(par, h, what)[:, :], (w_hi[par][:, cols], w_lo[par][:, cols]),
                                         (yT_hi[:, c, tokens], yT_lo[:, c, tokens]), c == 0, c == CB - 1)
                        t.then_inc(made, 1)
                    if isinstance(blk, int) and n == 0:
                        pe.wait_ge(cT_out, 2)
                    wait_past(pe, gated_done, n)
                    pe.matmul(bank(par, h, 2)[:, :], w_hi[par][0:2 * E1, PACK:PACK + P], cT[:, 512 * h:512 * (h + 1)],
                              start=True, stop=True).then_inc(made, 1)

                def down(blk, par, h, first, last):
                    n = 2 * blk + h
                    pe.wait_ge(lo_done, n + 1)
                    for j in range(HB):
                        rows = slice(P * j, P * (j + 1))
                        t = products(pe, acc[2 * h + j // 2][:, j % 2, :], (h_hi[h][:, rows], h_lo[h][:, rows]),
                                     (w_hi[par][:, 4 * P:PACK], w_lo[par][:, 4 * P:PACK]),
                                     first and j % 2 == 0, last and j % 2 == 1)
                    t.then_inc(added, 1)

                up(0, 0, 0)
                up(0, 0, 1)
                down(0, 0, 0, True, False)
                up(1, 1, 0)
                down(0, 0, 1, True, False)
                up(1, 1, 1)
                down(1, 1, 0, False, False)
                with pe.Fori(1, BLOCKS // 2) as i:
                    up(2 * i, 0, 0)
                    down(2 * i - 1, 1, 1, False, False)
                    up(2 * i, 0, 1)
                    down(2 * i, 0, 0, False, False)
                    up(2 * i + 1, 1, 0)
                    down(2 * i, 0, 1, False, False)
                    up(2 * i + 1, 1, 1)
                    down(2 * i + 1, 1, 0, False, False)
                down(BLOCKS - 1, 1, 1, False, True)

            @block.gpsimd
            def _(pool):
                def split_w(blk, par):
                    pool.wait_ge(w_hi_done, blk + 1)
                    low(pool, w_lo[par][:, :], pack[par][:, 0:PACK], w_hi[par][:, 0:PACK]).then_inc(w_lo_done, 1)

                split_w(0, 0)
                pool.wait_ge(yT_split, 2)
                low(pool, yT_lo[:, 1, :], yT[:, 1, :], yT_hi[:, 1, :]).then_inc(yT_split, 1)

                def work(blk, par):
                    for h in range(2):
                        n = 2 * blk + h
                        pool.wait_ge(hi_done, n + 1)
                        low(pool, h_lo[h][:, :], hid[h][:, :], h_hi[h][:, :]).then_inc(lo_done, 1)
                        if h == 0 and not (isinstance(blk, int) and blk == BLOCKS - 1):
                            split_w(blk + 1, 1 - par)

                blocks_but_last(pool, work)

            @block.vector
            def _(dve):
                for b in range(B):
                    dve.bn_stats(stats[:, b, :], k.x1[:, b, :]).then_inc(stats_done, 1)
                for b in range(B):
                    dve.wait_ge(stats_done, b + 1)
                    dve.bn_aggr(mv[:, b, :], stats[:, b, :]).then_inc(var_done, 1)
                for h in range(2):
                    dve.wait_ge(sd_done, h + 1)
                    dve.reciprocal(rstd[:, HB * h:HB * (h + 1)], sd[:, HB * h:HB * (h + 1)]).then_inc(rstd_done, 1)
                    dve.wait_ge(rstd_done, h + 1)
                    for b in range(HB * h, HB * (h + 1)):
                        dve.tensor_scalar(y[:, b, :], k.x1[:, b, :], mv[:, b, 0:1], rstd[:, b:b + 1],
                                          ALU.subtract, ALU.mult).then_inc(y_done, 1)

                def split_w(blk, par):
                    dve.wait_ge(w_in[par], 16 * earlier(blk, par) + 16)
                    wait_past(dve, added, 2 * (blk - 1))
                    dve.tensor_copy(w_hi[par][:, :], pack[par][:, :]).then_inc(w_hi_done, 1)

                split_w(0, 0)
                for c in range(CB):
                    dve.wait_ge(yT_out, 2 + c + 1)
                    dve.tensor_copy(yT_hi[:, c, :], yT[:, c, :]).then_inc(yT_split, 1)
                dve.wait_ge(yT_split, 2)
                low(dve, yT_lo[:, 0, :], yT[:, 0, :], yT_hi[:, 0, :]).then_inc(yT_split, 1)
                count = [0]

                def then(t):
                    t.then_inc(route, 1)
                    count[0] += 1
                    dve.wait_ge(route, count[0])

                wide = lambda a, n: a[:, :].unsqueeze(2).to_broadcast([P, B, n])
                dve.wait_ge(logits_made, 1)
                logits = acc[3][:, 0, :].rearrange("p (b e) -> p b e", b=B)
                dve.tensor_reduce(row["max"][:, :], logits, AX.X, ALU.max).then_inc(y_done, 1)
                dve.wait_ge(y_done, B + 1)
                then(dve.tensor_tensor(probs[:, :, :], logits, wide(row["max"], E1), ALU.subtract))
                dve.wait_ge(consts_in, 32)
                then(dve.tensor_copy(row["first"][:, :], row["max"][:, :]))
                dve.wait_ge(exp_done, 1)
                then(dve.tensor_reduce(row["sum"][:, :], probs[:, :, :], AX.X, ALU.add))
                then(dve.reciprocal(row["inv"][:, :], row["sum"][:, :]))
                then(dve.tensor_tensor(probs[:, :, :], probs[:, :, :], wide(row["inv"], E1), ALU.mult))
                for b in range(B):
                    t = dve.max(top[:, b, :], probs[:, b, :])
                then(t)
                for b in range(B):
                    t = dve.max_index(top_i[:, b, :], top[:, b, :], probs[:, b, :])
                then(t)
                then(dve.tensor_copy(top_f[:, :, :], top_i[:, :, :]))
                then(dve.tensor_reduce(row["topsum"][:, :], top[:, :, :], AX.X, ALU.add))
                then(dve.tensor_scalar(row["topsum"][:, :], row["topsum"][:, :], FEW, None, ALU.max))
                then(dve.reciprocal(row["topinv"][:, :], row["topsum"][:, :]))
                then(dve.tensor_tensor(top[:, :, :], top[:, :, :], wide(row["topinv"], K1), ALU.mult))
                then(dve.tensor_scalar(scaled[:, :, :], top[:, :, :], alpha[:, 0:1], None, ALU.mult))
                then(dve.tensor_scalar(active[:, :, :], scaled[:, :, :], TAU, None, ALU.is_ge))
                then(dve.tensor_reduce(row["best"][:, :], scaled[:, :, :], AX.X, ALU.max))
                then(dve.tensor_tensor(is_best[:, :, :], scaled[:, :, :], wide(row["best"], K1), ALU.is_equal))
                then(dve.scalar_tensor_tensor(where[:, :, :], is_best[:, :, :], -100.0,
                                              iota[:, 0:K1].unsqueeze(1).to_broadcast([P, B, K1]), ALU.mult, ALU.add))
                then(dve.tensor_reduce(row["first"][:, :], where[:, :, :], AX.X, ALU.min))
                then(dve.tensor_tensor(fallback[:, :, :], where[:, :, :], wide(row["first"], K1), ALU.is_equal))
                then(dve.tensor_reduce(row["idle"][:, :], active[:, :, :], AX.X, ALU.max))
                then(dve.tensor_scalar(row["idle"][:, :], row["idle"][:, :], -1.0, 1.0, ALU.mult, ALU.add))
                then(dve.tensor_tensor(fallback[:, :, :], fallback[:, :, :], wide(row["idle"], K1), ALU.mult))
                then(dve.tensor_tensor(active[:, :, :], active[:, :, :], fallback[:, :, :], ALU.max))
                then(dve.tensor_tensor(weight[:, :, :], top[:, :, :], active[:, :, :], ALU.mult))
                then(dve.tensor_reduce(row["wsum"][:, :], weight[:, :, :], AX.X, ALU.add))
                then(dve.tensor_scalar(row["wsum"][:, :], row["wsum"][:, :], FEW, None, ALU.max))
                then(dve.reciprocal(row["winv"][:, :], row["wsum"][:, :]))
                then(dve.tensor_tensor(weight[:, :, :], weight[:, :, :], wide(row["winv"], K1), ALU.mult))
                for b in range(B):
                    t = dve.tensor_tensor(spread[:, b, :, :], iota[:, :].unsqueeze(2).to_broadcast([P, E1, K1]),
                                          top_f[:, b:b + 1, :].to_broadcast([P, E1, K1]), ALU.is_equal)
                then(t)
                for b in range(B):
                    t = dve.tensor_tensor(spread[:, b, :, :], spread[:, b, :, :], weight[:, b:b + 1, :].to_broadcast([P, E1, K1]), ALU.mult)
                then(t)
                then(dve.tensor_reduce(combine[:, :, :].rearrange("p b e -> p (b e)"),
                                       spread[:, :, :, :].rearrange("p b e k -> p (b e) k"), AX.X, ALU.add))

                then(dve.tensor_copy(combine2[:, :, 0, :], combine[:, :, :]))
                low(dve, combine2[:, :, 1, :], combine[:, :, :], combine2[:, :, 0, :]).then_inc(c_split, 2)

                def work(blk, par):
                    for h in range(2):
                        n = 2 * blk + h
                        dve.wait_ge(silu_done, n + 1)
                        dve.wait_ge(made, 3 * n + 2)
                        dve.tensor_tensor(gated[h][:, :], bank(par, h, 1)[:, :], silu[h][:, :], ALU.mult).then_inc(gated_done, 1)
                        dve.wait_ge(made, 3 * n + 3)
                        dve.wait_ge(gated_done, n + 1)
                        wait_past(dve, lo_done, n - 1)
                        dve.tensor_tensor(hid[h][:, :], bank(par, h, 2)[:, :], gated[h][:, :], ALU.mult).then_inc(hid_done, 1)
                        dve.wait_ge(hid_done, n + 1)
                        wait_past(dve, added, n - 1)
                        dve.tensor_copy(h_hi[h][:, :], hid[h][:, :]).then_inc(hi_done, 1)
                        if h == 0 and not (isinstance(blk, int) and blk == BLOCKS - 1):
                            split_w(blk + 1, 1 - par)

                blocks_but_last(dve, work)
                dve.wait_ge(added, 2 * BLOCKS)
                for j in range(4):
                    dve.tensor_tensor(k.x1[:, 2 * j:2 * j + 2, :], k.x1[:, 2 * j:2 * j + 2, :], acc[j][:, :, :], ALU.add).then_inc(x_done, 1)
class Kept:

    def __init__(self, m):
        self.x1 = m.sb("x1", [P, B, C])
        self.z = m.sb("z", [P, B, C])
        self.xa = m.sb("xa", [P, B, C])
        self.keys1 = m.sb("keys1", [P, CB, T])
        self.vals1 = m.sb("vals1", [P, B, C])
        self.ident = m.sb("ident", [P, P])
        self.eps = m.sb("eps", [P, 1])


def build_program(nc, io):
    with Memory(nc) as m:
        kept = Kept(m)
        wkv_stage(nc, kept, io)
        attention_stage(nc, kept, io)
        experts0_stage(nc, kept, io)
        cross_stage(nc, kept, io)
        experts1_stage(nc, kept, io)


def rope_tables(np):
    f = np.float32
    freq = (f(1e6) ** (-np.arange(0, HD0, 2, dtype=f) / f(HD0))).astype(f)
    angle = np.arange(P, dtype=f)[:, None] * freq[None]
    cos, sin = np.cos(angle), np.sin(angle)
    cos, sin = np.concatenate([cos, cos], 1), np.concatenate([-sin, sin], 1)
    scale = f(HD0 ** -0.5)
    return np.stack([cos * scale, sin * scale, cos, sin], 1).astype(f)


def weights0(np, w1, w3, w2):
    columns = lambda w: w.reshape(E0, CB, P, FB, P).transpose(0, 2, 3, 1, 4).reshape(E0, P, FB, CB * P)
    down = w2.reshape(E0, FB, P, C).transpose(0, 2, 1, 3)
    return np.concatenate([columns(w1), columns(w3), down], 3).reshape(E0, P, FB * PACK)


def weights1(np, gate_up, down):
    gate = gate_up[:, :I1].reshape(BLOCKS, P, CB, P).transpose(0, 3, 2, 1).reshape(BLOCKS, P, CB * P)
    up = gate_up[:, I1:].reshape(BLOCKS, P, CB, P).transpose(0, 3, 2, 1).reshape(BLOCKS, P, CB * P)
    down = down.transpose(0, 2, 1).reshape(BLOCKS, P, C)
    expert = np.arange(BLOCKS * P).reshape(BLOCKS, 1, P) // I1
    one = (expert == np.arange(P)[None, :, None] % E1).astype(np.float32)
    return dict(pack=np.concatenate([gate, up, down, one], 2))


def kernel(**inputs):
    import ml_dtypes
    import numpy as np
    import concourse.bacc as bacc
    from concourse.bass_utils import run_bass_kernel_spmd

    a = {n: np.asarray(v) for n, v in inputs.items()}
    half = ml_dtypes.bfloat16
    column = lambda v: v.reshape(CB, P).T
    rows = lambda v: np.broadcast_to(v, (P,) + v.shape)
    pairs_apart = lambda w, h: w.reshape(C, h, HD0 // 2, 2).transpose(0, 1, 3, 2).reshape(C, h * HD0)
    visible = np.tril(np.ones((P, P), bool))
    arrays = dict(
        x=a["x"], ctxT=a["ctx_2048"].transpose(2, 0, 1),
        wkv_cols=np.stack([column(a[n]) for n in ("L0_xattn_w", "L0_xattn_u", "L1_xattn_bk")], 1),
        wk1T=a["L1_xattn_wk"].T, wv1T=a["L1_xattn_wv"].T, bv1=rows(a["L1_xattn_bv"]),
        ln_w=column(a["L0_ffn_ln_w"]),
        wq0=pairs_apart(a["L0_ffn_wq"], H0), wk0=pairs_apart(a["L0_ffn_wk"], KV0), wv0=a["L0_ffn_wv"], wo0=a["L0_ffn_wo"],
        ff_w=rows(a["L0_ffn_ff_ln_w"]), gate_w0=a["L0_ffn_gate_w"], pack0=weights0(np, a["L0_ffn_w1"], a["L0_ffn_w3"], a["L0_ffn_w2"]),
        wq1=a["L1_xattn_wq"], wo1=a["L1_xattn_wo"], bias_row=rows(np.stack([a["L1_xattn_bq"], a["L1_xattn_bo"]])),
        mask=a["mask_BxSxS2_ff0"],
        gate_w1=a["L1_ffn_gate_weight"].T, alpha=rows(a["L1_ffn_layer_alpha"].reshape(1)),
        **weights1(np, a["L1_ffn_gate_up_proj"], a["L1_ffn_down_proj"]),
        ident=np.eye(P, dtype=np.float32), identb=np.eye(P).astype(half), rope=rope_tables(np),
        causal=np.broadcast_to(np.where(visible, 0, -1e30).astype(half)[:, None], (P, G0, P)),
        iota=rows(np.arange(E1, dtype=np.float32)), before=(~visible).astype(half), ones=np.ones((P, P), half),
        head_mask=(np.arange(P)[:, None] // HD1 == np.arange(HPB)[None]).astype(np.float32),
    )
    nc = bacc.Bacc("TRN2", target_bir_lowering=False, num_devices=1)
    feed, io = {}, {}
    for name, value in arrays.items():
        value = np.ascontiguousarray(value)
        feed[f"in_{name}"] = value
        io[name] = nc.dram_tensor(f"in_{name}", value.shape, mybir.dt.from_np(value.dtype), kind="ExternalInput").ap()
    io["out"] = nc.dram_tensor("out_x", (B, P, C), fp32, kind="ExternalOutput").ap()
    build_program(nc, io)
    result = run_bass_kernel_spmd(nc, [feed], core_ids=[0])
    return result.results[0]["out_x"]
```

```python
from contextlib import ExitStack

import concourse.bass as bass
from concourse import mybir
from concourse.alu_op_type import AluOpType as ALU

fp32 = mybir.dt.float32
bf16 = mybir.dt.bfloat16
f32r = mybir.dt.float32r
u32 = mybir.dt.uint32
ACT = mybir.ActivationFunctionType
AX = mybir.AxisListType

P = 128
B = 8
C = 256
CB = C // P
T = B * P
HB = B // 2
PAD = P + 1
NEG = -1e38
LN_EPS = 1e-5


class Memory:

    def __init__(self, nc):
        self.nc, self.stack, self.sems = nc, ExitStack(), []

    def __enter__(self):
        self.stack.__enter__()
        return self

    def __exit__(self, *a):
        if a[0] is None and self.sems:
            runs = []
            for n in sorted(s.num for s in self.sems):
                if runs and runs[-1][1] == n:
                    runs[-1][1] = n + 1
                else:
                    runs.append([n, n + 1])
            with self.nc.Block() as block:

                @block.gpsimd
                def _(pool):
                    for first, end in runs:
                        pool.sem_clear(range(first, end))

        return self.stack.__exit__(*a)

    def sb(self, name, shape, dt=fp32):
        return self.stack.enter_context(self.nc.sbuf_tensor(name, shape, dt))

    def ps(self, name, shape, dt=fp32):
        return self.stack.enter_context(self.nc.psum_tensor(name, shape, dt))

    def sem(self, name):
        self.sems.append(self.stack.enter_context(self.nc.semaphore(name)))
        return self.sems[-1]


def wait_past(eng, sem, n):
    if not isinstance(n, int) or n > 0:
        eng.wait_ge(sem, n)


def low(eng, out, x, high):
    return eng.tensor_tensor(out, x, high.bitcast(fp32), ALU.subtract)


def products(pe, out, stationary, moving, first, last):
    (sh, sl), (mh, ml) = stationary, moving
    pe.matmul(out, sh, mh, start=first, stop=False, skip_group_check=True)
    pe.matmul(out, sh, ml, start=False, stop=False, skip_group_check=True)
    return pe.matmul(out, sl, mh, start=False, stop=last, skip_group_check=True)


def wkv_stage(nc, k, io):
    with Memory(nc) as m:
        ctxT = m.sb("ctxT", [P, CB, B, P])
        xn = m.sb("xn", [P, B, C])
        stats = m.sb("ln_stats", [P, B, 6])
        mv = m.sb("ln_mean_var", [P, B, 2])
        sd = m.sb("ln_sd", [P, B])
        rstd = m.sb("ln_rstd", [P, B])
        eps = k.eps
        wk1T = m.sb("wk1T", [P, CB, C])
        wv1T = m.sb("wv1T", [P, CB, C])
        bv1 = m.sb("bv1", [P, C])
        wkv_cols = m.sb("wkv_cols", [P, 3, CB])
        pad = lambda name: [m.sb(f"{name}{c}", [P, B, PAD]) for c in range(CB)]
        flat = lambda name: [m.sb(f"{name}{c}", [P, B, P]) for c in range(CB)]
        decay, kpad, omax = pad("decay"), pad("kpad"), pad("omax")
        qsum, psum = pad("qsum"), pad("psum_")
        a2, e2, ev2 = pad("a2_"), pad("e2_"), pad("ev2_")
        d2_, d1, a1, e1, ev1 = flat("d2_"), flat("d1_"), flat("a1_"), flat("e1_"), flat("ev1_")
        stage = [m.sb(f"a_stage{i}", [P, CHUNK]) for i in range(EARLY)]
        w_in, w_hi_done, w_lo_done = [m.sem(f"w_in{i}") for i in range(EARLY)], m.sem("w_hi_done"), m.sem("w_lo_done")
        kT_ps = m.ps("kT_ps", [P, CB, T])
        y_ps = m.ps("y_ps", [P, B, C])
        y_half = y_ps[:, :, :]

        x_in = [m.sem(f"x_in{h}") for h in range(2)]
        ctx_in, const_in, cols_in, w1_in = m.sem("ctx_in"), m.sem("const_in"), m.sem("cols_in"), m.sem("w1_in")
        eps_set, pads_set = m.sem("eps_set"), m.sem("pads_set")
        stats_done, var_done, sd_done, rstd_done = m.sem("stats_done"), m.sem("var_done"), m.sem("sd_done"), m.sem("rstd_done")
        xn_done, kT_done, kpad_done = m.sem("xn_done"), m.sem("kT_done"), m.sem("kpad_done")
        decay_done, omax_done, d2_done, d1_done = m.sem("decay_done"), m.sem("omax_done"), m.sem("d2_done"), m.sem("d1_done")
        relu_done, exp2_done, exp1_done = m.sem("relu_done"), m.sem("exp2_done"), m.sem("exp1_done")
        ev2_done, ev1_done, ap_done, aq_done = m.sem("ev2_done"), m.sem("ev1_done"), m.sem("ap_done"), m.sem("aq_done")
        qscan_done, pscan_done = m.sem("qscan_done"), m.sem("pscan_done")
        den_done, num_done, rden_done, yT_done = m.sem("den_done"), m.sem("num_done"), m.sem("rden_done"), m.sem("yT_done")
        den_log, first_inv = m.sem("den_log"), m.sem("first_inv")
        y_done, x1_done = m.sem("y_done"), m.sem("x1_done")
        keys_done, keys_out, vals_done, vals_raw, vals_out = m.sem("keys_done"), m.sem("keys_out"), m.sem("vals_done"), m.sem("vals_raw"), m.sem("vals_out")

        with nc.Block() as block:

            @block.sync
            def _(sp):
                for h in range(2):
                    sp.dma_start(k.x1[:, HB * h:HB * (h + 1), :],
                                 io["x"][HB * h:HB * (h + 1)].rearrange("b s c -> s b c")).then_inc(x_in[h], 16)
                sp.dma_start(k.ident[:, :], io["ident"]).then_inc(const_in, 16)
                for i in range(EARLY):
                    load_chunk(sp, io, stage[i], i).then_inc(w_in[i], 16)
                sp.dma_start(ctxT[:, :, :, :], io["ctxT"].rearrange("(cb p) b s -> p cb b s", p=P)).then_inc(ctx_in, 16)

            @block.scalar
            def _(act):
                act.dma_start(wkv_cols[:, :, :], io["wkv_cols"]).then_inc(cols_in, 16)
                act.dma_start(wk1T[:, :, :], io["wk1T"].rearrange("(cb p) o -> p cb o", p=P)).then_inc(w1_in, 16)
                act.dma_start(wv1T[:, :, :], io["wv1T"].rearrange("(cb p) o -> p cb o", p=P)).then_inc(w1_in, 16)
                act.dma_start(bv1[:, :], io["bv1"]).then_inc(w1_in, 16)
                def round_w(i):
                    act.wait_ge(w_in[i], 16)
                    act.activation(k.w0_hi[i][:, :], stage[i][:, :], ACT.Copy).then_inc(w_hi_done, 1)

                act.wait_ge(eps_set, 1)
                for h in range(2):
                    act.wait_ge(var_done, HB * (h + 1))
                    act.activation(sd[:, HB * h:HB * (h + 1)], mv[:, HB * h:HB * (h + 1), 1], ACT.Sqrt,
                                   bias=eps[:, 0:1]).then_inc(sd_done, 1)
                    if h == 0:
                        round_w(0)
                for c in range(CB):
                    for h in range(2):
                        act.wait_ge(kT_done, 2 * c + h + 1)
                        act.activation(kpad[c][:, HB * h:HB * (h + 1), 1:PAD],
                                       kT_ps[:, c, 512 * h:512 * (h + 1)].rearrange("p (b s) -> p b s", s=P),
                                       ACT.Copy).then_inc(kpad_done, 1)
                for i in range(1, EARLY):
                    round_w(i)
                relus = [0]

                def weights(d, pairs, done):
                    for out, sign in pairs:
                        act.activation(out, d, ACT.Relu, scale=sign).then_inc(relu_done, 1)
                    for out, sign in pairs:
                        relus[0] += 1
                        act.wait_ge(relu_done, relus[0])
                        act.activation(out, out, ACT.Exp, scale=-1.0).then_inc(done, 1)

                act.wait_ge(pads_set, 3 * CB)
                for c in range(CB):
                    act.wait_ge(d2_done, c + 1)
                    weights(d2_[c][:, :, :], ((e2[c][:, :, 1:PAD], 1.0), (a2[c][:, :, 1:PAD], -1.0)), exp2_done)
                for c in range(CB):
                    act.wait_ge(d1_done, c + 1)
                    weights(d1[c][:, :, :], ((a1[c][:, :, :], -1.0), (e1[c][:, :, :], 1.0)), exp1_done)
                act.wait_ge(cols_in, 16)

                def invert(c):
                    act.wait_ge(den_done, c + 1)
                    act.activation(d1[c][:, :, :], e1[c][:, :, :], ACT.Ln).then_inc(den_log, 1)
                    act.wait_ge(den_log, c + 1)
                    act.activation(d1[c][:, :, :], d1[c][:, :, :], ACT.Exp, scale=-1.0).then_inc(first_inv, 1)

                for ob in range(CB):
                    for h in range(2):
                        act.wait_ge(keys_done, 2 * ob + h + 1)
                        act.activation(k.keys1[:, ob, 512 * h:512 * (h + 1)], kT_ps[:, ob, 512 * h:512 * (h + 1)],
                                       ACT.Identity, bias=wkv_cols[:, 2, ob:ob + 1]).then_inc(keys_out, 1)
                for c in range(CB):
                    invert(c)
                for j in range(4):
                    act.wait_ge(vals_done, j + 1)
                    act.activation(k.vals1[:, 2 * j:2 * j + 2, :], y_ps[:, 2 * j:2 * j + 2, :], ACT.Copy).then_inc(vals_raw, 1)

            @block.tensor
            def _(pe):
                pe.wait_ge(const_in, 16)
                for c in range(CB):
                    for h in range(2):
                        for b in range(HB * h, HB * (h + 1)):
                            pe.wait_ge(xn_done, b + 1)
                            t = pe.transpose(kT_ps[:, c, P * b:P * (b + 1)], xn[:, b, P * c:P * (c + 1)], k.ident[:, :])
                        t.then_inc(kT_done, 1)
                pe.wait_ge(ctx_in, 16)
                pe.wait_ge(w1_in, 48)
                for b in range(B):
                    for c in range(CB):
                        t = pe.matmul(y_ps[:, b, :], ctxT[:, c, b, :], wv1T[:, c, :], start=(c == 0), stop=(c == CB - 1))
                    if b % 2:
                        t.then_inc(vals_done, 1)
                pe.wait_ge(kpad_done, 2 * CB)
                for ob in range(CB):
                    for h in range(2):
                        for c in range(CB):
                            t = pe.matmul(kT_ps[:, ob, 512 * h:512 * (h + 1)], wk1T[:, c, P * ob:P * (ob + 1)],
                                          ctxT[:, c, HB * h:HB * (h + 1), :], start=(c == 0), stop=(c == CB - 1))
                        t.then_inc(keys_done, 1)
                pe.wait_ge(vals_raw, 4)
                for c in range(CB):
                    pe.wait_ge(yT_done, c + 1)
                    for b in range(B):
                        t = pe.transpose(y_ps[:, b, P * c:P * (c + 1)], a1[c][:, b, :], k.ident[:, :])
                        if c == CB - 1 and b % 2:
                            t.then_inc(y_done, 1)

            @block.gpsimd
            def _(pool):
                for c in range(CB):
                    for buf in (a2[c], e2[c], ev2[c]):
                        pool.memset(buf[:, :, 0:1], 0.0).then_inc(pads_set, 1)
                for i in range(EARLY):
                    pool.wait_ge(w_hi_done, i + 1)
                    low(pool, k.w0_lo[i][:, :], stage[i][:, :], k.w0_hi[i][:, :]).then_inc(w_lo_done, 1)
                pool.wait_ge(ctx_in, 16)
                for c in range(CB):
                    pool.wait_ge(exp2_done, 2 * c + 1)
                    pool.tensor_tensor(ev2[c][:, :, 1:PAD], e2[c][:, :, 1:PAD], ctxT[:, c, :, :], ALU.mult).then_inc(ev2_done, 1)
                for c in range(CB):
                    pool.wait_ge(exp1_done, 2 * c + 1)
                    pool.wait_ge(qscan_done, c + 1)
                    pool.tensor_tensor(qsum[c][:, :, 0:P], qsum[c][:, :, 0:P], a1[c][:, :, :], ALU.mult).then_inc(aq_done, 1)
                    pool.wait_ge(exp1_done, 2 * c + 2)
                    pool.tensor_tensor(ev1[c][:, :, :], e1[c][:, :, :], ctxT[:, c, :, :], ALU.mult).then_inc(ev1_done, 1)
                pool.wait_ge(w1_in, 48)
                for b in range(B):
                    pool.wait_ge(vals_raw, b // 2 + 1)
                    pool.tensor_tensor(k.vals1[:, b, :], k.vals1[:, b, :], bv1[:, :], ALU.add).then_inc(vals_out, 1)

            @block.vector
            def _(dve):
                dve.memset(eps[:, :], LN_EPS).then_inc(eps_set, 1)
                for h in range(2):
                    dve.wait_ge(x_in[h], 16)
                    for b in range(HB * h, HB * (h + 1)):
                        dve.bn_stats(stats[:, b, :], k.x1[:, b, :]).then_inc(stats_done, 1)
                    for b in range(HB * h, HB * (h + 1)):
                        dve.wait_ge(stats_done, b + 1)
                        dve.bn_aggr(mv[:, b, :], stats[:, b, :]).then_inc(var_done, 1)
                    if h == 0:
                        dve.wait_ge(cols_in, 16)
                        for c in range(CB):
                            dve.memset(decay[c][:, :, 1:PAD], 0.0).then_inc(decay_done, 1)
                            dve.memset(decay[c][:, :, 0:1], NEG).then_inc(decay_done, 1)
                            dve.memset(kpad[c][:, :, 0:1], NEG).then_inc(decay_done, 1)
                            dve.wait_ge(decay_done, 4 * c + 1)
                            dve.tensor_scalar(decay[c][:, :, 1:PAD], decay[c][:, :, 1:PAD], wkv_cols[:, 0, c:c + 1], None,
                                              ALU.add).then_inc(decay_done, 1)
                for h in range(2):
                    dve.wait_ge(sd_done, h + 1)
                    dve.reciprocal(rstd[:, HB * h:HB * (h + 1)], sd[:, HB * h:HB * (h + 1)]).then_inc(rstd_done, 1)
                    dve.wait_ge(rstd_done, h + 1)
                    for b in range(HB * h, HB * (h + 1)):
                        dve.tensor_scalar(xn[:, b, :], k.x1[:, b, :], mv[:, b, 0:1], rstd[:, b:b + 1],
                                          ALU.subtract, ALU.mult).then_inc(xn_done, 1)
                for c in range(CB):
                    dve.wait_ge(kpad_done, 2 * c + 2)
                    dve.wait_ge(decay_done, 4 * c + 4)
                    dve.tensor_tensor_scan(omax[c][:, :, :].rearrange("p b s -> p (b s)"),
                                           decay[c][:, :, :].rearrange("p b s -> p (b s)"),
                                           kpad[c][:, :, :].rearrange("p b s -> p (b s)"),
                                           NEG, ALU.add, ALU.max).then_inc(omax_done, 1)
                    dve.wait_ge(omax_done, c + 1)
                    dve.scalar_tensor_tensor(d2_[c][:, :, :], omax[c][:, :, 0:P], wkv_cols[:, 0, c:c + 1],
                                             kpad[c][:, :, 1:PAD], ALU.add, ALU.subtract).then_inc(d2_done, 1)
                    dve.scalar_tensor_tensor(d1[c][:, :, :], omax[c][:, :, 0:P], wkv_cols[:, 1, c:c + 1],
                                             kpad[c][:, :, 1:PAD], ALU.subtract, ALU.subtract).then_inc(d1_done, 1)
                fl = lambda t, c: t[c][:, :, :].rearrange("p b s -> p (b s)")

                def q_scan(c):
                    dve.wait_ge(exp2_done, 2 * c + 2)
                    dve.wait_ge(pads_set, 3 * CB)
                    dve.tensor_tensor_scan(fl(qsum, c), fl(a2, c), fl(e2, c), 0.0, ALU.mult, ALU.add).then_inc(qscan_done, 1)

                def p_scan(c):
                    dve.wait_ge(ev2_done, c + 1)
                    dve.tensor_tensor_scan(fl(psum, c), fl(a2, c), fl(ev2, c), 0.0, ALU.mult, ALU.add).then_inc(pscan_done, 1)

                def denominator(c):
                    dve.wait_ge(aq_done, c + 1)
                    dve.wait_ge(exp1_done, 2 * c + 2)
                    dve.wait_ge(ev1_done, c + 1)
                    dve.tensor_tensor(e1[c][:, :, :], qsum[c][:, :, 0:P], e1[c][:, :, :], ALU.add).then_inc(den_done, 1)

                def weigh_state(c):
                    dve.wait_ge(pscan_done, c + 1)
                    dve.wait_ge(aq_done, c + 1)
                    dve.tensor_tensor(a1[c][:, :, :], psum[c][:, :, 0:P], a1[c][:, :, :], ALU.mult).then_inc(ap_done, 1)

                def numerator(c):
                    dve.wait_ge(ap_done, c + 1)
                    dve.wait_ge(ev1_done, c + 1)
                    dve.tensor_tensor(a1[c][:, :, :], a1[c][:, :, :], ev1[c][:, :, :], ALU.add).then_inc(num_done, 1)

                def residual(c):
                    dve.wait_ge(first_inv, c + 1)
                    dve.tensor_tensor(e1[c][:, :, :], e1[c][:, :, :], d1[c][:, :, :], ALU.mult).then_inc(rden_done, 1)

                def refine(c):
                    dve.wait_ge(rden_done, 2 * c + 1)
                    dve.scalar_tensor_tensor(e1[c][:, :, :], e1[c][:, :, :], 2.0, d1[c][:, :, :], ALU.subtract, ALU.mult).then_inc(rden_done, 1)

                def divide(c):
                    dve.wait_ge(num_done, c + 1)
                    dve.wait_ge(rden_done, 2 * c + 2)
                    dve.scalar_tensor_tensor(a1[c][:, :, :], a1[c][:, :, :], -1.0, e1[c][:, :, :], ALU.mult, ALU.mult).then_inc(yT_done, 1)

                for c in range(CB):
                    q_scan(c)
                    p_scan(c)
                weigh_state(0)
                denominator(0)
                numerator(0)
                weigh_state(1)
                denominator(1)
                numerator(1)
                residual(0)
                refine(0)
                divide(0)
                residual(1)
                refine(1)
                divide(1)
                for j in range(4):
                    dve.wait_ge(y_done, j + 1)
                    dve.tensor_tensor(k.x1[:, 2 * j:2 * j + 2, :], k.x1[:, 2 * j:2 * j + 2, :], y_ps[:, 2 * j:2 * j + 2, :],
                                      ALU.add).then_inc(x1_done, 1)
H0, KV0, HD0 = 16, 4, 128
G0 = H0 // KV0
WIDE = G0 * HD0
CHUNK = CB * WIDE

STAGES = 4
CHUNKS = 2 + H0 * HD0 // WIDE + H0 * HD0 // WIDE

EARLY = 3


def load_chunk(eng, io, out, i):
    if i < 6:
        name, at = ("wk0", 0) if i == 0 else ("wv0", 0) if i == 5 else ("wq0", WIDE * (i - 1))
        return eng.dma_start(out[:, :].rearrange("p (cb o) -> p cb o", cb=CB),
                             io[name][:, at:at + WIDE].rearrange("(cb p) o -> p cb o", p=P))
    return eng.dma_start(out[:, :].rearrange("p (h o) -> p h o", h=G0),
                         io["wo0"][WIDE * (i - 6):WIDE * (i - 5), :].rearrange("(h p) o -> p h o", p=P))


def attention_stage(nc, k, io):
    with Memory(nc) as m:
        stats, mv = m.sb("b_stats", [P, B, 6]), m.sb("b_mean_var", [P, B, 2])
        var_eps, rstd = m.sb("b_var_eps", [P, B]), m.sb("b_rstd", [P, B])
        mean_sq, rrms = m.sb("b_mean_sq", [P, B]), m.sb("b_rrms", [P, B])
        power = m.sb("b_power", [P, HB])
        stage = [m.sb(f"w_stage{i}", [P, CHUNK]) for i in range(STAGES)]
        w_hi = k.w0_hi + [m.sb(f"b_w_hi{i}", [P, CHUNK], f32r) for i in range(EARLY, CHUNKS)]
        w_lo = k.w0_lo + [m.sb(f"b_w_lo{i}", [P, CHUNK], f32r) for i in range(EARLY, CHUNKS)]
        ln_w = m.sb("ln_w", [P, CB])
        rope = m.sb("rope", [P, 4, HD0])
        causal = m.sb("causal", [P, G0, P], bf16)
        identb = m.sb("identb", [P, P], bf16)
        hn = m.sb("hn", [P, C])
        hT_hi, hT_lo = m.sb("hT_hi", [P, CB, P], f32r), m.sb("hT_lo", [P, CB, P], f32r)
        by_cos = [m.sb(f"by_cos{i}", [P, G0, HD0]) for i in range(2)]
        by_sin = [m.sb(f"by_sin{i}", [P, G0, HD0]) for i in range(2)]
        rot = [m.sb(f"rot{i}", [P, G0, HD0]) for i in range(2)]
        kT = [m.sb(f"kT{i}", [P, KV0, P]) for i in range(2)]
        qT = [m.sb(f"qT{i}", [P, H0, P]) for i in range(2)]
        v_hi = [m.sb(f"v_hi{i}", [P, KV0, HD0], f32r) for i in range(2)]
        v_lo = [m.sb(f"v_lo{i}", [P, KV0, HD0], f32r) for i in range(2)]
        negmax, rsum, rinv = m.sb("negmax", [P, H0]), m.sb("rsum", [P, H0]), m.sb("rinv", [P, H0])
        probs = [m.sb(f"probs{i}", [P, G0, P]) for i in range(2)]
        pn = [m.sb(f"probs_n{i}", [P, G0, P]) for i in range(2)]
        pT_hi = [m.sb(f"pT_hi{i}", [P, G0, P], f32r) for i in range(2)]
        pT_lo = [m.sb(f"pT_lo{i}", [P, G0, P], f32r) for i in range(2)]
        oT_hi = [m.sb(f"oT_hi{i}", [P, G0, P], f32r) for i in range(2)]
        oT_lo = [m.sb(f"oT_lo{i}", [P, G0, P], f32r) for i in range(2)]
        qkv_ps = [m.ps(f"qkv_ps{i}", [P, G0, HD0]) for i in range(2)]
        turn_ps = m.ps("turn_ps", [P, 4, P])
        s_ps = [m.ps(f"s_ps{i}", [P, G0, P]) for i in range(2)]
        pT_ps = m.ps("pT_ps", [P, G0, P])
        o_ps = m.ps("o_ps", [P, G0, P])
        wo_ps = m.ps("wo_ps", [P, C])
        flat = lambda a: a.rearrange("p h s -> p (h s)")

        s = lambda name: m.sem("b_" + name)
        consts_in, w_in = s("consts_in"), [s(f"w_in{i}") for i in range(STAGES)]
        w_hi_done, w_lo_done = s("w_hi"), [s(f"w_lo{i}") for i in range(CHUNKS)]
        stats_done, var_done, power_set, norm_step, z_done = s("stats"), s("var"), s("power_set"), s("norm_step"), s("z")
        hn_done, hT_made, hT_hi_done, hT_lo_done = s("hn"), s("hT_made"), s("hT_hi"), s("hT_lo")
        qkv_made, v_hi_done, v_lo_done = s("qkv_made"), s("v_hi"), s("v_lo")
        rope_mul, rot_done, rT_made, rT_out = s("rope_mul"), s("rot"), s("rT_made"), s("rT_out")
        s_made, max_done, exp_done, rinv_done, pn_done = s("s_made"), s("max"), s("exp"), s("rinv"), s("pn")
        pT_made, pT_hi_done, pT_lo_done = s("pT_made"), s("pT_hi"), s("pT_lo")
        o_made, o_hi_done, o_lo_done, wo_made, xa_done, ssq_done = s("o_made"), s("o_hi"), s("o_lo"), s("wo_made"), s("xa"), s("ssq")
        NG = 1 + KV0
        NP = NG + 1

        def pipeline(eng, step):
            def steps(it, par):
                for g in range(KV0):
                    step(it, par, g)

            steps(-1, 1)
            steps(0, 0)
            with eng.Fori(0, B // 2 - 1) as i:
                steps(2 * i + 1, 1)
                steps(2 * i + 2, 0)
            steps(B - 1, 1)
            steps(B, 0)

        def near(do, it, par, g, d):
            by, g = (g + d) // KV0, (g + d) % KV0
            of_sequence(do, it + by, par ^ (by & 1), g)

        def of_sequence(do, it, *rest):
            if not isinstance(it, int) or 0 <= it < B:
                do(it, *rest)

        def rotated(do, it, par, g):
            if g == 0:
                of_sequence(do, it, par, NG - 1)
            if g == 1:
                of_sequence(do, it + 1, 1 - par, 0)
            if g:
                of_sequence(do, it + 1, 1 - par, g)

        with nc.Block() as block:

            @block.sync
            def _(sp):
                def load(i):
                    if i - STAGES >= EARLY:
                        sp.wait_ge(w_lo_done[i - STAGES], 1)
                    load_chunk(sp, io, stage[i % STAGES], i).then_inc(w_in[i % STAGES], 16)

                load(EARLY)
                sp.dma_start(ln_w[:, :], io["ln_w"]).then_inc(consts_in, 16)
                sp.dma_start(rope[:, :, :], io["rope"]).then_inc(consts_in, 16)
                sp.dma_start(causal[:, :, :], io["causal"]).then_inc(consts_in, 16)
                sp.dma_start(identb[:, :], io["identb"]).then_inc(consts_in, 16)
                for i in range(EARLY + 1, CHUNKS):
                    load(i)

            @block.scalar
            def _(act):
                def round_w(i):
                    act.wait_ge(w_in[i % STAGES], 16 * ((i - EARLY) // STAGES + 1))
                    act.activation(w_hi[i][:, :], stage[i % STAGES][:, :], ACT.Copy).then_inc(w_hi_done, 1)

                round_w(EARLY)
                act.wait_ge(consts_in, 64)

                def round_h(f, par):
                    act.wait_ge(hT_made, f + 1)
                    wait_past(act, qkv_made, NP * f)
                    for c in range(CB):
                        act.activation(hT_hi[:, c, :], turn_ps[:, c, :], ACT.Copy, scale=ln_w[:, c:c + 1]).then_inc(hT_hi_done, 1)

                def rT_copy(f, par, j):
                    act.wait_ge(rT_made, NG * f + j + 1)
                    if j < 2:
                        wait_past(act, s_made, KV0 * (f - 1))
                    dst = kT[par][:, :, :] if j == 0 else qT[par][:, G0 * (j - 1):G0 * j, :]
                    act.activation(dst, turn_ps[:, :, :], ACT.Copy).then_inc(rT_out, 1)

                def round_v(f, par):
                    act.wait_ge(qkv_made, NP * (f + 1))
                    wait_past(act, o_made, KV0 * (f - 1))
                    act.activation(v_hi[par][:, :, :], qkv_ps[1][:, :, :], ACT.Copy).then_inc(v_hi_done, 1)

                def exps(it, par, g):
                    n = KV0 * it + g
                    act.wait_ge(max_done, n + 1)
                    wait_past(act, pn_done, n - 1)
                    for h in range(G0):
                        act.activation(probs[g % 2][:, h, :], s_ps[g % 2][:, h, :], ACT.Exp,
                                       bias=negmax[:, G0 * g + h:G0 * g + h + 1],
                                       accum_out=rsum[:, G0 * g + h:G0 * g + h + 1]).then_inc(exp_done, 1)

                def round_p(it, par, g):
                    n = KV0 * it + g
                    act.wait_ge(pT_made, n + 1)
                    wait_past(act, o_made, n - 1)
                    act.activation(pT_hi[g % 2][:, :, :], pT_ps[:, :, :], ACT.Copy).then_inc(pT_hi_done, 1)

                def round_o(it, par, g):
                    n = KV0 * it + g
                    act.wait_ge(o_made, n + 1)
                    wait_past(act, wo_made, n - 1)
                    act.activation(oT_hi[g % 2][:, :, :], o_ps[:, :, :], ACT.Copy).then_inc(o_hi_done, 1)

                def squares(it, par):
                    act.wait_ge(xa_done, it + 1)
                    act.activation(k.z[:, bass.ds(it, 1), :], k.xa[:, bass.ds(it, 1), :], ACT.Square,
                                   accum_out=k.ssq[:, bass.ds(it, 1)]).then_inc(ssq_done, 1)

                def step(it, par, g):
                    near(round_p, it, par, g, 0)
                    if g == 2:
                        of_sequence(squares, it - 1, 1 - par)
                    if g == 0:
                        of_sequence(round_v, it, par)
                        of_sequence(round_h, it + 1, 1 - par)
                    near(round_o, it, par, g, -1)
                    rotated(rT_copy, it, par, g)
                    near(exps, it, par, g, 2)
                    if isinstance(it, int) and it < 0:
                        for i in ((4, 5, 6), (7,), (8,), (9,))[g]:
                            round_w(i)

                pipeline(act, step)

            @block.tensor
            def _(pe):
                def turn_h(f, par):
                    pe.wait_ge(hn_done, f + 1)
                    wait_past(pe, rT_out, NG * f - 1)
                    for c in range(CB):
                        t = pe.transpose(turn_ps[:, c, :], hn[:, P * c:P * (c + 1)], k.ident[:, :])
                    t.then_inc(hT_made, 1)

                def project(f, par, c):
                    if c == 0:
                        pe.wait_ge(hT_lo_done, CB * (f + 1))
                        wait_past(pe, rope_mul, 2 * NG * f)
                    elif c == 1:
                        wait_past(pe, v_lo_done, f)
                    else:
                        pe.wait_ge(rope_mul, 2 * (NG * f + c - 1))
                    if isinstance(f, int) and f == 0:
                        if c == 0:
                            pe.wait_ge(consts_in, 64)
                        if c >= EARLY:
                            pe.wait_ge(w_lo_done[c], 1)
                    for cb in range(CB):
                        cols = slice(WIDE * cb, WIDE * (cb + 1))
                        t = products(pe, flat(qkv_ps[c % 2][:, :, :]), (hT_hi[:, cb, :], hT_lo[:, cb, :]),
                                     (w_hi[c][:, cols], w_lo[c][:, cols]), cb == 0, cb == CB - 1)
                    t.then_inc(qkv_made, 1)

                def turn_r(f, par, j):
                    pe.wait_ge(rot_done, NG * f + j + 1)
                    if j == NG - 1 and not (isinstance(f, int) and f == B - 1):
                        pe.wait_ge(hT_lo_done, CB * (f + 2))
                    elif isinstance(f, int) and f == 0 and j == 0:
                        pe.wait_ge(hT_lo_done, CB)
                    wait_past(pe, rT_out, NG * f + j)
                    for h in range(G0):
                        t = pe.transpose(turn_ps[:, h, :], rot[(par + j) % 2][:, h, :], k.ident[:, :])
                    t.then_inc(rT_made, 1)

                def scores(it, par, g):
                    n = KV0 * it + g
                    pe.wait_ge(rT_out, NG * it + g + 2)
                    wait_past(pe, exp_done, G0 * (n - 1))
                    pe.matmul(flat(s_ps[g % 2][:, :, :]), identb[:, :], flat(causal[:, :, :]), start=True, stop=False,
                              skip_group_check=True)
                    for h in range(G0):
                        t = pe.matmul(s_ps[g % 2][:, h, :], qT[par][:, G0 * g + h, :], kT[par][:, g, :],
                                      start=False, stop=(h == G0 - 1), skip_group_check=True)
                    t.then_inc(s_made, 1)

                def turn_p(it, par, g):
                    n = KV0 * it + g
                    pe.wait_ge(pn_done, n + 1)
                    wait_past(pe, pT_lo_done, n)
                    for h in range(G0):
                        t = pe.transpose(pT_ps[:, h, :], pn[g % 2][:, h, :], k.ident[:, :])
                    t.then_inc(pT_made, 1)

                def mix(it, par, g):
                    n = KV0 * it + g
                    pe.wait_ge(pT_lo_done, n + 1)
                    wait_past(pe, o_lo_done, n)
                    pe.wait_ge(v_lo_done, it + 1)
                    products(pe, flat(o_ps[:, :, :]), (v_hi[par][:, g, :], v_lo[par][:, g, :]),
                             (flat(pT_hi[g % 2][:, :, :]), flat(pT_lo[g % 2][:, :, :])), True, True).then_inc(o_made, 1)

                def output(it, par, g):
                    pe.wait_ge(o_lo_done, KV0 * it + g + 1)
                    if g == 0:
                        wait_past(pe, xa_done, it)
                    if isinstance(it, int) and it == 0:
                        pe.wait_ge(w_lo_done[NP + g], 1)
                    for h in range(G0):
                        cols = slice(C * h, C * (h + 1))
                        t = products(pe, wo_ps[:, :], (oT_hi[g % 2][:, h, :], oT_lo[g % 2][:, h, :]),
                                     (w_hi[NP + g][:, cols], w_lo[NP + g][:, cols]), g == 0 and h == 0, g == KV0 - 1 and h == G0 - 1)
                    t.then_inc(wo_made, 1)

                def step(it, par, g):
                    near(turn_p, it, par, g, 0)
                    near(scores, it, par, g, 2)
                    if g == 0:
                        of_sequence(turn_h, it + 1, 1 - par)
                    near(mix, it, par, g, -1)
                    near(output, it, par, g, -2)
                    rotated(turn_r, it, par, g)
                    for c in ((0, 1), (2,), (3,), (4, 5))[g]:
                        of_sequence(project, it + 1, 1 - par, c)

                pipeline(pe, step)

            @block.gpsimd
            def _(pool):
                eps4 = k.eps[:, 0:1].to_broadcast([P, HB])
                pool.memset(power[:, :], -0.5).then_inc(power_set, 1)
                pool.wait_ge(power_set, 1)
                for h in range(2):
                    part = slice(HB * h, HB * (h + 1))
                    pool.wait_ge(var_done, HB * (h + 1))
                    steps = ((var_eps, mv[:, part, 1], eps4, ALU.add), (rstd, var_eps[:, part], power[:, :], ALU.pow),
                             (mean_sq, mv[:, part, 1], rstd[:, part], ALU.mult), (mean_sq, mean_sq[:, part], rstd[:, part], ALU.mult),
                             (mean_sq, mean_sq[:, part], eps4, ALU.add), (rrms, mean_sq[:, part], power[:, :], ALU.pow))
                    for n, (out, x, y, op) in enumerate(steps):
                        pool.tensor_tensor(out[:, part], x, y, op).then_inc(norm_step, 1)
                        pool.wait_ge(norm_step, len(steps) * h + n + 1)

                def split_w(i):
                    pool.wait_ge(w_hi_done, i - EARLY + 1)
                    low(pool, w_lo[i][:, :], stage[i % STAGES][:, :], w_hi[i][:, :]).then_inc(w_lo_done[i], 1)

                split_w(4)

                def rotate(f, par, j):
                    i = (par + j) % 2
                    pool.wait_ge(rope_mul, 2 * (NG * f + j + 1))
                    wait_past(pool, rT_made, NG * f + j - 1)
                    pool.tensor_tensor(rot[i][:, :, :], by_cos[i][:, :, :], by_sin[i][:, :, :], ALU.add).then_inc(rot_done, 1)

                def normalise(it, par, g):
                    n = KV0 * it + g
                    pool.wait_ge(rinv_done, n + 1)
                    wait_past(pool, pT_made, n - 1)
                    pool.tensor_tensor(pn[g % 2][:, :, :], probs[g % 2][:, :, :],
                                       rinv[:, G0 * g:G0 * (g + 1)].unsqueeze(2).to_broadcast([P, G0, P]),
                                       ALU.mult).then_inc(pn_done, 1)

                def step(it, par, g):
                    near(normalise, it, par, g, 1)
                    rotated(rotate, it, par, g)
                    if isinstance(it, int) and it == 0:
                        split_w(NP + g)

                pipeline(pool, step)

            @block.vector
            def _(dve):
                for h in range(2):
                    for b in range(HB * h, HB * (h + 1)):
                        dve.bn_stats(stats[:, b, :], k.x1[:, b, :]).then_inc(stats_done, 1)
                    for b in range(HB * h, HB * (h + 1)):
                        dve.wait_ge(stats_done, b + 1)
                        dve.bn_aggr(mv[:, b, :], stats[:, b, :]).then_inc(var_done, 1)

                def normalise_half(h):
                    dve.wait_ge(norm_step, 6 * h + 2)
                    for b in range(HB * h, HB * (h + 1)):
                        dve.tensor_scalar(k.z[:, b, :], k.x1[:, b, :], mv[:, b, 0:1], rstd[:, b:b + 1],
                                          ALU.subtract, ALU.mult).then_inc(z_done, 1)

                def split_w(i):
                    dve.wait_ge(w_hi_done, i - EARLY + 1)
                    low(dve, w_lo[i][:, :], stage[i % STAGES][:, :], w_hi[i][:, :]).then_inc(w_lo_done[i], 1)

                def scale_h(f, par):
                    wait_past(dve, hT_made, f)
                    dve.tensor_scalar(hn[:, :], k.z[:, bass.ds(f, 1), :], rrms[:, bass.ds(f, 1)], None,
                                      ALU.mult).then_inc(hn_done, 1)

                def split_h(f, par):
                    dve.wait_ge(hT_hi_done, CB * (f + 1))
                    for c in range(CB):
                        dve.scalar_tensor_tensor(hT_lo[:, c, :], turn_ps[:, c, :], ln_w[:, c:c + 1], hT_hi[:, c, :].bitcast(fp32),
                                                 ALU.mult, ALU.subtract).then_inc(hT_lo_done, 1)

                def split_v(f, par):
                    dve.wait_ge(v_hi_done, f + 1)
                    low(dve, v_lo[par][:, :, :], qkv_ps[1][:, :, :], v_hi[par][:, :, :]).then_inc(v_lo_done, 1)

                def rotary(f, par, j):
                    i, tab = (par + j) % 2, 2 if j == 0 else 0
                    dve.wait_ge(qkv_made, NP * f + j + 1)
                    wait_past(dve, rot_done, NG * f + j - 1)
                    src, half = qkv_ps[j % 2], HD0 // 2
                    dve.tensor_tensor(by_cos[i][:, :, :], src[:, :, :],
                                      rope[:, tab:tab + 1, :].to_broadcast([P, G0, HD0]), ALU.mult).then_inc(rope_mul, 1)
                    swapped = by_sin[i][:, :, :].rearrange("p h (a d) -> p h a d", a=2)
                    pairs = src[:, :, :].rearrange("p h (a d) -> p h a d", a=2)[:, :, ::-1, :]
                    dve.tensor_tensor(swapped, pairs,
                                      rope[:, tab + 1:tab + 2, :].rearrange("p o (a d) -> p o a d", a=2)
                                      .to_broadcast([P, G0, 2, half]), ALU.mult).then_inc(rope_mul, 1)

                def maxima(it, par, g):
                    dve.wait_ge(s_made, KV0 * it + g + 1)
                    dve.tensor_reduce(negmax[:, G0 * g:G0 * (g + 1)], s_ps[g % 2][:, :, :], AX.X, ALU.max,
                                      negate=True).then_inc(max_done, 1)

                def reciprocals(it, par, g):
                    n = KV0 * it + g
                    dve.wait_ge(exp_done, G0 * (n + 1))
                    wait_past(dve, pn_done, n - KV0 + 1)
                    dve.reciprocal(rinv[:, G0 * g:G0 * (g + 1)], rsum[:, G0 * g:G0 * (g + 1)]).then_inc(rinv_done, 1)

                def split_p(it, par, g):
                    dve.wait_ge(pT_hi_done, KV0 * it + g + 1)
                    low(dve, pT_lo[g % 2][:, :, :], pT_ps[:, :, :], pT_hi[g % 2][:, :, :]).then_inc(pT_lo_done, 1)

                def split_o(it, par, g):
                    dve.wait_ge(o_hi_done, KV0 * it + g + 1)
                    low(dve, oT_lo[g % 2][:, :, :], o_ps[:, :, :], oT_hi[g % 2][:, :, :]).then_inc(o_lo_done, 1)

                def add_residual(it, par):
                    dve.wait_ge(wo_made, KV0 * (it + 1))
                    dve.tensor_tensor(k.xa[:, bass.ds(it, 1), :], k.z[:, bass.ds(it, 1), :], wo_ps[:, :].unsqueeze(1),
                                      ALU.add).then_inc(xa_done, 1)

                normalise_half(0)
                dve.wait_ge(norm_step, 6)
                dve.wait_ge(z_done, 1)
                scale_h(0, 0)
                normalise_half(1)
                dve.wait_ge(norm_step, 12)
                dve.wait_ge(z_done, B)
                dve.wait_ge(consts_in, 64)

                def step(it, par, g):
                    if g == 0 and not (isinstance(it, int) and it < 0):
                        of_sequence(scale_h, it + 1, 1 - par)
                    near(reciprocals, it, par, g, 1)
                    rotated(rotary, it, par, g)
                    near(split_p, it, par, g, 0)
                    if g == 0:
                        of_sequence(split_v, it, par)
                        of_sequence(split_h, it + 1, 1 - par)
                        if isinstance(it, int) and it < 0:
                            split_w(3)
                            split_w(5)
                    near(maxima, it, par, g, 2)
                    near(split_o, it, par, g, -1)
                    if g == 1:
                        of_sequence(add_residual, it - 1, 1 - par)

                pipeline(dve, step)
def earlier(j, par):
    return (j - par) // 2 if isinstance(j, int) else (j - par) >> 1


E0, FF0 = 8, 896
FB = FF0 // P
PACK = 4 * P + C
RING = 4
SLOTS = 256
SG = SLOTS // P
TILES = 2 * T // SLOTS + E0 - 1

MAGIC = 1.5 * 2.0 ** 23
QMAX, QEPS = 127.0, 1e-8


def experts0_stage(nc, k, io):
    x_slots = nc.dram_tensor("x_slots", (TILES * SLOTS, C), fp32, kind="Internal").ap()
    y_slots = k.y_slots
    with Memory(nc) as m:
        mean_sq, power, rrms = m.sb("c_mean_sq", [P, B]), m.sb("c_power", [P, B]), m.sb("c_rrms", [P, B])
        ff_w, gate_w = m.sb("ff_w", [P, C]), m.sb("gate_w", [P, CB, E0])
        iota_e, iota_t = m.sb("iota_e", [P, E0]), m.sb("iota_t", [P, TILES])
        before, ones = m.sb("before", [P, P], bf16), m.sb("ones", [P, P], bf16)
        zeros = m.sb("zeros", [P, 1920])
        h2, h2T = m.sb("h2", [P, B, C]), m.sb("h2T", [P, B, C])
        logits = m.sb("logits", [P, B, E0])
        top, top_i, top_f = m.sb("top", [P, B, 8]), m.sb("top_i", [P, B, 8], u32), m.sb("top_f", [P, B, 2])
        gap, gap_exp, gate_den = m.sb("gap", [P, B]), m.sb("gap_exp", [P, B]), m.sb("gate_den", [P, B])
        gates, slot = k.gates, k.slot
        pick = m.sb("pick", [P, 2, B, E0])
        picked = m.sb("picked", [P, B, E0], bf16)
        count, tiles_of = m.sb("count", [P, E0]), m.sb("tiles_of", [P, 4, E0])
        tile_end, first_slot = m.sb("tile_end", [P, E0]), m.sb("first_slot", [P, E0])
        place = m.sb("place", [P, B, E0])
        at = m.sb("at", [P, 2, B, E0])
        slot_f = m.sb("slot_f", [P, 2 * B])
        ended, expert_f = m.sb("ended", [P, TILES, E0]), m.sb("expert_f", [P, TILES])
        expert = m.sb("expert", [P, TILES], u32)
        w = [m.sb(f"c_w{f}", [P, PACK]) for f in range(FB)]
        w_hi = [m.sb(f"c_w_hi{f}", [P, PACK], f32r) for f in range(FB)]
        w_lo = [m.sb(f"c_w_lo{f}", [P, PACK], f32r) for f in range(FB)]
        xs = [m.sb(f"xs{i}", [P, SG, C]) for i in range(2)]
        xT_hi = [m.sb(f"xT_hi{i}", [P, CB, SLOTS], f32r) for i in range(2)]
        xT_lo = [m.sb(f"xT_lo{i}", [P, CB, SLOTS], f32r) for i in range(2)]
        silu = [m.sb(f"silu{i}", [P, SLOTS]) for i in range(2)]
        hid = [m.sb(f"hid{i}", [P, SLOTS]) for i in range(2)]
        h_hi = [m.sb(f"c_h_hi{i}", [P, SLOTS], f32r) for i in range(RING)]
        h_lo = [m.sb(f"c_h_lo{i}", [P, SLOTS], f32r) for i in range(RING)]
        ys = [m.sb(f"ys{i}", [P, SG, C]) for i in range(2)]
        w1 = m.sb("w1", [P, 2, CB, C])
        w_step = k.w_step
        w_top, w_inv = m.sb("w_top", [P, 2 * CB]), m.sb("w_inv", [P, 2 * CB])
        w_q = m.sb("w_q", [P, 2, CB, C], bf16)
        w_diag = m.sb("w_diag", [P, CB, P])
        ones32, identb = m.sb("ones32", [P, P]), m.sb("c_identb", [P, P], bf16)
        xT_ps = m.ps("xT_ps", [P, CB, SLOTS])
        gu_ps = [m.ps(f"gu_ps{i}", [P, 2, SLOTS]) for i in range(RING)]
        y_ps = [m.ps(f"ey_ps{i}", [P, SG, C]) for i in range(2)]
        cnt_ps = m.ps("cnt_ps", [P, 3, B, E0])

        s = lambda name: m.sem("c_" + name)
        consts_in, zeros_set, slots_clear = s("consts_in"), s("zeros_set"), s("slots_clear")
        rms_step, h2_done, h2T_made, h2T_out = s("rms"), s("h2"), s("h2T_made"), s("h2T_out")
        logits_made, logits_out, top_done, index_done, index_f = s("logits_made"), s("logits_out"), s("top"), s("index"), s("index_f")
        gap_done, gap_exp_done, gate_step = s("gap"), s("gap_exp"), s("gate_step")
        pick_done, picked_done, ranks_made, plan_step = s("pick"), s("picked"), s("ranks_made"), s("plan_step")
        slot_done, expert_done, sent = s("slot"), s("expert"), s("sent")
        w_in = [s(f"w_in{f}") for f in range(FB)]
        w_hi_done, w13_lo_done, w2_lo_done = s("w_hi"), s("w13_lo"), s("w2_lo")
        xs_in = [s(f"xs_in{i}") for i in range(2)]
        xT_made, xT_hi_done, xT_lo_done = s("xT_made"), s("xT_hi"), s("xT_lo")
        gu_made, silu_done, hid_done, h_hi_done, h_lo_done = s("gu_made"), s("silu"), s("hid"), s("h_hi"), s("h_lo")
        added, y_out = s("added"), s("y_out")
        stored = [s(f"stored{i}") for i in range(2)]
        base_done = s("base")
        w1_in, w_step_done, w_q_done, w_diag_done, w_turned, w_copied, row_made, row_out, ones_set = (
            s("w1_in"), s("w_step"), s("w_q"), s("w_diag"), s("w_turned"), s("w_copied"), s("row_made"), s("row_out"), s("ones_set"))

        def tiles(eng, step):
            step(0, 0)
            step(1, 1)
            with eng.Fori(1, TILES // 2) as i:
                step(2 * i, 0)
                step(2 * i + 1, 1)
            step(TILES - 1, 0)

        def ring_free(eng, sem, j, f):
            n = FB * j + f
            wait_past(eng, sem, n + 1 - (RING if f >= RING else FB if f == RING - 1 else FB - RING))

        def ahead(j, f, by):
            return (j, f + by) if f + by < FB else (j + 1, f + by - FB)

        def is_last(j):
            return isinstance(j, int) and j == TILES - 1

        with nc.Block() as block:

            @block.sync
            def _(sp):
                sp.dma_start(ff_w[:, :], io["ff_w"]).then_inc(consts_in, 16)
                sp.dma_start(gate_w[:, :, :], io["gate_w0"].rearrange("(cb p) e -> p cb e", p=P)).then_inc(consts_in, 16)
                sp.dma_start(iota_e[:, :], io["iota"][:, 0:E0]).then_inc(consts_in, 16)
                sp.dma_start(iota_t[:, :], io["iota"][:, 0:TILES]).then_inc(consts_in, 16)
                sp.dma_start(before[:, :], io["before"]).then_inc(consts_in, 16)
                sp.dma_start(ones[:, :], io["ones"]).then_inc(consts_in, 16)
                sp.dma_start(w1[:, 0, :, :], io["wq1"].rearrange("(ob p) c -> p ob c", p=P)).then_inc(w1_in, 16)
                sp.dma_start(w1[:, 1, :, :], io["wo1"].rearrange("(ob p) c -> p ob c", p=P)).then_inc(w1_in, 16)
                sp.dma_start(identb[:, :], io["identb"]).then_inc(w1_in, 16)
                sp.wait_ge(zeros_set, 1)
                flat = x_slots.rearrange("(p r) c -> p (r c)", p=P)
                for i in range(4):
                    sp.dma_start(flat[:, 1920 * i:1920 * (i + 1)], zeros[:, :]).then_inc(slots_clear, 16)
                sp.wait_ge(expert_done, 1)

                def load(j, par):
                    e = sp.value_load(expert[0:1, bass.ds(j, 1)], min_val=0, max_val=E0 - 1)
                    first = isinstance(j, int) and j == 0
                    if not first:
                        load_x(j, par)
                    for f in range(FB):
                        for split in (w_hi_done, w13_lo_done, w2_lo_done):
                            wait_past(sp, split, FB * (j - 1) + f + 1)
                        sp.dma_start(w[f][:, :], io["pack0"][bass.ds(e, 1), :, PACK * f:PACK * (f + 1)].rearrange("o p n -> (o p) n"))\
                            .then_inc(w_in[f], 16)
                    if first:
                        sp.wait_ge(sent, 16 * 2 * B)
                        load_x(j, par)

                def load_x(j, par):
                    wait_past(sp, xT_made, j - 1)
                    sp.dma_start(xs[par][:, :, :], x_slots[bass.ds(j * SLOTS, SLOTS), :].rearrange("(r p) c -> p r c", p=P)).then_inc(xs_in[par], 16)

                tiles(sp, load)
                for h in range(2):
                    sp.wait_ge(stored[h], 16 * ((TILES + 1 - h) // 2))

            @block.scalar
            def _(act):
                for n in range(B // 2):
                    act.wait_ge(h2T_made, n + 1)
                    act.activation(h2T[:, 2 * n:2 * n + 2, :], gu_ps[n][:, :, :], ACT.Copy).then_inc(h2T_out, 1)
                act.wait_ge(logits_made, 1)
                act.activation(logits[:, :, :], cnt_ps[:, 0, :, :], ACT.Copy).then_inc(logits_out, 1)
                act.wait_ge(gap_done, 1)
                act.activation(gap_exp[:, :], gap[:, :], ACT.Exp).then_inc(gap_exp_done, 1)

                def round_w(j, f):
                    act.wait_ge(w_in[f], 16 * j + 16)
                    wait_past(act, added, FB * (j - 1) + f + 1)
                    act.activation(w_hi[f][:, :], w[f][:, :], ACT.Copy).then_inc(w_hi_done, 1)

                def round_x(j, par):
                    act.wait_ge(xT_made, j + 1)
                    act.activation(xT_hi[par][:, :, :], xT_ps[:, :, :], ACT.Copy).then_inc(xT_hi_done, 1)

                def store(j, par):
                    act.wait_ge(added, FB * (j + 1))
                    wait_past(act, stored[par], 16 * earlier(j, par))
                    act.activation(ys[par][:, :, :], y_ps[par][:, :, :], ACT.Copy).then_inc(y_out, 1)
                    act.wait_ge(y_out, j + 1)
                    act.dma_start(y_slots[bass.ds(j * SLOTS, SLOTS), :].rearrange("(r p) c -> p r c", p=P),
                                  ys[par][:, :, :]).then_inc(stored[par], 16)

                def work(j, par):
                    for f in range(FB):
                        i = (par + f) % 2
                        n = FB * j + f
                        act.wait_ge(gu_made, n + 1)
                        wait_past(act, hid_done, n - 1)
                        act.activation(silu[i][:, :], gu_ps[f % RING][:, 0, :], ACT.Silu).then_inc(silu_done, 1)
                        if f == 3 and not (isinstance(j, int) and j == 0):
                            store(j - 1, 1 - par)
                        if f == 4 and not is_last(j):
                            round_x(j + 1, 1 - par)
                        if f + 3 < FB or not is_last(j):
                            round_w(*ahead(j, f, 3))

                act.wait_ge(w_turned, 2)
                act.activation(k.w_qT[:, :, :, :].rearrange("p i c o -> p (i c o)"), gu_ps[0][:, :, :].rearrange("p r s -> p (r s)").bitcast(bf16), ACT.Copy).then_inc(w_copied, 1)
                act.wait_ge(row_made, 1)
                act.activation(k.step_row[:, :], gu_ps[1][:, :, :].rearrange("p r s -> p (r s)")[:, 0:C], ACT.Copy).then_inc(row_out, 1)
                for f in range(3):
                    round_w(0, f)
                round_x(0, 0)
                tiles(act, work)
                store(TILES - 1, 0)

            @block.tensor
            def _(pe):
                for b in range(B):
                    pe.wait_ge(h2_done, b + 1)
                    for c in range(CB):
                        t = pe.transpose(gu_ps[b // 2][:, b % 2, P * c:P * (c + 1)], h2[:, b, P * c:P * (c + 1)], k.ident[:, :])
                    if b % 2:
                        t.then_inc(h2T_made, 1)
                pe.wait_ge(consts_in, 96)
                for b in range(B):
                    pe.wait_ge(h2T_out, b // 2 + 1)
                    for c in range(CB):
                        t = pe.matmul(cnt_ps[:, 0, b, :], h2T[:, b, P * c:P * (c + 1)], gate_w[:, c, :],
                                      start=(c == 0), stop=(c == CB - 1))
                t.then_inc(logits_made, 1)
                pe.wait_ge(picked_done, 1)
                pe.wait_ge(logits_out, 1)
                flat = lambda a: a.rearrange("p b e -> p (b e)")
                pe.matmul(flat(cnt_ps[:, 2, :, :]), ones[:, :], flat(picked[:, :, :]), start=True, stop=True, skip_group_check=True)
                pe.matmul(flat(cnt_ps[:, 1, :, :]), before[:, :], flat(picked[:, :, :]), start=True, stop=False, skip_group_check=True)
                for b in range(B - 1):
                    t = pe.matmul(cnt_ps[:, 1, b + 1:B, :], ones[:, :], picked[:, b:b + 1, :].to_broadcast([P, B - 1 - b, E0]),
                                  start=False, stop=(b == B - 2), skip_group_check=True)
                t.then_inc(ranks_made, 1)

                pe.wait_ge(w_q_done, 1)
                for i in range(2):
                    for c in range(CB):
                        for ob in range(CB):
                            t = pe.transpose(gu_ps[0][:, :, :].rearrange("p r s -> p (r s)").bitcast(bf16)[:, (i * CB + c) * C + P * ob:(i * CB + c) * C + P * (ob + 1)],
                                             w_q[:, i, ob, P * c:P * (c + 1)], identb[:, :])
                    t.then_inc(w_turned, 1)
                pe.wait_ge(w_diag_done, CB)
                pe.wait_ge(ones_set, 1)
                for n in range(CB):
                    t = pe.matmul(gu_ps[1][:, :, :].rearrange("p r s -> p (r s)")[:, P * n:P * (n + 1)], ones32[:, :], w_diag[:, n, :], start=True, stop=True)
                t.then_inc(row_made, 1)
                pe.wait_ge(w_copied, 1)
                pe.wait_ge(row_out, 1)

                def turn(j, par):
                    pe.wait_ge(xs_in[par], 16 * earlier(j, par) + 16)
                    wait_past(pe, xT_lo_done, j)
                    for r in range(SG):
                        for c in range(CB):
                            t = pe.transpose(xT_ps[:, c, P * r:P * (r + 1)], xs[par][:, r, P * c:P * (c + 1)], k.ident[:, :])
                    t.then_inc(xT_made, 1)

                def up(j, par, f):
                    if f == 0:
                        pe.wait_ge(xT_lo_done, j + 1)
                    pe.wait_ge(w13_lo_done, FB * j + f + 1)
                    ring_free(pe, hid_done, j, f)
                    for what in range(2):
                        for c in range(CB):
                            cols = slice(P * (2 * what + c), P * (2 * what + c + 1))
                            t = products(pe, gu_ps[f % RING][:, what, :], (w_hi[f][:, cols], w_lo[f][:, cols]),
                                         (xT_hi[par][:, c, :], xT_lo[par][:, c, :]), c == 0, c == CB - 1)
                    t.then_inc(gu_made, 1)

                def down(j, par, f):
                    n = FB * j + f
                    pe.wait_ge(h_lo_done, n + 1)
                    pe.wait_ge(w2_lo_done, n + 1)
                    if f == 0:
                        wait_past(pe, y_out, j - 1)
                    for r in range(SG):
                        rows = slice(P * r, P * (r + 1))
                        t = products(pe, y_ps[par][:, r, :], (h_hi[f % RING][:, rows], h_lo[f % RING][:, rows]),
                                     (w_hi[f][:, 4 * P:PACK], w_lo[f][:, 4 * P:PACK]), f == 0 and r == 0, f == FB - 1 and r == SG - 1)
                    t.then_inc(added, 1)

                def work(j, par):
                    for f in range(FB):
                        if f == 3 and not is_last(j):
                            turn(j + 1, 1 - par)
                        up(j, par, f)
                        if f >= 2:
                            down(j, par, f - 2)
                        elif not (isinstance(j, int) and j == 0):
                            down(j - 1, 1 - par, FB + f - 2)

                turn(0, 0)
                tiles(pe, work)
                down(TILES - 1, 0, FB - 2)
                down(TILES - 1, 0, FB - 1)

            @block.gpsimd
            def _(pool):
                pool.memset(power[:, :], -0.5).then_inc(rms_step, 1)
                pool.memset(ones32[:, :], 1.0).then_inc(ones_set, 1)
                pool.tensor_scalar(mean_sq[:, :], k.ssq[:, :], 1.0 / C, LN_EPS, ALU.mult, ALU.add).then_inc(rms_step, 1)
                pool.wait_ge(rms_step, 2)
                pool.tensor_tensor(rrms[:, :], mean_sq[:, :], power[:, :], ALU.pow).then_inc(rms_step, 1)
                for b in range(B):
                    pool.tensor_tensor(k.x1[:, b, :], k.x1[:, b, :], k.xa[:, b, :], ALU.add).then_inc(base_done, 1)
                pool.wait_ge(slots_clear, 64)
                for n in range(2 * B):
                    pool.wait_ge(slot_done, 1)
                    pool.wait_ge(h2_done, n % B + 1)
                    pool.indirect_dma_start(x_slots, bass.IndirectOffsetOnAxis(slot[:, n:n + 1], 0), h2[:, n % B, :],
                                            None).then_inc(sent, 16)
                def split_w(j, par):
                    for f in range(FB):
                        pool.wait_ge(w_hi_done, FB * j + f + 1)
                        low(pool, w_lo[f][:, 0:4 * P], w[f][:, 0:4 * P], w_hi[f][:, 0:4 * P]).then_inc(w13_lo_done, 1)

                tiles(pool, split_w)

            @block.vector
            def _(dve):
                dve.memset(zeros[:, :], 0.0).then_inc(zeros_set, 1)
                dve.wait_ge(rms_step, 3)
                dve.wait_ge(consts_in, 96)
                for b in range(B):
                    dve.scalar_tensor_tensor(h2[:, b, :], k.xa[:, b, :], rrms[:, b:b + 1], ff_w[:, :], ALU.mult, ALU.mult)\
                        .then_inc(h2_done, 1)
                dve.wait_ge(logits_out, 1)
                for b in range(B):
                    dve.max(top[:, b, :], logits[:, b, :]).then_inc(top_done, 1)
                for b in range(B):
                    dve.wait_ge(top_done, b + 1)
                    dve.max_index(top_i[:, b, :], top[:, b, :], logits[:, b, :]).then_inc(index_done, 1)
                dve.tensor_tensor(gap[:, :], top[:, :, 1], top[:, :, 0], ALU.subtract).then_inc(gap_done, 1)
                dve.wait_ge(index_done, B)
                dve.tensor_copy(top_f[:, :, :], top_i[:, :, 0:2]).then_inc(index_f, 1)
                dve.wait_ge(index_f, 1)
                for i in range(2):
                    dve.tensor_tensor(pick[:, i, :, :], iota_e[:, :].unsqueeze(1).to_broadcast([P, B, E0]),
                                      top_f[:, :, i:i + 1].to_broadcast([P, B, E0]), ALU.is_equal).then_inc(pick_done, 1)
                dve.wait_ge(pick_done, 2)
                dve.tensor_tensor(picked[:, :, :], pick[:, 0, :, :], pick[:, 1, :, :], ALU.add).then_inc(picked_done, 1)
                dve.wait_ge(gap_exp_done, 1)
                dve.tensor_scalar(gate_den[:, :], gap_exp[:, :], 1.0, None, ALU.add).then_inc(gate_step, 1)
                dve.wait_ge(gate_step, 1)
                dve.reciprocal(gates[:, 0, :], gate_den[:, :]).then_inc(gate_step, 1)
                dve.wait_ge(gate_step, 2)
                dve.tensor_tensor(gates[:, 1, :], gates[:, 0, :], gap_exp[:, :], ALU.mult).then_inc(gate_step, 1)
                dve.wait_ge(ranks_made, 1)
                dve.tensor_reduce(count[:, :], cnt_ps[:, 2, :, :].rearrange("p b e -> p e b"), AX.X, ALU.add).then_inc(plan_step, 1)
                dve.wait_ge(plan_step, 1)
                dve.tensor_scalar(tiles_of[:, 0, :], count[:, :], 0.0, None, ALU.is_gt).then_inc(plan_step, 1)
                for i in range(1, T // SLOTS):
                    dve.wait_ge(plan_step, i + 1)
                    dve.scalar_tensor_tensor(tiles_of[:, i, :], count[:, :], float(SLOTS * i), tiles_of[:, i - 1, :],
                                             ALU.is_gt, ALU.add).then_inc(plan_step, 1)
                last = T // SLOTS - 1
                dve.wait_ge(plan_step, last + 2)
                dve.tensor_tensor_scan(tile_end[:, :], tiles_of[:, last, :], tiles_of[:, last, :], 0.0, ALU.add, ALU.bypass)\
                    .then_inc(plan_step, 1)
                dve.wait_ge(plan_step, last + 3)
                dve.tensor_tensor(first_slot[:, :], tile_end[:, :], tiles_of[:, last, :], ALU.subtract).then_inc(plan_step, 1)
                dve.wait_ge(plan_step, last + 4)
                dve.scalar_tensor_tensor(place[:, :, :], first_slot[:, :].unsqueeze(1).to_broadcast([P, B, E0]), float(SLOTS),
                                         cnt_ps[:, 1, :, :], ALU.mult, ALU.add).then_inc(plan_step, 1)
                dve.wait_ge(plan_step, last + 5)
                for i in range(2):
                    dve.tensor_tensor(at[:, i, :, :], pick[:, i, :, :], place[:, :, :], ALU.mult).then_inc(plan_step, 1)
                dve.wait_ge(plan_step, last + 7)
                dve.tensor_reduce(slot_f[:, :], at[:, :, :, :].rearrange("p i b e -> p (i b) e"), AX.X, ALU.add).then_inc(plan_step, 1)
                dve.wait_ge(plan_step, last + 8)
                dve.tensor_copy(slot[:, :], slot_f[:, :]).then_inc(slot_done, 1)
                dve.tensor_tensor(ended[:, :, :], iota_t[:, :].unsqueeze(2).to_broadcast([P, TILES, E0]),
                                  tile_end[:, :].unsqueeze(1).to_broadcast([P, TILES, E0]), ALU.is_ge).then_inc(plan_step, 1)
                dve.wait_ge(plan_step, last + 9)
                dve.tensor_reduce(expert_f[:, :], ended[:, :, :], AX.X, ALU.add).then_inc(plan_step, 1)
                dve.wait_ge(plan_step, last + 10)
                dve.tensor_scalar(expert[:, :], expert_f[:, :], float(E0 - 1), None, ALU.min).then_inc(expert_done, 1)

                dve.wait_ge(w1_in, 48)
                flat_w = w1[:, :, :, :].rearrange("p i o c -> p (i o) c")
                dve.tensor_reduce(w_top[:, :], flat_w, AX.X, ALU.max, apply_absolute_value=True).then_inc(w_step_done, 1)
                dve.wait_ge(w_step_done, 1)
                dve.tensor_scalar(w_step[:, :], w_top[:, :], 1.0 / QMAX, QEPS, ALU.mult, ALU.max).then_inc(w_step_done, 1)
                dve.wait_ge(w_step_done, 2)
                dve.reciprocal(w_inv[:, :], w_step[:, :]).then_inc(w_step_done, 1)
                dve.wait_ge(w_step_done, 3)
                for n in range(2 * CB):
                    dve.tensor_scalar(flat_w[:, n, :], flat_w[:, n, :], w_inv[:, n:n + 1], QMAX, ALU.mult, ALU.min).then_inc(w_step_done, 1)
                dve.wait_ge(w_step_done, 3 + 2 * CB)
                dve.tensor_scalar(flat_w, flat_w, -QMAX, MAGIC, ALU.max, ALU.add).then_inc(w_step_done, 1)
                dve.wait_ge(w_step_done, 4 + 2 * CB)
                dve.tensor_scalar(w_q[:, :, :, :].rearrange("p i o c -> p (i o) c"), flat_w, MAGIC, None, ALU.subtract).then_inc(w_q_done, 1)
                for n in range(CB):
                    dve.tensor_scalar(w_diag[:, n, :], k.ident[:, :], w_step[:, CB + n:CB + n + 1], None, ALU.mult).then_inc(w_diag_done, 1)

                def split_w2(j, f):
                    dve.wait_ge(w_hi_done, FB * j + f + 1)
                    low(dve, w_lo[f][:, 4 * P:PACK], w[f][:, 4 * P:PACK], w_hi[f][:, 4 * P:PACK]).then_inc(w2_lo_done, 1)

                def split_x(j, par):
                    dve.wait_ge(xT_hi_done, j + 1)
                    low(dve, xT_lo[par][:, :, :], xT_ps[:, :, :], xT_hi[par][:, :, :]).then_inc(xT_lo_done, 1)

                def work(j, par):
                    for f in range(FB):
                        i = (par + f) % 2
                        n = FB * j + f
                        dve.wait_ge(silu_done, n + 1)
                        dve.tensor_tensor(hid[i][:, :], gu_ps[f % RING][:, 1, :], silu[i][:, :], ALU.mult).then_inc(hid_done, 1)
                        if f + 2 < FB or not is_last(j):
                            split_w2(*ahead(j, f, 2))
                        dve.wait_ge(hid_done, n + 1)
                        ring_free(dve, added, j, f)
                        dve.tensor_copy(h_hi[f % RING][:, :], hid[i][:, :]).then_inc(h_hi_done, 1)
                        dve.wait_ge(h_hi_done, n + 1)
                        low(dve, h_lo[f % RING][:, :], hid[i][:, :], h_hi[f % RING][:, :]).then_inc(h_lo_done, 1)
                        if f == 4 and not is_last(j):
                            split_x(j + 1, 1 - par)

                for f in range(2):
                    split_w2(0, f)
                split_x(0, 0)
                tiles(dve, work)
H1, HD1 = 16, 16
HG = 4
GROUPS = H1 // HG
HPB = P // HD1
STRIDE = P + HD1


def cross_stage(nc, k, io):
    with Memory(nc) as m:
        stats, mv = m.sb("d_stats", [P, B, 6]), m.sb("d_mean_var", [P, B, 2])
        var_eps, rstd, power = m.sb("d_var_eps", [P, B]), m.sb("d_rstd", [P, B]), m.sb("d_power", [P, B])
        y_pair = (k.z, k.xa)
        y = m.sb("d_y", [P, B, C])
        top, step_x, inv_x = m.sb("d_top", [P, 2, B]), m.sb("d_step", [P, 2, B]), m.sb("d_inv", [P, 2, B])
        yq = m.sb("d_yq", [P, B, C], bf16)
        yqT = m.sb("d_yqT", [P, CB, T], bf16)
        bias_row, bias_col = m.sb("bias_row", [P, C]), m.sb("bias_col", [P, CB])
        identb = m.sb("d_identb", [P, P], bf16)
        head_mask = m.sb("head_mask", [P, HPB])
        mask = m.sb("d_mask", [P, B, P])
        q1T = m.sb("q1T", [P, CB, T])
        qb = [m.sb(f"qb{i}", [P, CB, P]) for i in range(2)]
        kz = [m.sb(f"kz{i}", [P, H1, P]) for i in range(2)]
        vz = [m.sb(f"vz{i}", [P, CB, HPB * STRIDE]) for i in range(2)]
        sm = [m.sb(f"sm{g}", [P, HG, P]) for g in range(GROUPS)]
        probs = [m.sb(f"d_probs{g}", [P, HG, P]) for g in range(GROUPS)]
        pT = [m.sb(f"d_pT{g}", [P, HG, P]) for g in range(GROUPS)]
        negmax, rsum, rinv = (m.sb(n, [P, 2, H1]) for n in ("d_negmax", "d_rsum", "d_rinv"))
        warm = m.sb("d_warm", [P, 1])
        banks = [m.ps(f"d_bank{i}", [P, 512]) for i in range(8)]
        half = lambda i: banks[i][:, :].bitcast(bf16)

        s = lambda name: m.sem("d_" + name)
        consts_in, mask_in = s("consts_in"), s("mask_in")
        vz_set = s("vz_set")
        fetched = [s(f"fetched{b}") for b in range(B)]
        power_set, var_done, rstd_step, row_step, yq_done = s("power_set"), s("var"), s("rstd"), s("row_step"), s("yq")
        turned, yqT_out, q_made, q_done, qT_made, qT_out = (
            s("turned"), s("yqT_out"), s("q_made"), s("q"), s("qT_made"), s("qT_out"))
        qb_done, kz_done, vz_done = s("qb"), s("kz"), s("vz")
        s_made, sm_done, max_done, exp_done, rinv_done = s("s_made"), s("sm"), s("max"), s("exp"), s("rinv")
        pT_made, o_made, o_out = s("pT_made"), s("o_made"), s("o_out")
        pT_out = [s(f"pT_out{i}") for i in range(2)]
        warm_done, inv_done, divided = s("warm"), s("inv"), s("divided")
        bias_done, r_made, r_scaled, x3_done = s("bias"), s("r_made"), s("r_scaled"), s("x3")
        x3_stats = s("x3_stats")

        PARTS = ((0, 4), (4, 6), (6, 8))

        def row_steps(then, src, which, b0, b1):
            part = slice(b0, b1)
            then(nc.vector.tensor_reduce(top[:, which, part], src[:, part, :], AX.X, ALU.max, apply_absolute_value=True))
            then(nc.vector.tensor_scalar(step_x[:, which, part], top[:, which, part], 1.0 / QMAX, QEPS, ALU.mult, ALU.max))
            nc.vector.reciprocal(inv_x[:, which, part], step_x[:, which, part]).then_inc(inv_done, 1)

        def round_rows(then, src, which, n):
            part = slice(*PARTS[n])
            nc.vector.wait_ge(divided, B * which + PARTS[n][1])
            then(nc.vector.tensor_scalar(src[:, part, :], src[:, part, :], MAGIC, MAGIC + QMAX, ALU.add, ALU.min))
            nc.vector.tensor_scalar(yq[:, part, :], src[:, part, :], MAGIC - QMAX, MAGIC, ALU.max, ALU.subtract).then_inc(yq_done, 1)

        def sequences(eng, step):
            step(0, 0, False)
            with eng.Fori(0, B // 2 - 1) as i:
                step(2 * i + 1, 1, False)
                step(2 * i + 2, 0, False)
            step(B - 1, 1, True)

        with nc.Block() as block:

            @block.sync
            def _(sp):
                sp.dma_start(bias_row[:, :], io["bias_row"]).then_inc(consts_in, 16)
                sp.dma_start(bias_col[:, :], io["bias_col"]).then_inc(consts_in, 16)
                sp.dma_start(identb[:, :], io["identb"]).then_inc(consts_in, 16)
                sp.dma_start(head_mask[:, :], io["head_mask"]).then_inc(consts_in, 16)
                sp.dma_start(mask[:, :, :], io["mask"].rearrange("b q s -> q b s")).then_inc(mask_in, 16)

            @block.scalar
            def _(act):
                def divide(which, n):
                    act.wait_ge(inv_done, len(PARTS) * which + n + 1)
                    for b in range(*PARTS[n]):
                        act.activation(y[:, b, :], y[:, b, :], ACT.Copy, scale=inv_x[:, which, b:b + 1]).then_inc(divided, 1)

                def yqT_copy(which, n):
                    b0, b1 = PARTS[n]
                    for c in range(CB):
                        act.wait_ge(turned, CB * (len(PARTS) * which + n) + c + 1)
                        act.activation(yqT[:, c, P * b0:P * b1], half(2 + c)[:, P * b0:P * b1], ACT.Copy).then_inc(yqT_out, 1)

                def queries(n):
                    for b in range(*PARTS[n]):
                        act.wait_ge(q_made, b - b % 2 + 2)
                        act.activation(y[:, b, :], banks[4 + b // 2][:, C * (b % 2):C * (b % 2 + 1)], ACT.Copy,
                                       scale=step_x[:, 0, b:b + 1]).then_inc(q_done, 1)

                def qT_copy(h):
                    for c in range(CB):
                        n = CB * h + c
                        act.wait_ge(qT_made, n + 1)
                        act.activation(q1T[:, c, 512 * h:512 * (h + 1)], banks[n][:, :], ACT.Identity,
                                       bias=bias_col[:, c:c + 1], scale=k.w_step[:, c:c + 1]).then_inc(qT_out, 1)

                act.activation(warm[:, :], k.eps[:, :], ACT.Exp).then_inc(warm_done, 1)
                divide(0, 0)
                yqT_copy(0, 0)
                divide(0, 1)
                queries(0)
                act.wait_ge(consts_in, 64)
                yqT_copy(0, 1)
                divide(0, 2)
                qT_copy(0)
                yqT_copy(0, 2)
                queries(1)
                queries(2)
                qT_copy(1)

                def exps(it, par, g):
                    act.wait_ge(max_done, GROUPS * it + g + 1)
                    wait_past(act, pT_made, GROUPS * (it - 1) + g + 1)
                    if g == 0:
                        wait_past(act, rinv_done, it - 1)
                    for h in range(HG):
                        n = HG * g + h
                        t = act.activation(probs[g][:, h, :], sm[g][:, h, :], ACT.Exp, bias=negmax[:, par, n:n + 1],
                                           accum_out=rsum[:, par, n:n + 1])
                        t.then_inc(exp_done, 1)

                def pT_copy(it, g):
                    act.wait_ge(pT_made, GROUPS * it + g + 1)
                    wait_past(act, o_made, GROUPS * (it - 1) + g + 1)
                    act.activation(pT[g][:, :, :], banks[2 + g % 2][:, :].rearrange("p (h s) -> p h s", h=HG), ACT.Copy)\
                        .then_inc(pT_out[1], 1)

                def step(it, par, last):
                    for g in range(GROUPS):
                        exps(it, par, g)
                        if g == 2:
                            pT_copy(it, 1)
                        if g == 0 and not (isinstance(it, int) and it == 0):
                            pT_copy(it - 1, GROUPS - 1)

                sequences(act, step)
                pT_copy(B - 1, GROUPS - 1)
                act.wait_ge(o_out, B)
                divide(1, 0)
                divide(1, 1)
                yqT_copy(1, 0)
                divide(1, 2)
                yqT_copy(1, 1)
                yqT_copy(1, 2)

            @block.tensor
            def _(pe):
                pe.wait_ge(consts_in, 64)
                def project(which, n, products_done):
                    b0, b1 = PARTS[n]
                    done = len(PARTS) * which + n
                    pe.wait_ge(yq_done, done + 1)
                    wait_past(pe, yqT_out, CB * done)
                    for c in range(CB):
                        for b in range(b0, b1):
                            t = pe.transpose(half(2 + c)[:, P * b:P * (b + 1)], yq[:, b, P * c:P * (c + 1)], identb[:, :])
                        t.then_inc(turned, 1)
                    pe.wait_ge(yqT_out, CB * (done + 1))
                    for b in range(b0, b1):
                        for c in range(CB):
                            t = pe.matmul(banks[4 + b // 2][:, C * (b % 2):C * (b % 2 + 1)], yqT[:, c, P * b:P * (b + 1)],
                                          k.w_qT[:, which, c, :], start=(c == 0), stop=(c == CB - 1))
                        t.then_inc(products_done, 1)

                def turn_q(h):
                    pe.wait_ge(q_done, HB * (h + 1))
                    for c in range(CB):
                        for b in range(HB * h, HB * (h + 1)):
                            t = pe.transpose(banks[CB * h + c][:, P * (b % HB):P * (b % HB + 1)], y[:, b, P * c:P * (c + 1)], k.ident[:, :])
                        t.then_inc(qT_made, 1)

                project(0, 0, q_made)
                project(0, 1, q_made)
                turn_q(0)
                project(0, 2, q_made)

                def scores(it, par, g):
                    if g == 0:
                        pe.wait_ge(qb_done, it + 1)
                        pe.wait_ge(kz_done, 2 * (it + 1))
                    wait_past(pe, sm_done, GROUPS * it + g - 1)
                    pe.matmul(banks[g % 2][:, :], qb[par][:, g // 2, :],
                              kz[par][:, HG * g:HG * (g + 1), :].rearrange("p h s -> p (h s)"), start=True, stop=True).then_inc(s_made, 1)

                def turn_p(it, g):
                    pe.wait_ge(exp_done, H1 * it + HG * (g + 1))
                    wait_past(pe, pT_out[g % 2], GROUPS // 2 * it + g // 2)
                    for h in range(HG):
                        t = pe.transpose(banks[2 + g % 2][:, P * h:P * (h + 1)], probs[g][:, h, :], k.ident[:, :])
                    t.then_inc(pT_made, 1)

                def mix(it, par, g):
                    if g == 0:
                        pe.wait_ge(vz_done, it + 1)
                        wait_past(pe, o_out, it - 1)
                    pe.wait_ge(pT_out[g % 2], GROUPS // 2 * it + g // 2 + 1)
                    c = g // 2
                    for h in range(HG):
                        j = HG * (g % 2) + h
                        t = pe.matmul(banks[4 + par][:, P * c:P * (c + 1)], pT[g][:, h, :], vz[par][:, c, P * j:P * (j + 1)],
                                      start=(j == 0), stop=(j == HPB - 1))
                    t.then_inc(o_made, 1)

                pe.wait_ge(qT_out, CB)
                scores(0, 0, 0)
                scores(0, 0, 1)
                turn_q(1)

                def step(it, par, last):
                    for g in range(GROUPS):
                        if g < GROUPS - 2:
                            scores(it, par, g + 2)
                        elif not last:
                            scores(it + 1, 1 - par, g + 2 - GROUPS)
                        turn_p(it, g)
                        if g:
                            mix(it, par, g - 1)
                        elif not (isinstance(it, int) and it == 0):
                            mix(it - 1, 1 - par, GROUPS - 1)

                sequences(pe, step)
                mix(B - 1, 1, GROUPS - 1)
                for n in range(len(PARTS)):
                    project(1, n, r_made)

            @block.gpsimd
            def _(pool):
                pool.memset(power[:, :], -0.5).then_inc(power_set, 1)
                pool.wait_ge(power_set, 1)

                def fetch(b):
                    for i in range(2):
                        n = B * i + b
                        pool.indirect_dma_start(y_pair[i][:, b, :], None, k.y_slots, bass.IndirectOffsetOnAxis(k.slot[:, n:n + 1], 0))\
                            .then_inc(fetched[b], 16)

                def deviations(n):
                    b0, b1 = PARTS[n]
                    pool.wait_ge(var_done, b1)
                    pool.tensor_tensor(var_eps[:, b0:b1], mv[:, b0:b1, 1], k.eps[:, 0:1].to_broadcast([P, b1 - b0]), ALU.add).then_inc(rstd_step, 1)
                    pool.wait_ge(rstd_step, 2 * n + 1)
                    pool.tensor_tensor(rstd[:, b0:b1], var_eps[:, b0:b1], power[:, b0:b1], ALU.pow).then_inc(rstd_step, 1)

                for b in range(B):
                    fetch(b)
                    if b == 5:
                        deviations(0)
                deviations(1)
                for i in range(2):
                    pool.memset(vz[i][:, :, :], 0.0).then_inc(vz_set, 1)
                deviations(2)
                pool.wait_ge(consts_in, 64)

                def heads(f, par):
                    wait_past(pool, s_made, 4 * (f - 1))
                    for c in range(CB):
                        pool.tensor_tensor(kz[par][:, HPB * c:HPB * (c + 1), :],
                                           k.keys1[:, c:c + 1, bass.ds(f * P, P)].to_broadcast([P, HPB, P]),
                                           head_mask[:, :].unsqueeze(2).to_broadcast([P, HPB, P]), ALU.mult).then_inc(kz_done, 1)

                def slots(f, par):
                    wait_past(pool, s_made, GROUPS * (f - 1))
                    pool.tensor_copy(qb[par][:, :, :], q1T[:, :, bass.ds(f * P, P)]).then_inc(qb_done, 1)
                    wait_past(pool, o_made, GROUPS * (f - 1))
                    pool.tensor_copy(vz[par][:, :, :].rearrange("p c (j x) -> p c j x", x=STRIDE)[:, :, :, 0:HD1],
                                     k.vals1[:, bass.ds(f, 1), :].rearrange("p o (c j d) -> p (o c) j d", c=CB, d=HD1)).then_inc(vz_done, 1)

                heads(0, 0)
                pool.wait_ge(vz_set, 2)
                pool.wait_ge(qT_out, CB)
                slots(0, 0)

                def step(it, par, last):
                    if not last:
                        heads(it + 1, 1 - par)
                        if isinstance(it, int) and it == 0:
                            pool.wait_ge(qT_out, 2 * CB)
                        slots(it + 1, 1 - par)

                sequences(pool, step)
                pool.wait_ge(q_done, B)
                for b in range(B):
                    pool.tensor_tensor(k.x1[:, b, :], k.x1[:, b, :], bias_row[:, :], ALU.add).then_inc(bias_done, 1)
                for b in range(B):
                    pool.wait_ge(bias_done, b + 1)
                    pool.wait_ge(r_scaled, b + 1)
                    pool.tensor_tensor(k.x1[:, b, :], k.x1[:, b, :], y[:, b, :], ALU.add).then_inc(x3_done, 1)

            @block.vector
            def _(dve):
                count = [0]

                def then(t):
                    t.then_inc(row_step, 1)
                    count[0] += 1
                    dve.wait_ge(row_step, count[0])

                def combine(b):
                    dve.wait_ge(fetched[b], 32)
                    for i in range(2):
                        then(dve.scalar_tensor_tensor(k.x1[:, b, :], y_pair[i][:, b, :], k.gates[:, i, b:b + 1], k.x1[:, b, :],
                                                      ALU.mult, ALU.add))
                    then(dve.bn_stats(stats[:, b, :], k.x1[:, b, :]))
                    dve.bn_aggr(mv[:, b, :], stats[:, b, :]).then_inc(var_done, 1)

                def normalise_rows(n):
                    dve.wait_ge(rstd_step, 2 * n + 2)
                    for b in range(*PARTS[n]):
                        t = dve.tensor_scalar(y[:, b, :], k.x1[:, b, :], mv[:, b, 0:1], rstd[:, b:b + 1], ALU.subtract, ALU.mult)
                    then(t)

                for b in range(5):
                    combine(b)
                normalise_rows(0)
                row_steps(then, y, 0, *PARTS[0])
                combine(5)
                round_rows(then, y, 0, 0)
                combine(6)
                normalise_rows(1)
                row_steps(then, y, 0, *PARTS[1])
                combine(7)
                round_rows(then, y, 0, 1)
                normalise_rows(2)
                row_steps(then, y, 0, *PARTS[2])
                round_rows(then, y, 0, 2)
                dve.wait_ge(mask_in, 16)

                def add_mask(it, par, g):
                    dve.wait_ge(s_made, GROUPS * it + g + 1)
                    wait_past(dve, exp_done, H1 * (it - 1) + HG * (g + 1))
                    dve.scalar_tensor_tensor(sm[g][:, :, :], banks[g % 2][:, :].rearrange("p (h s) -> p h s", h=HG), HD1 ** -0.5,
                                             mask[:, bass.ds(it, 1), :].to_broadcast([P, HG, P]), ALU.mult, ALU.add).then_inc(sm_done, 1)
                    dve.wait_ge(sm_done, GROUPS * it + g + 1)
                    dve.tensor_reduce(negmax[:, par, HG * g:HG * (g + 1)], sm[g][:, :, :], AX.X, ALU.max, negate=True).then_inc(max_done, 1)

                def pT_copy(it, g):
                    dve.wait_ge(pT_made, GROUPS * it + g + 1)
                    wait_past(dve, o_made, GROUPS * (it - 1) + g + 1)
                    dve.tensor_copy(pT[g][:, :, :], banks[2 + g % 2][:, :].rearrange("p (h s) -> p h s", h=HG)).then_inc(pT_out[0], 1)

                def row_sums(it, par):
                    dve.wait_ge(exp_done, H1 * (it + 1))
                    dve.reciprocal(rinv[:, par, :], rsum[:, par, :]).then_inc(rinv_done, 1)

                def normalise(it, par):
                    dve.wait_ge(rinv_done, it + 1)
                    dve.wait_ge(o_made, GROUPS * (it + 1))
                    dve.tensor_tensor(y[:, bass.ds(it, 1), :].rearrange("p o (h d) -> p (o h) d", d=HD1),
                                      banks[4 + par][:, 0:C].rearrange("p (h d) -> p h d", d=HD1),
                                      rinv[:, par, :].unsqueeze(2).to_broadcast([P, H1, HD1]), ALU.mult).then_inc(o_out, 1)

                add_mask(0, 0, 0)
                add_mask(0, 0, 1)

                def step(it, par, last):
                    for g in range(GROUPS):
                        if g < GROUPS - 2:
                            add_mask(it, par, g + 2)
                        elif not last:
                            add_mask(it + 1, 1 - par, g + 2 - GROUPS)
                        if g == 1 and not (isinstance(it, int) and it == 0):
                            normalise(it - 1, 1 - par)
                        if g % 2 == 0:
                            pT_copy(it, g)
                    row_sums(it, par)

                sequences(dve, step)
                normalise(B - 1, 1)
                dve.wait_ge(o_out, B)
                row_steps(then, y, 1, *PARTS[0])
                row_steps(then, y, 1, *PARTS[1])
                round_rows(then, y, 1, 0)
                row_steps(then, y, 1, *PARTS[2])
                round_rows(then, y, 1, 1)
                round_rows(then, y, 1, 2)
                for b in range(B):
                    dve.wait_ge(r_made, b - b % 2 + 2)
                    acc = banks[4 + b // 2][:, C * (b % 2):C * (b % 2 + 1)]
                    dve.scalar_tensor_tensor(y[:, b, :], acc, step_x[:, 1, b:b + 1], k.step_row[:, :], ALU.mult, ALU.mult).then_inc(r_scaled, 1)
                for b in range(B):
                    dve.wait_ge(x3_done, b + 1)
                    dve.bn_stats(stats[:, b, :], k.x1[:, b, :]).then_inc(x3_stats, 1)
                for b in range(B):
                    dve.wait_ge(x3_stats, b + 1)
                    t = dve.bn_aggr(k.mv[:, b, :], stats[:, b, :])
                t.then_inc(x3_stats, 1)
E1, I1, K1 = 32, 96, 8
TAU = 0.05
FEW = 1e-12
BLOCKS = E1 * I1 // P
AHEAD = 4


def experts1_stage(nc, k, io):
    with Memory(nc) as m:
        var_eps, rstd, power = m.sb("e_var_eps", [P, B]), m.sb("e_rstd", [P, B]), m.sb("e_power", [P, B])
        y, yT = m.sb("e_y", [P, B, C]), m.sb("e_yT", [P, CB, T])
        gate_w = m.sb("e_gate_w", [P, CB, E1])
        iota = m.sb("e_iota", [P, E1])
        alpha = m.sb("alpha", [P, 1])
        probs = m.sb("e_probs", [P, B, E1])
        row = {n: m.sb("e_row_" + n, [P, B]) for n in ("max", "sum", "inv", "topsum", "topinv", "best", "idle", "first", "wsum", "winv")}
        top, top_i, top_f = m.sb("e_top", [P, B, K1]), m.sb("e_top_i", [P, B, K1], u32), m.sb("e_top_f", [P, B, K1])
        scaled, active, is_best = m.sb("scaled", [P, B, K1]), m.sb("active", [P, B, K1]), m.sb("is_best", [P, B, K1])
        where, fallback = m.sb("where", [P, B, K1]), m.sb("fallback", [P, B, K1])
        weight = m.sb("weight", [P, B, K1])
        spread = m.sb("spread", [P, B, E1, K1])
        combine = m.sb("combine", [P, B, E1])
        combine2 = m.sb("combine2", [P, B, 2, E1], f32r)
        cT = m.sb("cT", [2 * E1, T], f32r)
        yT_hi, yT_lo = m.sb("e_yT_hi", [P, CB, T], f32r), m.sb("e_yT_lo", [P, CB, T], f32r)
        pack = [m.sb(f"pack{i}", [P, PACK + P]) for i in range(2)]
        w_hi = [m.sb(f"e_w_hi{i}", [P, PACK + P], f32r) for i in range(AHEAD)]
        w_lo = [m.sb(f"e_w_lo{i}", [P, PACK], f32r) for i in range(AHEAD)]
        early = [m.sb(f"e_early{i}", [P, 512]) for i in range(2 * AHEAD)]
        early_up = [m.sb(f"e_early_up{i}", [P, 512]) for i in range(2 * AHEAD)]
        silu = [m.sb(f"e_silu{i}", [P, 512]) for i in range(2)]
        gated = [m.sb(f"e_gated{i}", [P, 512]) for i in range(2)]
        hid = [m.sb(f"e_hid{i}", [P, 512]) for i in range(2)]
        h_hi = [m.sb(f"e_h_hi{i}", [P, 512], f32r) for i in range(2)]
        h_lo = [m.sb(f"e_h_lo{i}", [P, 512], f32r) for i in range(2)]
        ring = [m.ps(f"e_ring{i}", [P, 512]) for i in range(4)]
        acc = [m.ps(f"e_acc{i}", [P, 2, C]) for i in range(4)]

        s = lambda name: m.sem("e_" + name)
        consts_in, gate_in = s("consts_in"), s("gate_in")
        rstd_step, y_done = s("rstd"), s("y")
        turned, yT_out, logits_made, route, exp_done = s("turned"), s("yT_out"), s("logits"), s("route"), s("exp")
        yT_split, c_split, c_turned, cT_out = s("yT_split"), s("c_split"), s("c_turned"), s("cT_out")
        w_in = [s(f"w_in{i}") for i in range(2)]
        w_hi_done, w_lo_done = s("w_hi"), s("w_lo")
        gates_made, ups_made, c_made, up_out = s("gates_made"), s("ups_made"), s("c_made"), s("up_out")
        silu_done, gated_done, hid_done, hi_done, lo_done = s("silu"), s("gated"), s("hid"), s("h_hi"), s("h_lo")
        added, x_done, out_done = s("added"), s("x_out"), s("out_done")

        def blocks(eng, step, last_apart=False):
            for r in range(AHEAD):
                step(r, r)
            with eng.Fori(1, BLOCKS // AHEAD - last_apart) as i:
                for r in range(AHEAD):
                    step(AHEAD * i + r, r)
            if last_apart:
                for r in range(AHEAD):
                    step(BLOCKS - AHEAD + r, r)

        def is_early(blk):
            return isinstance(blk, int) and blk < AHEAD

        def bank(blk, par, h, what):
            n = 2 * (blk if is_early(blk) else AHEAD + par) + h
            if not is_early(blk):
                return ring[(3 * n + what) % 4]
            return ring[n % 4] if what == 2 else ring[(2 * n + what) % 4]

        def next_split(blk, par, do):
            if isinstance(blk, int) and not AHEAD <= blk + AHEAD - 1 < BLOCKS:
                return
            do(blk + AHEAD - 1, (par - 1) % AHEAD)

        with nc.Block() as block:

            @block.sync
            def _(sp):
                sp.dma_start(gate_w[:, :, :], io["gate_w1"].rearrange("(cb p) e -> p cb e", p=P)).then_inc(gate_in, 16)
                sp.dma_start(iota[:, :], io["iota"]).then_inc(consts_in, 16)
                sp.dma_start(alpha[:, :], io["alpha"]).then_inc(consts_in, 16)

                def load(blk, par):
                    par %= 2
                    wait_past(sp, w_lo_done, blk - 1)
                    sp.dma_start(pack[par][:, :], io["pack"][bass.ds(blk, 1), :, :].rearrange("o p n -> (o p) n")).then_inc(w_in[par], 16)

                blocks(sp, load)
                for j in range(4):
                    sp.wait_ge(x_done, j + 1)
                    sp.dma_start(io["out"][2 * j:2 * j + 2].rearrange("b s c -> s b c"), k.x1[:, 2 * j:2 * j + 2, :]).then_inc(out_done, 16)
                sp.wait_ge(out_done, 64)

            @block.scalar
            def _(act):
                def round_w(blk, par):
                    act.wait_ge(w_in[par % 2], 16 * earlier(blk, par % 2) + 16)
                    wait_past(act, added, 2 * (blk - AHEAD + 1))
                    act.activation(w_hi[par][:, :], pack[par % 2][:, :], ACT.Copy).then_inc(w_hi_done, 1)

                round_w(0, 0)
                for h in range(2):
                    for c in range(CB):
                        n = CB * h + c
                        act.wait_ge(turned, n + 1)
                        act.activation(yT[:, c, 512 * h:512 * (h + 1)], ring[n][:, :], ACT.Copy).then_inc(yT_out, 1)
                for r in range(1, AHEAD):
                    round_w(r, r)
                act.wait_ge(route, 2)
                act.activation(probs[:, :, :], probs[:, :, :], ACT.Exp).then_inc(exp_done, 1)
                for n in range(2 * AHEAD):
                    act.wait_ge(gates_made, n + 1)
                    act.activation(early[n][:, :], bank(n // 2, n // 2, n % 2, 0)[:, :], ACT.Silu).then_inc(silu_done, 1)
                    act.wait_ge(ups_made, n + 1)
                    act.activation(early_up[n][:, :], bank(n // 2, n // 2, n % 2, 1)[:, :], ACT.Copy).then_inc(up_out, 1)

                act.wait_ge(c_turned, 2)
                for h in range(2):
                    act.activation(cT[:, 512 * h:512 * (h + 1)], acc[h][0:2 * E1, :, :].rearrange("p r c -> p (r c)"), ACT.Copy)\
                        .then_inc(cT_out, 1)

                def work(blk, par):
                    for h in range(2):
                        n = 2 * blk + h
                        if not is_early(blk):
                            act.wait_ge(gates_made, n + 1)
                            wait_past(act, gated_done, n - 1)
                            act.activation(silu[h][:, :], bank(blk, par, h, 0)[:, :], ACT.Silu).then_inc(silu_done, 1)
                    next_split(blk, par, round_w)

                blocks(act, work, last_apart=True)

            @block.tensor
            def _(pe):
                for h in range(2):
                    pe.wait_ge(y_done, HB * (h + 1))
                    for c in range(CB):
                        for b in range(HB):
                            t = pe.transpose(ring[CB * h + c][:, P * b:P * (b + 1)], y[:, HB * h + b, P * c:P * (c + 1)], k.ident[:, :])
                        t.then_inc(turned, 1)
                pe.wait_ge(gate_in, 16)
                pe.wait_ge(yT_out, 2 * CB)
                for b in range(B):
                    for c in range(CB):
                        t = pe.matmul(acc[3][:, 0, E1 * b:E1 * (b + 1)], yT[:, c, P * b:P * (b + 1)], gate_w[:, c, :],
                                      start=(c == 0), stop=(c == CB - 1))
                t.then_inc(logits_made, 1)

                def turn_c():
                    pe.wait_ge(c_split, 2)
                    for h in range(2):
                        for b in range(HB):
                            t = pe.transpose(acc[h][0:2 * E1, :, :].rearrange("p r c -> p (r c)")[:, P * b:P * (b + 1)],
                                             combine2[:, HB * h + b, :, :].rearrange("p i e -> p (i e)").bitcast(fp32), k.ident[:, :])
                        t.then_inc(c_turned, 1)

                def multiply(blk, par, h, what):
                    for c in range(CB):
                        cols, tokens = slice(P * (2 * what + c), P * (2 * what + c + 1)), slice(512 * h, 512 * (h + 1))
                        t = products(pe, bank(blk, par, h, what)[:, :], (w_hi[par][:, cols], w_lo[par][:, cols]),
                                     (yT_hi[:, c, tokens], yT_lo[:, c, tokens]), c == 0, c == CB - 1)
                    return t

                def gates(blk, par, h):
                    n = 2 * blk + h
                    if h == 0:
                        pe.wait_ge(w_lo_done, blk + 1)
                    if is_early(blk):
                        if n == 0:
                            pe.wait_ge(yT_split, 4)
                        wait_past(pe, silu_done, n - 1)
                    else:
                        pe.wait_ge(hid_done, n - 1)
                    multiply(blk, par, h, 0).then_inc(gates_made, 1)

                def ups(blk, par, h):
                    n = 2 * blk + h
                    if is_early(blk):
                        wait_past(pe, up_out, n - 1)
                    else:
                        pe.wait_ge(silu_done, n)
                    multiply(blk, par, h, 1).then_inc(ups_made, 1)

                for n in range(2 * AHEAD):
                    gates(n // 2, n // 2, n % 2)
                    ups(n // 2, n // 2, n % 2)
                turn_c()

                def up(blk, par, h):
                    n = 2 * blk + h
                    if is_early(blk):
                        wait_past(pe, hid_done, n - 3)
                        if n == 0:
                            pe.wait_ge(up_out, 2 * AHEAD)
                            pe.wait_ge(cT_out, 2)
                    else:
                        gates(blk, par, h)
                        ups(blk, par, h)
                        pe.wait_ge(gated_done, n)
                    pe.matmul(bank(blk, par, h, 2)[:, :], w_hi[par][0:2 * E1, PACK:PACK + P], cT[:, 512 * h:512 * (h + 1)],
                              start=True, stop=True).then_inc(c_made, 1)

                def down(blk, par, h, first, last):
                    n = 2 * blk + h
                    pe.wait_ge(lo_done, n + 1)
                    for j in range(HB):
                        rows = slice(P * j, P * (j + 1))
                        t = products(pe, acc[2 * h + j // 2][:, j % 2, :], (h_hi[h][:, rows], h_lo[h][:, rows]),
                                     (w_hi[par][:, 4 * P:PACK], w_lo[par][:, 4 * P:PACK]),
                                     first and j % 2 == 0, last and j % 2 == 1)
                    t.then_inc(added, 1)

                for n in range(2 * AHEAD):
                    up(n // 2, n // 2, n % 2)
                    if n >= 2:
                        down(n // 2 - 1, n // 2 - 1, n % 2, n // 2 == 1, False)
                down(AHEAD - 1, AHEAD - 1, 0, False, False)
                with pe.Fori(1, BLOCKS // AHEAD) as i:
                    for r in range(AHEAD):
                        up(AHEAD * i + r, r, 0)
                        down(AHEAD * i + r - 1, (r - 1) % AHEAD, 1, False, False)
                        up(AHEAD * i + r, r, 1)
                        down(AHEAD * i + r, r, 0, False, False)
                down(BLOCKS - 1, AHEAD - 1, 1, False, True)

            @block.gpsimd
            def _(pool):
                pool.memset(power[:, :], -0.5).then_inc(rstd_step, 1)
                pool.tensor_tensor(var_eps[:, :], k.mv[:, :, 1], k.eps[:, 0:1].to_broadcast([P, B]), ALU.add).then_inc(rstd_step, 1)
                pool.wait_ge(rstd_step, 2)
                pool.tensor_tensor(rstd[:, :], var_eps[:, :], power[:, :], ALU.pow).then_inc(rstd_step, 1)

                def split_w(blk, par):
                    pool.wait_ge(w_hi_done, blk + 1)
                    low(pool, w_lo[par][:, :], pack[par % 2][:, 0:PACK], w_hi[par][:, 0:PACK]).then_inc(w_lo_done, 1)

                split_w(0, 0)
                pool.wait_ge(yT_split, 2)
                low(pool, yT_lo[:, 1, :], yT[:, 1, :], yT_hi[:, 1, :]).then_inc(yT_split, 1)
                for r in range(1, AHEAD):
                    split_w(r, r)

                def work(blk, par):
                    for h in range(2):
                        n = 2 * blk + h
                        pool.wait_ge(hi_done, n + 1)
                        low(pool, h_lo[h][:, :], hid[h][:, :], h_hi[h][:, :]).then_inc(lo_done, 1)
                    next_split(blk, par, split_w)

                blocks(pool, work, last_apart=True)

            @block.vector
            def _(dve):
                dve.wait_ge(rstd_step, 3)
                for b in range(B):
                    dve.tensor_scalar(y[:, b, :], k.x1[:, b, :], k.mv[:, b, 0:1], rstd[:, b:b + 1],
                                      ALU.subtract, ALU.mult).then_inc(y_done, 1)

                for c in range(CB):
                    dve.wait_ge(yT_out, 2 + c + 1)
                    dve.tensor_copy(yT_hi[:, c, :], yT[:, c, :]).then_inc(yT_split, 1)
                dve.wait_ge(yT_split, 2)
                low(dve, yT_lo[:, 0, :], yT[:, 0, :], yT_hi[:, 0, :]).then_inc(yT_split, 1)
                count = [0]

                def then(t):
                    t.then_inc(route, 1)
                    count[0] += 1
                    dve.wait_ge(route, count[0])

                wide = lambda a, n: a[:, :].unsqueeze(2).to_broadcast([P, B, n])
                dve.wait_ge(logits_made, 1)
                logits = acc[3][:, 0, :].rearrange("p (b e) -> p b e", b=B)
                dve.tensor_reduce(row["max"][:, :], logits, AX.X, ALU.max).then_inc(y_done, 1)
                dve.wait_ge(y_done, B + 1)
                then(dve.tensor_tensor(probs[:, :, :], logits, wide(row["max"], E1), ALU.subtract))
                dve.wait_ge(consts_in, 32)
                then(dve.tensor_copy(row["first"][:, :], row["max"][:, :]))
                dve.wait_ge(exp_done, 1)
                then(dve.tensor_reduce(row["sum"][:, :], probs[:, :, :], AX.X, ALU.add))
                then(dve.reciprocal(row["inv"][:, :], row["sum"][:, :]))
                then(dve.tensor_tensor(probs[:, :, :], probs[:, :, :], wide(row["inv"], E1), ALU.mult))
                for b in range(B):
                    t = dve.max(top[:, b, :], probs[:, b, :])
                then(t)
                for b in range(B):
                    t = dve.max_index(top_i[:, b, :], top[:, b, :], probs[:, b, :])
                then(t)
                then(dve.tensor_copy(top_f[:, :, :], top_i[:, :, :]))
                then(dve.tensor_reduce(row["topsum"][:, :], top[:, :, :], AX.X, ALU.add))
                then(dve.tensor_scalar(row["topsum"][:, :], row["topsum"][:, :], FEW, None, ALU.max))
                then(dve.reciprocal(row["topinv"][:, :], row["topsum"][:, :]))
                then(dve.tensor_tensor(top[:, :, :], top[:, :, :], wide(row["topinv"], K1), ALU.mult))
                then(dve.tensor_scalar(scaled[:, :, :], top[:, :, :], alpha[:, 0:1], None, ALU.mult))
                then(dve.tensor_scalar(active[:, :, :], scaled[:, :, :], TAU, None, ALU.is_ge))
                then(dve.tensor_reduce(row["best"][:, :], scaled[:, :, :], AX.X, ALU.max))
                then(dve.tensor_tensor(is_best[:, :, :], scaled[:, :, :], wide(row["best"], K1), ALU.is_equal))
                then(dve.scalar_tensor_tensor(where[:, :, :], is_best[:, :, :], -100.0,
                                              iota[:, 0:K1].unsqueeze(1).to_broadcast([P, B, K1]), ALU.mult, ALU.add))
                then(dve.tensor_reduce(row["first"][:, :], where[:, :, :], AX.X, ALU.min))
                then(dve.tensor_tensor(fallback[:, :, :], where[:, :, :], wide(row["first"], K1), ALU.is_equal))
                then(dve.tensor_reduce(row["idle"][:, :], active[:, :, :], AX.X, ALU.max))
                then(dve.tensor_scalar(row["idle"][:, :], row["idle"][:, :], -1.0, 1.0, ALU.mult, ALU.add))
                then(dve.tensor_tensor(fallback[:, :, :], fallback[:, :, :], wide(row["idle"], K1), ALU.mult))
                then(dve.tensor_tensor(active[:, :, :], active[:, :, :], fallback[:, :, :], ALU.max))
                then(dve.tensor_tensor(weight[:, :, :], top[:, :, :], active[:, :, :], ALU.mult))
                then(dve.tensor_reduce(row["wsum"][:, :], weight[:, :, :], AX.X, ALU.add))
                then(dve.tensor_scalar(row["wsum"][:, :], row["wsum"][:, :], FEW, None, ALU.max))
                then(dve.reciprocal(row["winv"][:, :], row["wsum"][:, :]))
                then(dve.tensor_tensor(weight[:, :, :], weight[:, :, :], wide(row["winv"], K1), ALU.mult))
                for b in range(B):
                    t = dve.tensor_tensor(spread[:, b, :, :], iota[:, :].unsqueeze(2).to_broadcast([P, E1, K1]),
                                          top_f[:, b:b + 1, :].to_broadcast([P, E1, K1]), ALU.is_equal)
                then(t)
                for b in range(B):
                    t = dve.tensor_tensor(spread[:, b, :, :], spread[:, b, :, :], weight[:, b:b + 1, :].to_broadcast([P, E1, K1]), ALU.mult)
                then(t)
                then(dve.tensor_reduce(combine[:, :, :].rearrange("p b e -> p (b e)"),
                                       spread[:, :, :, :].rearrange("p b e k -> p (b e) k"), AX.X, ALU.add))

                then(dve.tensor_copy(combine2[:, :, 0, :], combine[:, :, :]))
                low(dve, combine2[:, :, 1, :], combine[:, :, :], combine2[:, :, 0, :]).then_inc(c_split, 2)

                def work(blk, par):
                    for h in range(2):
                        n = 2 * blk + h
                        dve.wait_ge(silu_done, n + 1)
                        if is_early(blk):
                            dve.wait_ge(up_out, n + 1)
                            up_of, silu_of = early_up[n], early[n]
                        else:
                            dve.wait_ge(ups_made, n + 1)
                            up_of, silu_of = bank(blk, par, h, 1), silu[h]
                        dve.tensor_tensor(gated[h][:, :], up_of[:, :], silu_of[:, :], ALU.mult).then_inc(gated_done, 1)
                        dve.wait_ge(c_made, n + 1)
                        dve.wait_ge(gated_done, n + 1)
                        wait_past(dve, lo_done, n - 1)
                        dve.tensor_tensor(hid[h][:, :], bank(blk, par, h, 2)[:, :], gated[h][:, :], ALU.mult).then_inc(hid_done, 1)
                        dve.wait_ge(hid_done, n + 1)
                        wait_past(dve, added, n - 1)
                        dve.tensor_copy(h_hi[h][:, :], hid[h][:, :]).then_inc(hi_done, 1)

                blocks(dve, work)
                dve.wait_ge(added, 2 * BLOCKS)
                for j in range(4):
                    dve.tensor_tensor(k.x1[:, 2 * j:2 * j + 2, :], k.x1[:, 2 * j:2 * j + 2, :], acc[j][:, :, :], ALU.add).then_inc(x_done, 1)
class Kept:

    def __init__(self, m):
        self.x1 = m.sb("x1", [P, B, C])
        self.z = m.sb("z", [P, B, C])
        self.xa = m.sb("xa", [P, B, C])
        self.ssq = m.sb("ssq", [P, B])
        self.keys1 = m.sb("keys1", [P, CB, T])
        self.vals1 = m.sb("vals1", [P, B, C])
        self.ident = m.sb("ident", [P, P])
        self.eps = m.sb("eps", [P, 1])
        self.mv = m.sb("mean_var", [P, B, 2])

    def early(self, m):
        self.w0_hi = [m.sb(f"w0_hi{i}", [P, CHUNK], f32r) for i in range(EARLY)]
        self.w0_lo = [m.sb(f"w0_lo{i}", [P, CHUNK], f32r) for i in range(EARLY)]

    def later(self, nc, m):
        self.w_qT, self.w_step, self.step_row = m.sb("w_qT", [P, 2, CB, C], bf16), m.sb("w_step", [P, 2 * CB]), m.sb("step_row", [P, C])
        self.slot, self.gates = m.sb("slot", [P, 2 * B], u32), m.sb("gates", [P, 2, B])
        self.y_slots = nc.dram_tensor("y_slots", (TILES * SLOTS, C), fp32, kind="Internal").ap()


def build_program(nc, io):
    with Memory(nc) as m:
        kept = Kept(m)
        with Memory(nc) as m_early:
            kept.early(m_early)
            wkv_stage(nc, kept, io)
            attention_stage(nc, kept, io)
        with Memory(nc) as m_later:
            kept.later(nc, m_later)
            experts0_stage(nc, kept, io)
            cross_stage(nc, kept, io)
            experts1_stage(nc, kept, io)


def rope_tables(np):
    f = np.float32
    freq = (f(1e6) ** (-np.arange(0, HD0, 2, dtype=f) / f(HD0))).astype(f)
    angle = np.arange(P, dtype=f)[:, None] * freq[None]
    cos, sin = np.cos(angle), np.sin(angle)
    cos, sin = np.concatenate([cos, cos], 1), np.concatenate([-sin, sin], 1)
    scale = f(HD0 ** -0.5)
    return np.stack([cos * scale, sin * scale, cos, sin], 1).astype(f)


def weights0(np, w1, w3, w2):
    columns = lambda w: w.reshape(E0, CB, P, FB, P).transpose(0, 2, 3, 1, 4).reshape(E0, P, FB, CB * P)
    down = w2.reshape(E0, FB, P, C).transpose(0, 2, 1, 3)
    return np.concatenate([columns(w1), columns(w3), down], 3).reshape(E0, P, FB * PACK)


def weights1(np, gate_up, down):
    gate = gate_up[:, :I1].reshape(BLOCKS, P, CB, P).transpose(0, 3, 2, 1).reshape(BLOCKS, P, CB * P)
    up = gate_up[:, I1:].reshape(BLOCKS, P, CB, P).transpose(0, 3, 2, 1).reshape(BLOCKS, P, CB * P)
    down = down.transpose(0, 2, 1).reshape(BLOCKS, P, C)
    expert = np.arange(BLOCKS * P).reshape(BLOCKS, 1, P) // I1
    one = (expert == np.arange(P)[None, :, None] % E1).astype(np.float32)
    return dict(pack=np.concatenate([gate, up, down, one], 2))


def kernel(**inputs):
    import ml_dtypes
    import numpy as np
    import concourse.bacc as bacc
    from concourse.bass_utils import run_bass_kernel_spmd

    a = {n: np.asarray(v) for n, v in inputs.items()}
    half = ml_dtypes.bfloat16
    column = lambda v: v.reshape(CB, P).T
    rows = lambda v: np.broadcast_to(v, (P,) + v.shape)
    pairs_apart = lambda w, h: w.reshape(C, h, HD0 // 2, 2).transpose(0, 1, 3, 2).reshape(C, h * HD0)
    visible = np.tril(np.ones((P, P), bool))
    arrays = dict(
        x=a["x"], ctxT=a["ctx_2048"].transpose(2, 0, 1),
        wkv_cols=np.stack([column(a[n]) for n in ("L0_xattn_w", "L0_xattn_u", "L1_xattn_bk")], 1),
        wk1T=a["L1_xattn_wk"].T, wv1T=a["L1_xattn_wv"].T, bv1=rows(a["L1_xattn_bv"]),
        ln_w=column(a["L0_ffn_ln_w"]),
        wq0=pairs_apart(a["L0_ffn_wq"], H0), wk0=pairs_apart(a["L0_ffn_wk"], KV0), wv0=a["L0_ffn_wv"], wo0=a["L0_ffn_wo"],
        ff_w=rows(a["L0_ffn_ff_ln_w"]), gate_w0=a["L0_ffn_gate_w"], pack0=weights0(np, a["L0_ffn_w1"], a["L0_ffn_w3"], a["L0_ffn_w2"]),
        wq1=a["L1_xattn_wq"], wo1=a["L1_xattn_wo"], bias_row=rows(a["L1_xattn_bo"]), bias_col=column(a["L1_xattn_bq"]),
        mask=a["mask_BxSxS2_ff0"],
        gate_w1=a["L1_ffn_gate_weight"].T, alpha=rows(a["L1_ffn_layer_alpha"].reshape(1)),
        **weights1(np, a["L1_ffn_gate_up_proj"], a["L1_ffn_down_proj"]),
        ident=np.eye(P, dtype=np.float32), identb=np.eye(P).astype(half), rope=rope_tables(np),
        causal=np.broadcast_to(np.where(visible, 0, -1e30).astype(half)[:, None], (P, G0, P)),
        iota=rows(np.arange(E1, dtype=np.float32)), before=(~visible).astype(half), ones=np.ones((P, P), half),
        head_mask=(np.arange(P)[:, None] // HD1 == np.arange(HPB)[None]).astype(np.float32),
    )
    nc = bacc.Bacc("TRN2", target_bir_lowering=False, num_devices=1)
    feed, io = {}, {}
    for name, value in arrays.items():
        value = np.ascontiguousarray(value)
        feed[f"in_{name}"] = value
        io[name] = nc.dram_tensor(f"in_{name}", value.shape, mybir.dt.from_np(value.dtype), kind="ExternalInput").ap()
    io["out"] = nc.dram_tensor("out_x", (B, P, C), fp32, kind="ExternalOutput").ap()
    build_program(nc, io)
    result = run_bass_kernel_spmd(nc, [feed], core_ids=[0])
    return result.results[0]["out_x"]
```
